# Optimizing a Trainium2 kernel written in Bass

```python
import numpy as np
import jax
import jax.numpy as jnp

def _softmax(x, axis=-1):
    return jax.nn.softmax(x, axis=axis)

def _gelu(x):
    return jax.nn.gelu(x, approximate=True)

def _silu(x):
    return jax.nn.silu(x)

def _sigmoid(x):
    return jax.nn.sigmoid(x)

def _layernorm(x, axis=-1, eps=1e-05):
    m = jnp.mean(x, axis=axis, keepdims=True)
    v = jnp.var(x, axis=axis, keepdims=True)
    return (x - m) / jnp.sqrt(v + eps)

def _scatter_add(tgt, idx, src, axis=0):
    return tgt.at[idx].add(src)

def _segment_sum(src, seg, n):
    return jax.ops.segment_sum(src, seg, n)
kernel_name = 'mk_flamingo_gated_d4_seqx_r8_a27d3c'

def setup_inputs(seed: int=0):
    np.random.seed(seed)
    _w = jnp.asarray

    def _rec_inputs():
        import jax
        import jax.numpy as jnp
        _rk = jax.random.key(seed)
        x = -0.0002928 + 1 * jax.random.normal(jax.random.fold_in(_rk, 1), (32, 128, 128), jnp.float32)
        _lenS = 128 - jax.random.randint(jax.random.fold_in(_rk, 7), (32,), 0, max(1, 128 // 4) + 1, jnp.int32)
        _lenS2 = 128 - jax.random.randint(jax.random.fold_in(_rk, 8), (32,), 0, max(1, 128 // 4) + 1, jnp.int32)
        _ctx_1024P = jax.random.normal(jax.random.fold_in(_rk, 11), (32, 16, 128), jnp.float32)
        _ctx_1024c = jax.random.dirichlet(jax.random.fold_in(_rk, 511), 0.3 * jnp.ones((16,), jnp.float32), (32, 128))
        _ctx_1024t = jnp.einsum('bsk,bkd->bsd', _ctx_1024c, _ctx_1024P)
        _ctx_1024t = _ctx_1024t * jax.lax.rsqrt(jnp.mean(jnp.square(_ctx_1024t)) + 1e-12) * 0.953939
        ctx_1024 = -1.39393e-06 + 0.999914 * (_ctx_1024t + 0.3 * jax.random.normal(jax.random.fold_in(_rk, 611), (32, 128, 128), jnp.float32))
        _validS = jnp.arange(128)[None, :] < _lenS[:, None]
        _validS2 = jnp.arange(128)[None, :] < _lenS2[:, None]
        _causal = jnp.tril(jnp.ones((128, 128), dtype=bool))
        mask_BxSxS2_ff0 = jnp.where(jnp.ones((32, 128, 128), dtype=bool), 0.0, -1000000000.0).astype(jnp.float32)
        mask_BxS2_ik0 = jnp.where(jnp.broadcast_to(_validS2[:, :], (32, 128)), 0, 1).astype(jnp.int32)
        _g = jax.random.normal(jax.random.fold_in(_rk, 9001), (2, 4), jnp.float32)
        _g = jnp.sign(_g) * jnp.maximum(jnp.abs(_g), 1.0) + (_g == 0) * 1.0
        g_xattn = _g[0]
        g_ffn = _g[1]
        return (x, ctx_1024, mask_BxSxS2_ff0, mask_BxS2_ik0, g_xattn, g_ffn)
    x, ctx_1024, mask_BxSxS2_ff0, mask_BxS2_ik0, g_xattn, g_ffn = _rec_inputs()

    def _L0_xattn_setup():
        import jax, jax.numpy as jnp
        import numpy as np
        import math
        D_MODEL = 128
        N_HEAD = 16
        B = 2
        L = 256

        def _linear(x, W, b):
            return jnp.einsum('bld,od->blo', x, W) + b
        key = jax.random.key(seed)
        ks = jax.random.split(key, 11)
        s = 1.0 / math.sqrt(D_MODEL)
        inp = {'q': jax.random.normal(ks[0], (B, L, D_MODEL), jnp.float32), 'k': jax.random.normal(ks[1], (B, L, D_MODEL), jnp.float32), 'v': jax.random.normal(ks[2], (B, L, D_MODEL), jnp.float32), 'wq': jax.random.normal(ks[3], (D_MODEL, D_MODEL), jnp.float32) * s, 'bq': jnp.zeros((D_MODEL,), jnp.float32), 'wk': jax.random.normal(ks[4], (D_MODEL, D_MODEL), jnp.float32) * s, 'bk': jnp.zeros((D_MODEL,), jnp.float32), 'wv': jax.random.normal(ks[5], (D_MODEL, D_MODEL), jnp.float32) * s, 'bv': jnp.zeros((D_MODEL,), jnp.float32), 'wo': jax.random.normal(ks[6], (D_MODEL, D_MODEL), jnp.float32) * s, 'bo': jnp.zeros((D_MODEL,), jnp.float32)}
        return inp
    _L0_xattn_all = _L0_xattn_setup()
    _L0_xattn_in = {k: v for k, v in _L0_xattn_all.items() if k in ('wq', 'bq', 'wk', 'bk', 'wv', 'bv', 'wo', 'bo')}
    del _L0_xattn_all

    def _L0_ffn_setup():
        import jax, jax.numpy as jnp
        import numpy as np
        EMBED_DIM = 128
        HIDDEN = 4 * EMBED_DIM
        BATCH, SEQ = (4, 512)
        EPS = 1e-05

        def _quant_weight(w):
            s = jnp.clip(jnp.mean(jnp.abs(w)), EPS, None)
            wq = jnp.clip(jnp.round(w / s), -1.0, 1.0) * s
            return w + jax.lax.stop_gradient(wq - w)

        def _quant_act(x):
            scale = 127.0 / jnp.clip(jnp.max(jnp.abs(x), axis=-1, keepdims=True), EPS, None)
            xq = jnp.clip(jnp.round(x * scale), -128.0, 127.0) / scale
            return x + jax.lax.stop_gradient(xq - x)

        def _bitlinear(x, w):
            return jnp.einsum('bsi,oi->bso', _quant_act(x), _quant_weight(w))
        key = jax.random.key(seed)
        k1, k2, k3 = jax.random.split(key, 3)
        x = jax.random.normal(k1, (BATCH, SEQ, EMBED_DIM), dtype=jnp.float32)
        w1 = jax.random.normal(k2, (HIDDEN, EMBED_DIM), dtype=jnp.float32) * (1.0 / np.sqrt(EMBED_DIM))
        w2 = jax.random.normal(k3, (EMBED_DIM, HIDDEN), dtype=jnp.float32) * (1.0 / np.sqrt(HIDDEN))
        return {'x': x, 'w1': w1, 'w2': w2}
    _L0_ffn_all = _L0_ffn_setup()
    _L0_ffn_in = {k: v for k, v in _L0_ffn_all.items() if k in ('w1', 'w2')}
    del _L0_ffn_all

    def _L1_xattn_setup():
        import jax, jax.numpy as jnp
        import numpy as np
        key0 = jax.random.key(seed)
        kq, kk, kv = jax.random.split(key0, 3)
        B, S, E = (4, 256, 128)
        query = jax.random.normal(kq, (B, S, E), dtype=jnp.float32)
        key = jax.random.normal(kk, (B, S, E), dtype=jnp.float32)
        value = jax.random.normal(kv, (B, S, E), dtype=jnp.float32)
        attn_mask = jnp.zeros((B, S, S), dtype=jnp.float32)
        return {'query': query, 'key': key, 'value': value, 'attn_mask': attn_mask}
    _L1_xattn_all = _L1_xattn_setup()
    _L1_xattn_in = {k: v for k, v in _L1_xattn_all.items() if k in ()}
    del _L1_xattn_all

    def _L1_ffn_setup():
        import jax, jax.numpy as jnp
        import numpy as np
        HIDDEN = 128
        INNER = 512

        def _weight_quant(w):
            scale = 1.0 / jnp.clip(jnp.mean(jnp.abs(w)), 1e-05)
            wq = jnp.clip(jnp.round(w * scale), -1.0, 1.0) / scale
            return w + jax.lax.stop_gradient(wq - w)

        def _act_quant(x):
            scale = 127.0 / jnp.clip(jnp.max(jnp.abs(x), axis=-1, keepdims=True), 1e-05)
            xq = jnp.clip(jnp.round(x * scale), -128.0, 127.0) / scale
            return x + jax.lax.stop_gradient(xq - x)

        def _bitlinear(x, w):
            return jnp.einsum('bsi,oi->bso', _act_quant(x), _weight_quant(w))
        key = jax.random.key(seed)
        k0, k1, k2, k3 = jax.random.split(key, 4)
        x = jax.random.normal(k0, (4, 256, HIDDEN), dtype=jnp.float32)
        w_gate = jax.random.normal(k1, (INNER, HIDDEN), dtype=jnp.float32) / np.sqrt(HIDDEN)
        w_up = jax.random.normal(k2, (INNER, HIDDEN), dtype=jnp.float32) / np.sqrt(HIDDEN)
        w_down = jax.random.normal(k3, (HIDDEN, INNER), dtype=jnp.float32) / np.sqrt(INNER)
        return {'x': x, 'w_gate': w_gate, 'w_up': w_up, 'w_down': w_down}
    _L1_ffn_all = _L1_ffn_setup()
    _L1_ffn_in = {k: v for k, v in _L1_ffn_all.items() if k in ('w_gate', 'w_up', 'w_down')}
    del _L1_ffn_all

    def _L2_xattn_setup():
        import jax, jax.numpy as jnp
        import numpy as np
        D_MODEL = 128
        N_HEAD = 16
        D_HEAD = D_MODEL // N_HEAD
        key = jax.random.key(seed)
        ks = jax.random.split(key, 6)
        B, L, M = (2, 256, 256)
        q = jax.random.normal(ks[0], (B, L, D_MODEL), dtype=jnp.float32)
        kv = jax.random.normal(ks[1], (B, L, D_MODEL), dtype=jnp.float32)
        mem = jax.random.normal(ks[2], (B, M, D_MODEL), dtype=jnp.float32)
        s = 1.0 / np.sqrt(D_MODEL)
        w_q = jax.random.normal(ks[3], (D_MODEL, D_MODEL), dtype=jnp.float32) * s
        w_kv = jax.random.normal(ks[4], (D_MODEL, 2 * D_HEAD), dtype=jnp.float32) * s
        w_concat = jax.random.normal(ks[5], (D_MODEL, D_MODEL), dtype=jnp.float32) * s
        return {'q': q, 'kv': kv, 'mem': mem, 'w_q': w_q, 'w_kv': w_kv, 'w_concat': w_concat}
    _L2_xattn_all = _L2_xattn_setup()
    _L2_xattn_in = {k: v for k, v in _L2_xattn_all.items() if k in ('w_q', 'w_kv', 'w_concat')}
    del _L2_xattn_all

    def _L2_ffn_setup():
        import jax, jax.numpy as jnp
        import numpy as np
        B, S, D = (4, 256, 128)
        E, F = (8, 512)
        key = jax.random.key(seed)
        ks = jax.random.split(key, 5)
        x = jax.random.normal(ks[0], (B, S, D), dtype=jnp.float32)
        switch_w = jax.random.normal(ks[1], (D, E), dtype=jnp.float32) * D ** (-0.5)
        switch_b = jnp.zeros((E,), dtype=jnp.float32)
        w1 = jax.random.normal(ks[2], (E, D, F), dtype=jnp.float32) * D ** (-0.5)
        b1 = jnp.zeros((E, F), dtype=jnp.float32)
        w2 = jax.random.normal(ks[3], (E, F, D), dtype=jnp.float32) * F ** (-0.5)
        b2 = jnp.zeros((E, D), dtype=jnp.float32)
        return {'x': x, 'switch_w': switch_w, 'switch_b': switch_b, 'w1': w1, 'b1': b1, 'w2': w2, 'b2': b2}
    _L2_ffn_all = _L2_ffn_setup()
    _L2_ffn_in = {k: v for k, v in _L2_ffn_all.items() if k in ('switch_w', 'switch_b', 'w1', 'b1', 'w2', 'b2')}
    del _L2_ffn_all

    def _L3_xattn_setup():
        import jax, jax.numpy as jnp
        import numpy as np
        B, S, D, H = (2, 256, 128, 16)
        DK = D // H
        SQRT_DK = DK ** 0.5
        NEG = -1000000000.0
        key = jax.random.key(seed)
        ks = jax.random.split(key, 7)
        scale = 1.0 / np.sqrt(D)
        return {'x': jax.random.normal(ks[0], (B, S, D), jnp.float32), 'encoder_output': jax.random.normal(ks[1], (B, S, D), jnp.float32), 'mask': jax.random.randint(ks[2], (B, S), 0, 2, jnp.int32), 'WQ': jax.random.normal(ks[3], (D, D), jnp.float32) * scale, 'WK': jax.random.normal(ks[4], (D, D), jnp.float32) * scale, 'WV': jax.random.normal(ks[5], (D, D), jnp.float32) * scale, 'WO': jax.random.normal(ks[6], (D, D), jnp.float32) * scale}
    _L3_xattn_all = _L3_xattn_setup()
    _L3_xattn_in = {k: v for k, v in _L3_xattn_all.items() if k in ('WQ', 'WK', 'WV', 'WO')}
    del _L3_xattn_all

    def _L3_ffn_setup():
        import jax, jax.numpy as jnp
        import numpy as np
        D_MODEL = 128
        EXPANSION = 4
        D_HIDDEN = D_MODEL * EXPANSION
        NUM_STAGES = int(np.log2(D_HIDDEN))

        def butterfly(y, weights, dim):
            lead = y.shape[:-1]
            for stage in range(weights.shape[0]):
                s = 2 ** stage
                nb = dim // (2 * s)
                yr = y.reshape(*lead, nb, 2, s)
                a = yr[..., 0, :]
                b = yr[..., 1, :]
                w = weights[stage].reshape(nb, s, 2, 2)
                na = w[..., 0, 0] * a + w[..., 0, 1] * b
                nb2 = w[..., 1, 0] * a + w[..., 1, 1] * b
                y = jnp.stack([na, nb2], axis=-2).reshape(*lead, dim)
            return y
        key = jax.random.key(seed)
        ks = jax.random.split(key, 6)
        B, S = (4, 256)
        x = jax.random.normal(ks[0], (B, S, D_MODEL), jnp.float32)
        W_exp = jax.random.normal(ks[1], (D_MODEL, D_HIDDEN), jnp.float32) * 0.02
        b_exp = jnp.zeros((D_HIDDEN,), jnp.float32)
        up_weights = jax.random.normal(ks[2], (NUM_STAGES, D_HIDDEN // 2, 2, 2), jnp.float32) * 0.02
        up_bias = jnp.zeros((D_HIDDEN,), jnp.float32)
        down_weights = jax.random.normal(ks[3], (NUM_STAGES, D_HIDDEN // 2, 2, 2), jnp.float32) * 0.02
        W_con = jax.random.normal(ks[4], (D_HIDDEN, D_MODEL), jnp.float32) * 0.02
        b_con = jnp.zeros((D_MODEL,), jnp.float32)
        down_bias = jnp.zeros((D_MODEL,), jnp.float32)
        return dict(x=x, W_exp=W_exp, b_exp=b_exp, up_weights=up_weights, up_bias=up_bias, down_weights=down_weights, W_con=W_con, b_con=b_con, down_bias=down_bias)
    _L3_ffn_all = _L3_ffn_setup()
    _L3_ffn_in = {k: v for k, v in _L3_ffn_all.items() if k in ('W_exp', 'b_exp', 'up_weights', 'up_bias', 'down_weights', 'W_con', 'b_con', 'down_bias')}
    del _L3_ffn_all
    return {'x': x, 'ctx_1024': ctx_1024, 'mask_BxSxS2_ff0': mask_BxSxS2_ff0, 'mask_BxS2_ik0': mask_BxS2_ik0, 'g_xattn': g_xattn, 'g_ffn': g_ffn, 'L0_xattn_wq': _L0_xattn_in['wq'], 'L0_xattn_bq': _L0_xattn_in['bq'], 'L0_xattn_wk': _L0_xattn_in['wk'], 'L0_xattn_bk': _L0_xattn_in['bk'], 'L0_xattn_wv': _L0_xattn_in['wv'], 'L0_xattn_bv': _L0_xattn_in['bv'], 'L0_xattn_wo': _L0_xattn_in['wo'], 'L0_xattn_bo': _L0_xattn_in['bo'], 'L0_ffn_w1': _L0_ffn_in['w1'], 'L0_ffn_w2': _L0_ffn_in['w2'], 'L1_ffn_w_gate': _L1_ffn_in['w_gate'], 'L1_ffn_w_up': _L1_ffn_in['w_up'], 'L1_ffn_w_down': _L1_ffn_in['w_down'], 'L2_xattn_w_q': _L2_xattn_in['w_q'], 'L2_xattn_w_kv': _L2_xattn_in['w_kv'], 'L2_xattn_w_concat': _L2_xattn_in['w_concat'], 'L2_ffn_switch_w': _L2_ffn_in['switch_w'], 'L2_ffn_switch_b': _L2_ffn_in['switch_b'], 'L2_ffn_w1': _L2_ffn_in['w1'], 'L2_ffn_b1': _L2_ffn_in['b1'], 'L2_ffn_w2': _L2_ffn_in['w2'], 'L2_ffn_b2': _L2_ffn_in['b2'], 'L3_xattn_WQ': _L3_xattn_in['WQ'], 'L3_xattn_WK': _L3_xattn_in['WK'], 'L3_xattn_WV': _L3_xattn_in['WV'], 'L3_xattn_WO': _L3_xattn_in['WO'], 'L3_ffn_W_exp': _L3_ffn_in['W_exp'], 'L3_ffn_b_exp': _L3_ffn_in['b_exp'], 'L3_ffn_up_weights': _L3_ffn_in['up_weights'], 'L3_ffn_up_bias': _L3_ffn_in['up_bias'], 'L3_ffn_down_weights': _L3_ffn_in['down_weights'], 'L3_ffn_W_con': _L3_ffn_in['W_con'], 'L3_ffn_b_con': _L3_ffn_in['b_con'], 'L3_ffn_down_bias': _L3_ffn_in['down_bias']}

def reference(x, ctx_1024, mask_BxSxS2_ff0, mask_BxS2_ik0, g_xattn, g_ffn, L0_xattn_wq, L0_xattn_bq, L0_xattn_wk, L0_xattn_bk, L0_xattn_wv, L0_xattn_bv, L0_xattn_wo, L0_xattn_bo, L0_ffn_w1, L0_ffn_w2, L1_ffn_w_gate, L1_ffn_w_up, L1_ffn_w_down, L2_xattn_w_q, L2_xattn_w_kv, L2_xattn_w_concat, L2_ffn_switch_w, L2_ffn_switch_b, L2_ffn_w1, L2_ffn_b1, L2_ffn_w2, L2_ffn_b2, L3_xattn_WQ, L3_xattn_WK, L3_xattn_WV, L3_xattn_WO, L3_ffn_W_exp, L3_ffn_b_exp, L3_ffn_up_weights, L3_ffn_up_bias, L3_ffn_down_weights, L3_ffn_W_con, L3_ffn_b_con, L3_ffn_down_bias):
    import jax
    import jax.numpy as jnp

    def _L0_xattn_ref(q, k, v, wq, bq, wk, bk, wv, bv, wo, bo):
        import jax, jax.numpy as jnp
        import numpy as np
        import math
        D_MODEL = 128
        N_HEAD = 16
        B = 2
        L = 256

        def _linear(x, W, b):
            return jnp.einsum('bld,od->blo', x, W) + b
        b, l, d_model = q.shape
        h = N_HEAD
        d = d_model // h
        qh = _linear(q, wq, bq).reshape(b, h, l, d)
        kh = _linear(k, wk, bk).reshape(b, h, l, d)
        vh = _linear(v, wv, bv).reshape(b, h, l, d)
        kt = kh.reshape(b, h, d, l)
        score = jnp.einsum('bhij,bhjk->bhik', qh, kt) / math.sqrt(d)
        attn = jax.nn.softmax(score, axis=-1)
        out = jnp.einsum('bhls,bhsd->bhld', attn, vh).reshape(b, l, d_model)
        return _linear(out, wo, bo)

    def _L0_ffn_ref(x, w1, w2):
        import jax, jax.numpy as jnp
        import numpy as np
        EMBED_DIM = 128
        HIDDEN = 4 * EMBED_DIM
        BATCH, SEQ = (4, 512)
        EPS = 1e-05

        def _quant_weight(w):
            s = jnp.clip(jnp.mean(jnp.abs(w)), EPS, None)
            wq = jnp.clip(jnp.round(w / s), -1.0, 1.0) * s
            return w + jax.lax.stop_gradient(wq - w)

        def _quant_act(x):
            scale = 127.0 / jnp.clip(jnp.max(jnp.abs(x), axis=-1, keepdims=True), EPS, None)
            xq = jnp.clip(jnp.round(x * scale), -128.0, 127.0) / scale
            return x + jax.lax.stop_gradient(xq - x)

        def _bitlinear(x, w):
            return jnp.einsum('bsi,oi->bso', _quant_act(x), _quant_weight(w))
        h = jax.nn.gelu(_bitlinear(x, w1), approximate=False)
        return _bitlinear(h, w2)

    def _L1_xattn_ref(query, key, value, attn_mask):
        import jax, jax.numpy as jnp
        import numpy as np
        E = query.shape[-1]
        scale = 1.0 / jnp.sqrt(jnp.asarray(E, dtype=query.dtype))
        qk = jnp.einsum('bqe,bke->bqk', query, key) * scale + attn_mask
        attn = jax.nn.softmax(qk, axis=-1)
        out = jnp.einsum('bqk,bke->bqe', attn, value)
        return out

    def _L1_ffn_ref(x, w_gate, w_up, w_down):
        import jax, jax.numpy as jnp
        import numpy as np
        HIDDEN = 128
        INNER = 512

        def _weight_quant(w):
            scale = 1.0 / jnp.clip(jnp.mean(jnp.abs(w)), 1e-05)
            wq = jnp.clip(jnp.round(w * scale), -1.0, 1.0) / scale
            return w + jax.lax.stop_gradient(wq - w)

        def _act_quant(x):
            scale = 127.0 / jnp.clip(jnp.max(jnp.abs(x), axis=-1, keepdims=True), 1e-05)
            xq = jnp.clip(jnp.round(x * scale), -128.0, 127.0) / scale
            return x + jax.lax.stop_gradient(xq - x)

        def _bitlinear(x, w):
            return jnp.einsum('bsi,oi->bso', _act_quant(x), _weight_quant(w))
        gate = jax.nn.silu(_bitlinear(x, w_gate))
        up = _bitlinear(x, w_up)
        return _bitlinear(gate * up, w_down)

    def _L2_xattn_ref(q, kv, mem, w_q, w_kv, w_concat):
        import jax, jax.numpy as jnp
        import numpy as np
        D_MODEL = 128
        N_HEAD = 16
        D_HEAD = D_MODEL // N_HEAD
        B, L, D = q.shape
        c = jnp.concatenate([mem, kv], axis=1)
        qh = (q @ w_q).reshape(B, L, N_HEAD, D_HEAD).transpose(0, 2, 1, 3)
        kvp = c @ w_kv
        k, v = (kvp[..., :D_HEAD], kvp[..., D_HEAD:])
        attn_score = jnp.einsum('bhid,bjd->bhij', qh, k) / np.sqrt(D_HEAD)
        attn_prob = jax.nn.softmax(attn_score, axis=-1)
        out = jnp.einsum('bhij,bjd->bhid', attn_prob, v)
        out = out.transpose(0, 2, 1, 3).reshape(B, L, D)
        return out @ w_concat

    def _L2_ffn_ref(x, switch_w, switch_b, w1, b1, w2, b2):
        import jax, jax.numpy as jnp
        import numpy as np
        B, S, D = (4, 256, 128)
        E, F = (8, 512)
        b, s, d = x.shape
        t = x.reshape(-1, d)
        logits = t @ switch_w + switch_b
        route_prob = jax.nn.softmax(logits, axis=-1)
        route_prob_max = jnp.max(route_prob, axis=-1)
        routes = jnp.argmax(route_prob, axis=-1)
        out = jnp.zeros_like(t)
        n_experts = w1.shape[0]
        for e in range(n_experts):
            h = jax.nn.gelu(t @ w1[e] + b1[e])
            y = h @ w2[e] + b2[e]
            mask = (routes == e)[:, None]
            out = jnp.where(mask, y, out)
        out = out * route_prob_max[:, None]
        return out.reshape(b, s, d)

    def _L3_xattn_ref(x, encoder_output, mask, WQ, WK, WV, WO):
        import jax, jax.numpy as jnp
        import numpy as np
        B, S, D, H = (2, 256, 128, 16)
        DK = D // H
        SQRT_DK = DK ** 0.5
        NEG = -1000000000.0
        b, s, d = x.shape
        q = (x @ WQ).reshape(b, s, H, DK).transpose(0, 2, 1, 3)
        k = (encoder_output @ WK).reshape(b, s, H, DK).transpose(0, 2, 1, 3)
        v = (encoder_output @ WV).reshape(b, s, H, DK).transpose(0, 2, 1, 3)
        scores = jnp.einsum('bhqd,bhkd->bhqk', q, k) / SQRT_DK
        future = jnp.triu(jnp.ones((s, s), jnp.int32), 1)
        m = mask[:, None, :, None] + future[None, None, :, :]
        scores = jnp.where(m != 0, NEG, scores)
        attn = jax.nn.softmax(scores, axis=-1)
        ctx = jnp.einsum('bhqk,bhkd->bqhd', attn, v).reshape(b, s, d)
        return ctx @ WO

    def _L3_ffn_ref(x, W_exp, b_exp, up_weights, up_bias, down_weights, W_con, b_con, down_bias):
        import jax, jax.numpy as jnp
        import numpy as np
        D_MODEL = 128
        EXPANSION = 4
        D_HIDDEN = D_MODEL * EXPANSION
        NUM_STAGES = int(np.log2(D_HIDDEN))

        def butterfly(y, weights, dim):
            lead = y.shape[:-1]
            for stage in range(weights.shape[0]):
                s = 2 ** stage
                nb = dim // (2 * s)
                yr = y.reshape(*lead, nb, 2, s)
                a = yr[..., 0, :]
                b = yr[..., 1, :]
                w = weights[stage].reshape(nb, s, 2, 2)
                na = w[..., 0, 0] * a + w[..., 0, 1] * b
                nb2 = w[..., 1, 0] * a + w[..., 1, 1] * b
                y = jnp.stack([na, nb2], axis=-2).reshape(*lead, dim)
            return y
        h = jnp.einsum('bsd,dh->bsh', x, W_exp) + b_exp
        h = butterfly(h, up_weights, D_HIDDEN)
        h = jax.nn.gelu(h + up_bias, approximate=False)
        h = butterfly(h, down_weights, D_HIDDEN)
        y = jnp.einsum('bsh,hd->bsd', h, W_con) + b_con
        return y + down_bias
    x = x + jnp.tanh(g_xattn[0]) * _L0_xattn_ref(_layernorm(x, axis=-1), ctx_1024, ctx_1024, L0_xattn_wq, L0_xattn_bq, L0_xattn_wk, L0_xattn_bk, L0_xattn_wv, L0_xattn_bv, L0_xattn_wo, L0_xattn_bo)
    x = x + jnp.tanh(g_ffn[0]) * _L0_ffn_ref(_layernorm(x, axis=-1), L0_ffn_w1, L0_ffn_w2)
    x = x + jnp.tanh(g_xattn[1]) * _L1_xattn_ref(_layernorm(x, axis=-1), ctx_1024, ctx_1024, mask_BxSxS2_ff0)
    x = x + jnp.tanh(g_ffn[1]) * _L1_ffn_ref(_layernorm(x, axis=-1), L1_ffn_w_gate, L1_ffn_w_up, L1_ffn_w_down)
    x = x + jnp.tanh(g_xattn[2]) * _L2_xattn_ref(_layernorm(x, axis=-1), ctx_1024, ctx_1024, L2_xattn_w_q, L2_xattn_w_kv, L2_xattn_w_concat)
    x = x + jnp.tanh(g_ffn[2]) * _L2_ffn_ref(_layernorm(x, axis=-1), L2_ffn_switch_w, L2_ffn_switch_b, L2_ffn_w1, L2_ffn_b1, L2_ffn_w2, L2_ffn_b2)
    x = x + jnp.tanh(g_xattn[3]) * _L3_xattn_ref(_layernorm(x, axis=-1), ctx_1024, mask_BxS2_ik0, L3_xattn_WQ, L3_xattn_WK, L3_xattn_WV, L3_xattn_WO)
    x = x + jnp.tanh(g_ffn[3]) * _L3_ffn_ref(_layernorm(x, axis=-1), L3_ffn_W_exp, L3_ffn_b_exp, L3_ffn_up_weights, L3_ffn_up_bias, L3_ffn_down_weights, L3_ffn_W_con, L3_ffn_b_con, L3_ffn_down_bias)
    return x

_drawn_inputs = setup_inputs


def setup_inputs(seed=0):
    import zlib

    import numpy as np

    out = dict(_drawn_inputs(seed))
    spreads = {'L0_xattn_bq': (0.0, 0.445),
     'L0_xattn_bk': (0.0, 0.431),
     'L0_xattn_bv': (0.0, 0.334),
     'L0_xattn_bo': (0.0, 0.1),
     'L2_ffn_switch_b': (0.0, 0.1),
     'L2_ffn_b1': (0.0, 0.516),
     'L2_ffn_b2': (0.0, 0.345),
     'L3_ffn_b_exp': (0.0, 0.1),
     'L3_ffn_up_bias': (0.0, 0.1),
     'L3_ffn_b_con': (0.0, 0.1),
     'L3_ffn_down_bias': (0.0, 0.1)}
    factors = {'g_ffn': 6.195}
    for name, (base, spread) in spreads.items():
        noise = np.random.default_rng([zlib.crc32(name.encode()), seed]).standard_normal(out[name].shape)
        drawn = base * np.exp(spread * noise) if base else spread * noise
        out[name] = jnp.asarray(drawn.astype(out[name].dtype))
    for name, factor in factors.items():
        out[name] = (out[name] * factor).astype(out[name].dtype)
    return out
```

```python
from contextlib import ExitStack

import concourse.bass as bass
from concourse import mybir

ALU = mybir.AluOpType
ACT = mybir.ActivationFunctionType
AX = mybir.AxisListType
F32 = mybir.dt.float32
BF16 = mybir.dt.bfloat16
I32 = mybir.dt.int32

P = 128
NT = 32
NH, DH = 16, 8
NJ, NA = 4, 4
PG = P // NJ
HID = 512
NC = HID // P
NE = 8
GT = 4
NG = NT // GT
STAGES = 9
EPS = 1e-5
MAGIC = 1.5 * 2.0 ** 23
QMAX = 127.0
NEG = -1e9
SCORE_SCALE = DH ** -0.5
L1_SCALE = P ** -0.5
LOOP_FROM, LOOP_TO = 4, 30

LAST_PHASE = "F3"
ORDER = ["L0", "F0", "L1", "F1", "L2", "F2", "L3", "F3"]


def gated_layers(nc, A, out, q_scratch, v_scratch, o_scratch):
    phases = ORDER[:ORDER.index(LAST_PHASE) + 1]
    ctx = ExitStack()
    with ctx:
        def sb(name, shape, dt=F32):
            return ctx.enter_context(nc.sbuf_tensor(name, shape, dt))

        def sem(name):
            return ctx.enter_context(nc.semaphore(name))

        bank = [ctx.enter_context(nc.psum_tensor(f"bank{i}", [P, 512], F32)) for i in range(8)]

        x = sb("x", [P, NT * P])
        context = sb("context", [P, NT * P])
        contextT = sb("contextT", [P, NT * P])
        shared = sb("shared", [P, NT * P])
        add_mask = open_mask = shared
        stats = sb("stats", [P, NT, 6])
        mean = sb("mean", [P, NT])
        rstd = sb("rstd", [P, NT])
        var_a = sb("var_a", [P, NT])
        var_b = sb("var_b", [P, NT])
        mean_mat = sb("mean_mat", [P, P])
        ident = sb("ident", [P, P])
        ident_bf = sb("ident_bf", [P, P], BF16)
        ones = sb("ones", [P, P])
        gates = sb("gates", [P, 8])
        tgate = sb("tgate", [P, 8])

        l0_nat = sb("l0_nat", [P, 4, P])
        l0_T = sb("l0_T", [P, 4, P])
        bq_row = sb("bq_row", [P, P])
        bv_row = sb("bv_row", [P, P])
        bo_row = sb("bo_row", [P, P])
        key_add_l0 = sb("key_add_l0", [P, P])
        key_add = sb("key_add", [P, 1])
        late = sb("late", [P, 8 * HID])
        quant_src = late[:, 0:3 * HID].rearrange("p (i f) -> p i f", i=3)
        quant_tmp = late[:, 3 * HID:6 * HID].rearrange("p (i f) -> p i f", i=3)
        bf_t = late[:, 0:4 * HID].rearrange("p (i f) -> p i f", i=4)
        bf_w = late[:, 4 * HID:8 * HID].rearrange("p (i f) -> p i f", i=2)
        quant_bf = sb("quant_bf", [P, 3, HID], BF16)
        quant_sum = sb("quant_sum", [P, 3])
        quant_scale = sb("quant_scale", [P, 3])
        quant_inv = sb("quant_inv", [P, 3])
        ffn_wT = sb("ffn_wT", [P, 3, HID], BF16)
        ffn_sw = sb("ffn_sw", [P, 3])
        wq_pad = sb("wq_pad", [P, NA, NJ, PG])
        wk_pad = sb("wk_pad", [P, NA, NJ, PG])
        l2_wq = sb("l2_wq", [P, P])
        l2_wkv = sb("l2_wkv", [P, 2 * DH])
        l2_wo = sb("l2_wo", [P, P])
        l3_wq = sb("l3_wq", [P, P])
        l3_wk = sb("l3_wk", [P, P])
        l3_wv = sb("l3_wv", [P, P])
        l3_wo = sb("l3_wo", [P, P])
        future_add = sb("future_add", [P, P])
        future_one = sb("future_one", [P, P])
        mask_nat = sb("mask_nat", [NT, P], I32)
        mask_f = sb("mask_f", [NT, P])
        keep = sb("keep", [P, NT])
        switch_w = sb("switch_w", [P, NE])
        switch_b = sb("switch_b", [P, NE])
        moe_w1 = sb("moe_w1", [P, NE, HID])
        moe_w2 = sb("moe_w2", [P, NE, NC, P])
        moe_b1 = sb("moe_b1", [P, NE * NC])
        moe_b1n = sb("moe_b1n", [NE * NC, P])
        moe_b2 = sb("moe_b2", [NE, P])
        con_nat = sb("con_nat", [P, NC, P])
        con_bias = sb("con_bias", [P, 2, P])
        bf_up = sb("bf_up", [P, 2, 2, HID])
        bf_dn = sb("bf_dn", [P, 2, HID])
        up_bias = sb("up_bias", [P, NC])
        up_row = sb("up_row", [1, HID])
        w_down = sb("w_down", [P, NC, P])

        stage_q = moe_w1[:, :, :].rearrange("p e (c d) -> p (e c) d", d=P)
        stage_v = moe_w2[:, :, :, :].rearrange("p e c d -> p (e c) d")

        xn = sb("xn", [P, 2, P])
        xnT = sb("xnT", [P, 2, P])
        hid_space = sb("hid_space", [P, 8 * HID // 2])
        ctx_pad = hid_space[:, 0:2 * HID].rearrange("p (b a j d) -> p b a j d", b=2, a=NA, j=NJ)
        q_rows = hid_space[:, 2 * HID:4 * HID].rearrange("p (b a j d) -> p b a j d", b=2, a=NA, j=NJ)
        hid = hid_space[:, 0:2 * HID].rearrange("p (b f) -> p b f", b=2)
        hid2 = hid_space[:, 2 * HID:4 * HID].rearrange("p (b f) -> p b f", b=2)
        ctx_one = sb("ctx_one", [P, 2, P])
        qT = sb("qT", [P, 2, NA, P])
        kT = sb("kT", [P, 2, NA, P])
        vals = sb("vals", [P, 2, NH, DH + 1])
        nmax = sb("nmax", [P, 2, NA, NJ, PG])
        masked = hid2.rearrange("p b (a k) -> p b a k", a=NA)
        probs = sb("probs", [P, NJ, NA, P])
        o_inv = sb("o_inv", [P, 2, NH])
        o_tok = sb("o_tok", [P, 2, P])
        oT = sb("oT", [P, 2, P])
        hidT = context[:, :].rearrange("p (b f) -> p b f", b=2)
        hid_bf = sb("hid_bf", [P, 2, HID], BF16)
        hidT_bf = sb("hidT_bf", [P, 2, HID], BF16)
        xq_f = sb("xq_f", [P, 2, P])
        xq_bf = sb("xq_bf", [P, 2, P], BF16)
        xqT_bf = sb("xqT_bf", [P, 2, P], BF16)
        small = sb("small", [P, 2, 16])
        logits = sb("logits", [P, NT, NE])
        route_a = sb("route_a", [P, NT, NE])
        route_b = sb("route_b", [P, NT, NE])
        route_m = sb("route_m", [P, 3, NT])
        expert_no = sb("expert_no", [P, NE])
        expert_up = sb("expert_up", [P, NE])
        gate_of = sb("gate_of", [P, NT, NE])
        gateT = sb("gateT", [NE, 2, P])

        s = {}
        FOUR_A_TILE = {"st", "sp", "ex", "mx", "mk", "pv", "qb"}
        OF_L0_TOO = {"qp", "kp", "ke", "qe", "st", "ex", "mx", "ma", "mt", "sp", "pv", "oi", "on", "cs"}

        def shared_name(name):
            phase, _, signal = name.partition("_")
            a_tile = 5 if signal == "qa" else 4 if signal in FOUR_A_TILE else 1
            if phase in ("L0", "L2", "L3") and (phase != "L0" or signal in OF_L0_TOO):
                before = {"L0": 0, "L2": 1, "L3": 2}[phase] - (signal not in OF_L0_TOO)
                if signal in ("mk", "om", "causal"):
                    before = 0
                return "att_" + signal, before * a_tile * NT
            if phase in ("F0", "F1"):
                return "bit_" + signal, (phase == "F1" and signal != "hm") * a_tile * NT
            return name, 0

        def S(name):
            name = shared_name(name)[0]
            if name not in s:
                s[name] = sem(name)
            return s[name]

        def wait(eng, name, value):
            if not isinstance(value, int) or value > 0:
                eng.wait_ge(S(name), value + shared_name(name)[1])
                if not isinstance(value, int) and eng.engine in (nc.sync.engine, nc.gpsimd.engine):
                    eng.sem_inc(S("sp_passed" if eng.engine == nc.sync.engine else "pool_passed"), 1)

        def live(u):
            return not isinstance(u, int) or 0 <= u < NT

        def each_tile(eng, body, lead=1, tail=1):
            for t in range(-lead, LOOP_FROM):
                body(t, t % 2)
            with eng.Fori(LOOP_FROM, LOOP_TO - 1, 2) as i:
                body(i, 0)
                body(i + 1, 1)
            for t in range(LOOP_TO, NT + tail):
                body(t, t % 2)

        def tile_of(buf, t):
            return buf[:, bass.ds(t * P, P)]

        def column(buf, t):
            return buf[:, bass.ds(t, 1)]

        def over_blocks(ap, n):
            return ap.unsqueeze(1).broadcast_to([ap.shape[0], n, ap.shape[1]])

        ATT = {
            "L0": dict(gate=0), "L2": dict(gate=2), "L3": dict(gate=3),
        }

        def pad_weights(pool, layer):
            pool.wait_ge(S("w_att"), 16 * 7)
            if layer == "L2":
                pool.memset(wq_pad[:, :, :, :], 0.0).then_inc(S("pad"), 1)
                pool.memset(wk_pad[:, :, :, :], 0.0).then_inc(S("pad"), 1)
                pool.wait_ge(S("pad"), 2)
                pool.tensor_copy(wq_pad[:, :, :, 0:DH].rearrange("i a j d -> i (a j) d"),
                                 l2_wq[:, :].rearrange("i (h d) -> i h d", d=DH)).then_inc(S("pad"), 1)
                pool.tensor_copy(wk_pad[:, 0, :, 0:DH], over_blocks(l2_wkv[:, 0:DH], NJ)).then_inc(S("pad"), 1)
            else:
                wait(pool, "L2_qp", NT)
                wait(pool, "L2_kp", NT)
                pool.tensor_copy(wq_pad[:, :, :, 0:DH].rearrange("i a j d -> i (a j) d"),
                                 l3_wq[:, :].rearrange("i (h d) -> i h d", d=DH)).then_inc(S("pad"), 1)
                pool.tensor_copy(wk_pad[:, :, :, 0:DH].rearrange("i a j d -> i (a j) d"),
                                 l3_wk[:, :].rearrange("i (h d) -> i h d", d=DH)).then_inc(S("pad"), 1)

        block = ctx.enter_context(nc.Block())

        @block.sync
        def _(sp):
            tok = "b s d -> s b d"
            for c in range(4):
                b = slice(8 * c, 8 * c + 8)
                sp.dma_start(x[:, 1024 * c:1024 * c + 1024].rearrange("p (b d) -> p b d", d=P),
                             A["x"][b].rearrange(tok)).then_inc(S("x_in"), 16)
                if c == 0:
                    sp.dma_start(l0_nat[:, 0, :], A["L0_xattn_wq"]).then_inc(S("w_l0"), 16)
                    sp.dma_start(l0_nat[:, 1, :], A["L0_xattn_wk"]).then_inc(S("w_l0"), 16)
                    sp.dma_start(l0_nat[:, 2, :], A["L0_xattn_wv"]).then_inc(S("w_l0"), 16)
                    sp.dma_start(l0_nat[:, 3, :], A["L0_xattn_wo"]).then_inc(S("w_l0"), 16)
            for c in range(4):
                b = slice(8 * c, 8 * c + 8)
                sp.dma_start(context[:, 1024 * c:1024 * c + 1024].rearrange("p (b d) -> p b d", d=P),
                             A["ctx_1024"][b].rearrange(tok)).then_inc(S("ctx_in"), 16)

            def l0b(t, p):
                u = t + 2
                if live(u):
                    wait(sp, "L0_q_in", 16 * u)
                    wait(sp, "L0_qp", u - 1)
                    sp.dma_start(q_rows[:, p, :, :, 0:DH].rearrange("i a j d -> i (a j) d"),
                                 q_scratch[bass.ds(u, 1)].rearrange("u h i d -> i (u h) d")).then_inc(S("L0_q_in"), 16)
                    wait(sp, "L0_v_in", 16 * u)
                    wait(sp, "L0_pv", 4 * (u - 1))
                    sp.dma_start(vals[:, p, :, 0:DH],
                                 v_scratch[bass.ds(u, 1)].rearrange("u h i d -> i (u h) d")).then_inc(S("L0_v_in"), 16)
                u = t - 1
                if live(u):
                    wait(sp, "L0_o_out", 16 * u)
                    wait(sp, "L0_on", u + 1)
                    sp.dma_start(o_scratch[bass.ds(u, 1)].rearrange("u h i d -> i (u h) d"),
                                 o_tok[:, 1 - p, :].rearrange("i (h d) -> i h d", d=DH)).then_inc(S("L0_o_out"), 16)
                u = t - 2
                if live(u):
                    wait(sp, "L0_o_out", 16 * (u + 1))
                    wait(sp, "L0_o_in", 16 * u)
                    sp.dma_start(tile_of(shared, u),
                                 o_scratch[bass.ds(u, 1)].rearrange("u h (r c) d -> (u h r) (c d)", r=8)
                                 ).then_inc(S("L0_o_in"), 16)

            for c in range(4):
                sp.wait_ge(S("a_qv"), 2 * 8 * (c + 1))
                for scratch, stage in ((q_scratch, stage_q), (v_scratch, stage_v)):
                    sp.dma_start(scratch[8 * c:8 * c + 8].rearrange("u h (r c) d -> (h r) u (c d)", r=8),
                                 stage[:, 8 * c:8 * c + 8, :]).then_inc(S("l0a_stored"), 16)
            sp.wait_ge(S("l0a_stored"), 16 * 8)
            sp.wait_ge(S("pool_set"), 9)
            each_tile(sp, l0b, lead=2, tail=2)

            sp.wait_ge(S("c_os"), NT)
            sp.dma_start(add_mask[:, :].rearrange("p (b d) -> p b d", d=P),
                         A["mask_BxSxS2_ff0"].rearrange(tok)).then_inc(S("mask_in"), 16)
            sp.dma_start(moe_w1[:, :, :], A["L2_ffn_w1"].rearrange("e d f -> d e f")).then_inc(S("w_exp"), 16)
            sp.dma_start(moe_w2[:, :, :, :].rearrange("p e c d -> p (e c) d"),
                         A["L2_ffn_w2"].rearrange("e (c p) d -> p (e c) d", p=P)).then_inc(S("w_exp"), 16)
            if "F1" in phases:
                sp.wait_ge(S("wq_ready"), 2)
                for i, name in enumerate(("L1_ffn_w_gate", "L1_ffn_w_up")):
                    sp.dma_start(quant_src[:, i, :].rearrange("p (c d) -> p c d", d=P),
                                 A[name].rearrange("(c p) d -> p c d", p=P)).then_inc(S("w_f1"), 16)
                sp.dma_start(quant_src[:, 2, :], A["L1_ffn_w_down"]).then_inc(S("w_f1"), 16)
            if "F3" in phases:
                for n in range(2 * STAGES):
                    src = A["L3_ffn_up_weights"][n] if n < STAGES else A["L3_ffn_down_weights"][2 * STAGES - 1 - n]
                    if n >= 2:
                        wait(sp, "bf_used", n - 1)
                    else:
                        sp.wait_ge(S("wq_ready"), 5)
                    wait(sp, "bf_in", 16 * n)
                    sp.dma_start(bf_w[:, n % 2, :],
                                 src.rearrange("k i j -> (k i j)").unsqueeze(0).broadcast_to([P, 1024])
                                 ).then_inc(S("bf_in"), 16)

            if "L3" in phases:
                sp.wait_ge(S("F2_hp"), NG * NE * NC)
                sp.dma_start(open_mask[:, :].bitcast(I32),
                             A["mask_BxS2_ik0"].rearrange("b s -> (b s)").unsqueeze(0).broadcast_to([P, NT * P])
                             ).then_inc(S("open_in"), 16)
            done = {"L0": "c_res", "F0": "F0_res", "L1": "L1_res", "F1": "F1_res", "L2": "L2_res",
                    "F2": "B_res", "L3": "L3_res", "F3": "F3_res"}[LAST_PHASE]

            def store(t, p):
                u = t - 1
                if live(u):
                    wait(sp, done, u + 1)
                    sp.dma_start(out[bass.ds(u, 1)].rearrange("u s d -> (u s) d"),
                                 tile_of(x, u)).then_inc(S("stored"), 16)
            each_tile(sp, store)
            sp.wait_ge(S("stored"), 16 * NT)
            wait(sp, "L0_o_in", 16 * NT)

        @block.gpsimd
        def _(pool):
            n_set = 0

            def const(ins):
                nonlocal n_set
                n_set += 1
                ins.then_inc(S("pool_set"), 1)

            def settle():
                pool.wait_ge(S("pool_set"), n_set)

            const(pool.memset(ident[:, :], 0.0))
            const(pool.memset(ones[:, :], 1.0))
            settle()
            const(pool.affine_select(out=ident[:, :], in_=ident[:, :], compare_op=ALU.not_equal, fill=1.0,
                                     base=0, pattern=[[-1, P]], channel_multiplier=1))
            settle()
            const(pool.tensor_copy(ident_bf[:, :], ident[:, :]))
            settle()
            const(pool.memset(key_add[:, :], 0.0))
            const(pool.memset(ctx_pad[:, :, :, :, :], 0.0))
            const(pool.memset(q_rows[:, :, :, :, :], 0.0))
            const(pool.memset(nmax[:, :, :, :, :], 0.0))
            const(pool.memset(vals[:, :, :, :], 1.0))
            settle()
            for j in range(NJ):
                const(pool.affine_select(out=key_add[:, :], in_=key_add[:, :], compare_op=ALU.not_equal,
                                         fill=1.0, base=-(PG * j + DH), pattern=[[0, 1]], channel_multiplier=1))
                settle()
            pool.wait_ge(S("bias_in"), 16 * 4)
            const(pool.affine_select(out=key_add_l0[:, :].rearrange("p n -> p n"), in_=key_add_l0[:, :],
                                     compare_op=ALU.not_equal, fill=1.0, base=-DH, pattern=[[0, P]],
                                     channel_multiplier=1))
            settle()
            for j in range(1, NJ):
                const(pool.affine_select(out=key_add_l0[:, :], in_=key_add_l0[:, :],
                                         compare_op=ALU.not_equal, fill=1.0, base=-(PG * j + DH),
                                         pattern=[[0, P]], channel_multiplier=1))
                settle()
            pool.memset(future_add[:, :], 0.0).then_inc(S("fut"), 1)
            pool.memset(future_one[:, :], 0.0).then_inc(S("fut"), 1)
            pool.wait_ge(S("fut"), 2)
            pool.affine_select(out=future_add[:, :], in_=future_add[:, :], compare_op=ALU.is_ge, fill=NEG,
                               base=0, pattern=[[-1, P]], channel_multiplier=1).then_inc(S("fut"), 1)
            pool.affine_select(out=future_one[:, :], in_=future_one[:, :], compare_op=ALU.is_ge, fill=1.0,
                               base=0, pattern=[[1, P]], channel_multiplier=-1).then_inc(S("fut"), 1)
            pool.iota(expert_no[:, :], [[1, NE]], base=0, channel_multiplier=0,
                      allow_small_or_imprecise_dtypes=True).then_inc(S("fut"), 1)

            def ctx_copy(layer, padded):
                def body(t, p):
                    u = t + 1
                    if live(u):
                        if padded:
                            wait(pool, layer + "_kp", u - 1)
                            pool.tensor_copy(ctx_pad[:, 1 - p, :, :, 0:DH].rearrange("i a j d -> i (a j) d"),
                                             tile_of(contextT, u).rearrange("i (h d) -> i h d", d=DH)
                                             ).then_inc(S(layer + "_cs"), 1)
                        else:
                            wait(pool, layer + "_vp", u - 1)
                            pool.tensor_copy(ctx_one[:, 1 - p, :], tile_of(contextT, u)
                                             ).then_inc(S(layer + "_cs"), 1)
                    if layer == "L3" and live(t):
                        for j in range(NJ):
                            wait(pool, "L3_ex", 4 * t + j + 1)
                            pool.affine_select(out=probs[:, j, :, :], in_=probs[:, j, :, :],
                                               compare_op=ALU.is_ge, fill=0.0, base=0,
                                               pattern=[[0, NA], [1, P]],
                                               channel_multiplier=-1).then_inc(S("L3_causal"), 1)
                each_tile(pool, body)


            def keep_ctxT(t, p):
                if live(t):
                    wait(pool, "a_cs", t + 1)
                    pool.tensor_copy(tile_of(contextT, t), oT[:, p, :]).then_inc(S("a_ctxT"), 1)
            each_tile(pool, keep_ctxT)
            ctx_copy("L0", True)
            if "L2" in phases:
                pad_weights(pool, "L2")

            if "L2" in phases:
                ctx_copy("L2", False)
            if "F3" in phases:
                pool.wait_ge(S("w_f3"), 16 * 2)
                pool.wait_ge(S("con_T"), 1)
                pool.wait_ge(S("wq_ready"), 5)
                step = 0
                for n in range(2 * STAGES):
                    up = n < STAGES
                    k = n if up else 2 * STAGES - 1 - n
                    w_n = 2 ** k
                    src, dst = n % 2, (n + 1) % 2
                    pool.wait_ge(S("bf_in"), 16 * (n + 1))
                    wv = bf_w[:, n % 2, :].rearrange("p (n s c) -> p c n s", s=w_n, c=4)
                    if up:
                        m = 2

                        def half(buf, i):
                            return buf.rearrange("p m (n two s) -> p two m n s", two=2, s=w_n)[:, i]

                        def tmp(i):
                            return bf_t[:, i, :].rearrange("p (m n s) -> p m n s", m=m, s=w_n)

                        def wgt(c):
                            return wv[:, c].unsqueeze(1).broadcast_to([P, m, HID // 2 // w_n, w_n])
                        a_in, b_in = half(bf_up[:, src], 0), half(bf_up[:, src], 1)
                        a_out, b_out = half(bf_up[:, dst], 0), half(bf_up[:, dst], 1)
                        order = (0, 1, 2, 3)
                    else:
                        src, dst = (n - STAGES) % 2, (n - STAGES + 1) % 2

                        def half(buf, i):
                            return buf.rearrange("p (n two s) -> p two n s", two=2, s=w_n)[:, i]

                        def tmp(i):
                            return bf_t[:, i, 0:HID // 2].rearrange("p (n s) -> p n s", s=w_n)

                        def wgt(c):
                            return wv[:, c]
                        a_in, b_in = half(bf_dn[:, src], 0), half(bf_dn[:, src], 1)
                        a_out, b_out = half(bf_dn[:, dst], 0), half(bf_dn[:, dst], 1)
                        order = (0, 2, 1, 3)
                    for i, (c, d) in enumerate(zip(order, (a_in, b_in, a_in, b_in))):
                        last = pool.tensor_tensor(tmp(i), d, wgt(c), ALU.mult)
                        last.then_inc(S("bf_step"), 1)
                    step += 4
                    pool.wait_ge(S("bf_step"), step)
                    pool.tensor_tensor(a_out, tmp(0), tmp(1), ALU.add).then_inc(S("bf_step"), 1)
                    pool.tensor_tensor(b_out, tmp(2), tmp(3), ALU.add).then_inc(S("bf_step"), 1)
                    step += 2
                    pool.wait_ge(S("bf_step"), step)
                    pool.sem_inc(S("bf_used"), 1)
            if "L3" in phases:
                pad_weights(pool, "L3")
                ctx_copy("L3", False)

        @block.scalar
        def _(act):
            def row(name):
                return A[name].unsqueeze(0).broadcast_to([P, A[name].shape[0]])
            act.dma_start(gates[:, 0:4], row("g_xattn")).then_inc(S("gates_in"), 16)
            act.dma_start(gates[:, 4:8], row("g_ffn")).then_inc(S("gates_in"), 16)
            act.dma_start(bq_row[:, :], row("L0_xattn_bq")).then_inc(S("bias_in"), 16)
            act.dma_start(bv_row[:, :], row("L0_xattn_bv")).then_inc(S("bias_in"), 16)
            act.dma_start(bo_row[:, :], row("L0_xattn_bo")).then_inc(S("bias_in"), 16)
            act.dma_start(key_add_l0[:, :], row("L0_xattn_bk")).then_inc(S("bias_in"), 16)
            act.dma_start(quant_src[:, 0, :].rearrange("p (c d) -> p c d", d=P),
                          A["L0_ffn_w1"].rearrange("(c p) d -> p c d", p=P)).then_inc(S("w_f0"), 16)
            act.dma_start(quant_src[:, 2, :], A["L0_ffn_w2"]).then_inc(S("w_f0"), 16)
            act.dma_start(l2_wq[:, :], A["L2_xattn_w_q"]).then_inc(S("w_att"), 16)
            act.dma_start(l2_wkv[:, :], A["L2_xattn_w_kv"]).then_inc(S("w_att"), 16)
            act.dma_start(l2_wo[:, :], A["L2_xattn_w_concat"]).then_inc(S("w_att"), 16)
            act.dma_start(l3_wq[:, :], A["L3_xattn_WQ"]).then_inc(S("w_att"), 16)
            act.dma_start(l3_wk[:, :], A["L3_xattn_WK"]).then_inc(S("w_att"), 16)
            act.dma_start(l3_wv[:, :], A["L3_xattn_WV"]).then_inc(S("w_att"), 16)
            act.dma_start(l3_wo[:, :], A["L3_xattn_WO"]).then_inc(S("w_att"), 16)
            act.dma_start(switch_w[:, :], A["L2_ffn_switch_w"]).then_inc(S("w_moe"), 16)
            act.dma_start(switch_b[:, :], row("L2_ffn_switch_b")).then_inc(S("w_moe"), 16)
            act.dma_start(moe_b1n[:, :], A["L2_ffn_b1"].rearrange("e (c p) -> (e c) p", p=P)).then_inc(S("w_moe"), 16)
            act.dma_start(moe_b2[:, :], A["L2_ffn_b2"]).then_inc(S("w_moe"), 16)
            act.dma_start(con_nat[:, :, :], A["L3_ffn_W_con"].rearrange("(c p) d -> p c d", p=P)).then_inc(S("w_con"), 16)
            act.dma_start(con_bias[:, 0, :], row("L3_ffn_b_con")).then_inc(S("w_con"), 16)
            act.dma_start(con_bias[:, 1, :], row("L3_ffn_down_bias")).then_inc(S("w_con"), 16)
            act.dma_start(up_row[:, :], A["L3_ffn_up_bias"].unsqueeze(0)).then_inc(S("w_con"), 16)
            act.dma_start(bf_up[:, 0, 0, :], A["L3_ffn_W_exp"]).then_inc(S("w_f3"), 16)
            act.dma_start(bf_up[:, 0, 1, :], row("L3_ffn_b_exp")).then_inc(S("w_f3"), 16)
            act.dma_start(mask_nat[:, :], A["mask_BxS2_ik0"]).then_inc(S("keep_in"), 16)

            act.wait_ge(S("gates_in"), 32)
            act.activation(tgate[:, :], gates[:, :], ACT.Tanh).then_inc(S("tgate"), 1)

            def root(n):
                act.wait_ge(S("var"), n)
                act.activation(var_a[:, :], var_b[:, :], ACT.Sqrt).then_inc(S("std"), 1)

            root(1)

            def l0a(t, p):
                u = t
                if live(u):
                    wait(act, "a_xt", u + 1)
                    wait(act, "a_qp", u - 1)
                    act.activation(xnT[:, p, :], bank[p][:, 0:P], ACT.Copy).then_inc(S("a_xe"), 1)
            each_tile(act, l0a)

            def attention(layer):
                wide = layer != "L2"

                def body(t, p):
                    u = t - 1
                    if live(u) and layer != "L0":
                        wait(act, layer + "_ot", u + 1)
                        wait(act, layer + "_yp", u - 1)
                        act.activation(oT[:, 1 - p, :], bank[4][:, 256:384], ACT.Copy).then_inc(S(layer + "_oe"), 1)
                    u = t + 1
                    if live(u):
                        if layer != "L0":
                            wait(act, layer + "_xt", u + 1)
                            wait(act, layer + "_qp", u - 1)
                            act.activation(xnT[:, 1 - p, :], bank[7][:, 0:P], ACT.Copy).then_inc(S(layer + "_xe"), 1)
                            wait(act, layer + "_vp", u + 1)
                            wait(act, layer + "_pv", 4 * (u - 1))
                            if wide:
                                act.activation(vals[:, 1 - p, :, 0:DH],
                                               bank[7][:, P:2 * P].rearrange("k (h d) -> k h d", d=DH),
                                               ACT.Copy).then_inc(S(layer + "_ve"), 1)
                            else:
                                act.activation(vals[:, 1 - p, 0, 0:DH], bank[7][:, P:P + DH],
                                               ACT.Copy).then_inc(S(layer + "_ve"), 1)
                        wait(act, layer + "_qp", u + 1)
                        wait(act, layer + "_st", 4 * (u - 1))
                        act.activation(qT[:, 1 - p, :, :].rearrange("c a q -> c (a q)"), bank[5][:, :], ACT.Copy,
                                       scale=SCORE_SCALE).then_inc(S(layer + "_qe"), 1)
                    if live(t):
                        for j in range(NJ):
                            wait(act, layer + "_st", 4 * t + j + 1)
                            wait(act, layer + "_pv", 4 * (t - 1) + j + 1)
                            act.activation(probs[:, j, :, :].rearrange("k a q -> k (a q)"), bank[2 + j % 2][:, :],
                                           ACT.Exp).then_inc(S(layer + "_ex"), 1)
                each_tile(act, body)

            attention("L0")

            def l0c(t, p):
                if live(t):
                    wait(act, "c_ot", t + 1)
                    wait(act, "c_yp", t - 1)
                    act.activation(oT[:, p, :], bank[p][:, 0:P], ACT.Copy).then_inc(S("c_oe"), 1)
            each_tile(act, l0c)

            def bit_ffn(layer, gated):
                def body(t, p):
                    u = t + 1
                    if live(u):
                        wait(act, layer + "_xt", u + 1)
                        wait(act, layer + "_hp", u - 1)
                        act.activation(xqT_bf[:, 1 - p, :], bank[5][:, :].bitcast(BF16)[:, 0:P],
                                       ACT.Copy).then_inc(S(layer + "_xe"), 1)
                        wait(act, layer + "_hp", u + 1)
                        wait(act, layer + "_hq", u - 1)
                        act.activation(hid[:, 1 - p, :], bank[2 * (1 - p)][:, :], ACT.Silu if gated else ACT.Gelu,
                                       scale=small[:, 1 - p, 3:4]).then_inc(S(layer + "_ge"), 1)
                    if live(t):
                        wait(act, layer + "_ht", t + 1)
                        wait(act, layer + "_yp", t - 1)
                        act.activation(hidT_bf[:, p, :], bank[4][:, :].bitcast(BF16)[:, 0:HID],
                                       ACT.Copy).then_inc(S(layer + "_he"), 1)
                each_tile(act, body)

            if "F0" in phases:
                root(2)
                bit_ffn("F0", False)
            if "L1" in phases:
                root(3)

                def l1(t, p):
                    u = t + 1
                    if live(u):
                        wait(act, "L1_xt", u + 1)
                        wait(act, "L1_sp", u - 1)
                        act.activation(xnT[:, 1 - p, :], bank[0][:, 0:P], ACT.Copy).then_inc(S("L1_xe"), 1)
                        wait(act, "L1_nm", u + 1)
                        wait(act, "L1_tp", u - 1)
                        act.activation(hid2[:, 1 - p, 0:P], hid[:, 1 - p, 0:P], ACT.Exp,
                                       bias=small[:, 1 - p, 0:1],
                                       accum_out=small[:, 1 - p, 1:2]).then_inc(S("L1_ex"), 1)
                    if live(t):
                        wait(act, "L1_tp", t + 1)
                        wait(act, "L1_pv", t - 1)
                        act.activation(oT[:, p, :], bank[2][:, 0:P], ACT.Copy).then_inc(S("L1_te"), 1)
                each_tile(act, l1)
            if "F1" in phases:
                root(4)
                bit_ffn("F1", True)
            if "L2" in phases:
                root(5)
                attention("L2")
            if "F2" in phases:
                root(6)

                def route(t, p):
                    if live(t):
                        wait(act, "R_xt", t + 1)
                        wait(act, "R_lp", t - 1)
                        wait(act, "R_xd", t - 1)
                        act.activation(xnT[:, p, :], bank[p][:, 0:P], ACT.Copy).then_inc(S("R_xe"), 1)
                each_tile(act, route)
                act.wait_ge(S("R_sub"), 1)
                act.activation(route_a[:, :, :], route_b[:, :, :], ACT.Exp).then_inc(S("R_exp"), 1)

                def experts(g):
                    for e in range(NE):
                        n = g * NE + e
                        wait(act, "F2_yt", GT * (n - 1))
                        for c in range(NC):
                            wait(act, "F2_hp", n * NC + c + 1)
                            act.activation(hidT[:, e % 2, c * HID:(c + 1) * HID], bank[c][:, :],
                                           ACT.Gelu_apprx_tanh,
                                           bias=moe_b1[:, e * NC + c:e * NC + c + 1]).then_inc(S("F2_ge"), 1)
                act.wait_ge(S("R_b1"), 1)
                experts(0)
                with act.Fori(1, NG, 1) as g:
                    experts(g)
            if "L3" in phases:
                root(7)
                attention("L3")
            if "F3" in phases:
                root(8)
                act.wait_ge(S("f3_bias"), 1)

                def f3(t, p):
                    u = t + 1
                    if live(u):
                        wait(act, "F3_xt", u + 1)
                        wait(act, "F3_hp", u - 1)
                        act.activation(xnT[:, 1 - p, :], bank[4][:, 0:P], ACT.Copy).then_inc(S("F3_xe"), 1)
                        wait(act, "F3_hp", u + 1)
                        wait(act, "F3_yp", u - 1)
                        for c in range(NC):
                            g = act.activation(hid[:, 1 - p, c * P:(c + 1) * P], bank[1 - p][:, c * P:(c + 1) * P],
                                               ACT.Gelu, bias=up_bias[:, c:c + 1])
                        g.then_inc(S("F3_ge"), 1)
                each_tile(act, f3)

        @block.tensor
        def _(pe):
            pe.wait_ge(S("pool_set"), 4)
            pe.wait_ge(S("w_l0"), 64)
            for i in range(4):
                m = pe.transpose(bank[7][:, i * P:(i + 1) * P], l0_nat[:, i, :], ident[:, :])
            m.then_inc(S("wT"), 1)
            pe.wait_ge(S("w_con"), 64)
            for i in range(NC):
                m = pe.transpose(bank[6][:, i * P:(i + 1) * P], con_nat[:, i, :], ident[:, :])
            m.then_inc(S("wT"), 1)
            pe.wait_ge(S("w_moe"), 16 * 4)
            pe.transpose(bank[5][:, 0:NE * NC], moe_b1n[:, :], ident[0:NE * NC, 0:NE * NC]).then_inc(S("wT"), 1)
            pe.wait_ge(S("mask_f"), 1)
            pe.transpose(bank[5][:, P:P + NT], mask_f[:, :], ident[0:NT, 0:NT]).then_inc(S("wT"), 1)
            pe.wait_ge(S("wT_out"), 1)

            def l0a(t, p):
                u = t
                if live(u):
                    wait(pe, "a_xn", u + 1)
                    wait(pe, "a_xe", u - 1)
                    wait(pe, "a_cs", u - 1)
                    pe.transpose(bank[p][:, 0:P], xn[:, p, :], ident[:, :])
                    pe.transpose(bank[4 + p][:, 0:P], ctx_one[:, p, :], ident[:, :]).then_inc(S("a_xt"), 1)
                    wait(pe, "a_xe", u + 1)
                    wait(pe, "a_cs", u + 1)
                    wait(pe, "a_qv", 2 * (u - 1))
                    pe.matmul(bank[2 + p][:, 0:P], xnT[:, p, :], l0_T[:, 0, :], start=True, stop=True)
                    pe.matmul(bank[2 + p][:, P:2 * P], oT[:, p, :], l0_T[:, 2, :], start=True,
                              stop=True).then_inc(S("a_qp"), 1)
            each_tile(pe, l0a)

            def attention(layer):
                wide = layer != "L2"
                if layer == "L0":
                    pe.wait_ge(S("pool_set"), 17)
                else:
                    pe.wait_ge(S("pad"), 4 if layer == "L2" else 6)

                def tokens(u, p):
                    wait(pe, layer + "_xn", u + 1)
                    wait(pe, layer + "_ve", u)
                    pe.transpose(bank[7][:, 0:P], xn[:, p, :], ident[:, :]).then_inc(S(layer + "_xt"), 1)

                def own_values(u, p):
                    wait(pe, layer + "_xe", u + 1)
                    if wide:
                        m = pe.matmul(bank[7][:, P:2 * P], ctx_one[:, p, :], l3_wv[:, :], start=True, stop=True)
                    else:
                        m = pe.matmul(bank[7][:, P:P + DH], ctx_one[:, p, :], l2_wkv[:, DH:2 * DH],
                                      start=True, stop=True)
                    m.then_inc(S(layer + "_vp"), 1)

                def keys(u, p):
                    wait(pe, layer + "_cs", u + 1)
                    wait(pe, layer + "_ke", u)
                    for a in range(NA if wide else 1):
                        o = bank[6][:, a * P:(a + 1) * P]
                        if layer == "L0":
                            m = pe.matmul(o, ctx_pad[:, p, a, :, :].rearrange("i j d -> i (j d)"), l0_T[:, 1, :],
                                          start=True, stop=True)
                        else:
                            m = pe.matmul(o, wk_pad[:, a, :, :].rearrange("i j d -> i (j d)"),
                                          tile_of(contextT, u), start=True, stop=True)
                    m.then_inc(S(layer + "_kp"), 1)

                def queries(u, p):
                    wait(pe, layer + "_ma", u)
                    if layer == "L0":
                        wait(pe, "L0_q_in", 16 * (u + 1))
                    else:
                        wait(pe, layer + "_xe", u + 1)
                    for a in range(NA):
                        o = bank[5][:, a * P:(a + 1) * P]
                        if layer == "L0":
                            m = pe.transpose(o, q_rows[:, p, a, :, :].rearrange("i j d -> i (j d)"), ident[:, :])
                        else:
                            m = pe.matmul(o, wq_pad[:, a, :, :].rearrange("i j d -> i (j d)"), xnT[:, p, :],
                                          start=True, stop=True)
                    m.then_inc(S(layer + "_qp"), 1)

                def keys_of(p, j, a, rows):
                    return kT[PG * j:PG * j + rows, p, a if wide else 0, :]

                def scores(u, p, j):
                    if j == 0:
                        wait(pe, layer + "_qe", u + 1)
                        wait(pe, layer + "_ke", u + 1)
                    wait(pe, layer + "_mx", 4 * u + j - 1)
                    for a in range(NA):
                        m = pe.matmul(bank[j % 2][:, a * P:(a + 1) * P], qT[PG * j:PG * j + DH, p, a, :],
                                      keys_of(p, j, a, DH), start=True, stop=True)
                    m.then_inc(S(layer + "_sp"), 1)

                def scores_by_key(t, p, j):
                    if j == 0:
                        wait(pe, layer + "_ma", t + 1)
                    wait(pe, layer + "_ex", 4 * t + j - 1)
                    for a in range(NA):
                        m = pe.matmul(bank[2 + j % 2][:, a * P:(a + 1) * P], keys_of(p, j, a, DH + 1),
                                      qT[PG * j:PG * j + DH + 1, p, a, :], start=True, stop=True)
                    m.then_inc(S(layer + "_st"), 1)

                def values(t, p, j):
                    if j == 0:
                        wait(pe, layer + ("_on" if layer == "L0" else "_res"), t)
                        if layer == "L0":
                            wait(pe, "L0_v_in", 16 * (t + 1))
                        else:
                            wait(pe, layer + "_ve", t + 1)
                        if layer == "L3":
                            wait(pe, "L3_om", t + 1)
                            pe.matmul(bank[4][:, 0:NH * (DH + 1)], hid[:, p, 0:P],
                                      vals[:, p, :, :].rearrange("k h d -> k (h d)"), start=True, stop=True)
                    wait(pe, "L3_causal" if layer == "L3" else layer + "_ex", 4 * t + j + 1)
                    for a in range(NA):
                        h = NJ * a + j
                        m = pe.matmul(bank[4][:, h * (DH + 1):(h + 1) * (DH + 1)], probs[:, j, a, :],
                                      vals[:, p, h if wide else 0, :], start=(layer != "L3"),
                                      stop=True,
                                      skip_group_check=(layer == "L3"))
                    m.then_inc(S(layer + "_pv"), 1)

                def body(t, p):
                    if live(t):
                        wait(pe, layer + "_mx", 4 * (t + 1))
                        for a in range(NA):
                            m = pe.transpose(bank[5][:, a * P:(a + 1) * P],
                                             nmax[:, p, a, :, :].rearrange("q j d -> q (j d)"), ident[:, :])
                        m.then_inc(S(layer + "_mt"), 1)
                    if live(t - 1) and layer != "L0":
                        wait(pe, layer + "_on", t)
                        wait(pe, layer + "_oe", t - 1)
                        pe.transpose(bank[4][:, 256:384], o_tok[:, 1 - p, :], ident[:, :]).then_inc(S(layer + "_ot"), 1)
                    if live(t + 1):
                        if layer != "L0":
                            tokens(t + 1, 1 - p)
                        keys(t + 1, 1 - p)
                    if live(t - 1) and layer != "L0":
                        wait(pe, layer + "_oe", t)
                        wait(pe, layer + "_res", t - 1)
                        pe.matmul(bank[4][:, 384:512], oT[:, 1 - p, :], (l2_wo if layer == "L2" else l3_wo)[:, :],
                                  start=True, stop=True).then_inc(S(layer + "_yp"), 1)
                    if live(t + 1):
                        if layer != "L0":
                            own_values(t + 1, 1 - p)
                        queries(t + 1, 1 - p)
                    for j in range(NJ):
                        if live(t):
                            scores_by_key(t, p, j)
                        if live(t + 1):
                            scores(t + 1, 1 - p, j)
                        if live(t) and j > 0:
                            values(t, p, j - 1)
                    if live(t):
                        values(t, p, NJ - 1)
                each_tile(pe, body)

            attention("L0")

            def l0c(t, p):
                u = t + 1
                if live(u):
                    wait(pe, "c_os", u + 1)
                    wait(pe, "c_oe", u - 1)
                    pe.transpose(bank[1 - p][:, 0:P], o_tok[:, 1 - p, :], ident[:, :]).then_inc(S("c_ot"), 1)
                if live(t):
                    wait(pe, "c_oe", t + 1)
                    wait(pe, "c_res", t - 1)
                    pe.matmul(bank[2 + p][:, 0:P], oT[:, p, :], l0_T[:, 3, :], start=True,
                              stop=True).then_inc(S("c_yp"), 1)
            each_tile(pe, l0c)

            def bit_ffn(layer, gated):
                for i in (0, 1, 2):
                    if i == 1 and not gated:
                        continue
                    n = {("F0", 0): 1, ("F0", 2): 2, ("F1", 0): 3, ("F1", 1): 4, ("F1", 2): 5}[layer, i]
                    pe.wait_ge(S("wq_ready"), n)
                    for c in range(NC):
                        m = pe.transpose(bank[i][:, :].bitcast(BF16)[:, c * P:(c + 1) * P],
                                         quant_bf[:, i, c * P:(c + 1) * P], ident_bf[:, :])
                    m.then_inc(S("wqT"), 1)
                pe.wait_ge(S("wqT_out"), 2 if not gated else 5)

                def body(t, p):
                    u = t + 1
                    if live(u):
                        wait(pe, layer + "_xn", u + 1)
                        wait(pe, layer + "_xe", u)
                        pe.transpose(bank[5][:, :].bitcast(BF16)[:, 0:P], xq_bf[:, 1 - p, :],
                                     ident_bf[:, :]).then_inc(S(layer + "_xt"), 1)
                        wait(pe, layer + "_xe", u + 1)
                        wait(pe, layer + "_hm" if gated else layer + "_ge", u - 1)
                        m = pe.matmul(bank[2 * (1 - p)][:, :], xqT_bf[:, 1 - p, :], ffn_wT[:, 0, :],
                                      start=True, stop=True)
                        if gated:
                            m = pe.matmul(bank[2 * (1 - p) + 1][:, :], xqT_bf[:, 1 - p, :], ffn_wT[:, 1, :],
                                          start=True, stop=True)
                        m.then_inc(S(layer + "_hp"), 1)
                    if live(t):
                        wait(pe, layer + "_hq", t + 1)
                        wait(pe, layer + "_he", t)
                        for c in range(NC):
                            m = pe.transpose(bank[4][:, :].bitcast(BF16)[:, c * P:(c + 1) * P],
                                             hid_bf[:, p, c * P:(c + 1) * P], ident_bf[:, :])
                        m.then_inc(S(layer + "_ht"), 1)
                    if live(t):
                        wait(pe, layer + "_he", t + 1)
                        wait(pe, layer + "_res", t - 1)
                        for c in range(NC):
                            m = pe.matmul(bank[6 + p][:, 0:P], hidT_bf[:, p, c * P:(c + 1) * P],
                                          ffn_wT[:, 2, c * P:(c + 1) * P], start=(c == 0), stop=(c == NC - 1))
                        m.then_inc(S(layer + "_yp"), 1)
                each_tile(pe, body)

            if "F0" in phases:
                pe.wait_ge(S("wsum"), 1)
                pe.matmul(bank[7][:, 0:3], mean_mat[:, :], quant_sum[:, 0:3], start=True,
                          stop=True).then_inc(S("wmean"), 1)
                bit_ffn("F0", False)
            if "L1" in phases:
                def l1(t, p):
                    u = t + 1
                    if live(u):
                        wait(pe, "L1_xn", u + 1)
                        wait(pe, "L1_xe", u)
                        pe.transpose(bank[0][:, 0:P], xn[:, 1 - p, :], ident[:, :]).then_inc(S("L1_xt"), 1)
                        wait(pe, "L1_xe", u + 1)
                        wait(pe, "L1_sm", u)
                        pe.matmul(bank[1][:, 0:P], xnT[:, 1 - p, :], tile_of(contextT, u), start=True,
                                  stop=True).then_inc(S("L1_sp"), 1)
                    if live(t):
                        wait(pe, "L1_te", t + 1)
                        wait(pe, "L1_res", t - 1)
                        pe.matmul(bank[3 + p][:, 0:P], oT[:, p, :], tile_of(context, t), start=True,
                                  stop=True).then_inc(S("L1_pv"), 1)
                    if live(u):
                        wait(pe, "L1_ex", u + 1)
                        wait(pe, "L1_te", u)
                        pe.transpose(bank[2][:, 0:P], hid2[:, 1 - p, 0:P], ident[:, :]).then_inc(S("L1_tp"), 1)
                each_tile(pe, l1)
            if "F1" in phases:
                pe.wait_ge(S("wsum"), 2)
                pe.matmul(bank[7][:, 0:3], mean_mat[:, :], quant_sum[:, 0:3], start=True,
                          stop=True).then_inc(S("wmean"), 1)
                bit_ffn("F1", True)
            if "L2" in phases:
                attention("L2")
            if "F2" in phases:
                def route(t, p):
                    if live(t):
                        wait(pe, "R_xn", t + 1)
                        wait(pe, "R_xe", t - 1)
                        pe.transpose(bank[p][:, 0:P], xn[:, p, :], ident[:, :]).then_inc(S("R_xt"), 1)
                        wait(pe, "R_xe", t + 1)
                        wait(pe, "R_lg", t - 1)
                        pe.matmul(bank[2 + p][:, 0:NE], xnT[:, p, :], switch_w[:, :], start=True,
                                  stop=True).then_inc(S("R_lp"), 1)
                each_tile(pe, route)

                def experts(g):
                    rhs = shared[:, bass.ds(g * (GT * P), GT * P)]
                    for k in range(NE + 1):
                        if k < NE:
                            for c in range(NC):
                                n = g * NE + k
                                wait(pe, "F2_ge", (n - 1) * NC + c + 1)
                                pe.matmul(bank[c][:, :], moe_w1[:, k, c * P:(c + 1) * P], rhs, start=True,
                                          stop=True).then_inc(S("F2_hp"), 1)
                        if k > 0:
                            e = k - 1
                            n = g * NE + e
                            wait(pe, "F2_ge", (n + 1) * NC)
                            for i in range(GT):
                                wait(pe, "F2_res", n * GT + i - 1)
                                for c in range(NC):
                                    m = pe.matmul(bank[4 + i % 2][:, 0:P],
                                                  hidT[:, e % 2, c * HID + i * P:c * HID + (i + 1) * P],
                                                  moe_w2[:, e, c, :], start=(c == 0), stop=(c == NC - 1))
                                m.then_inc(S("F2_yt"), 1)
                pe.wait_ge(S("R_xd"), NT)
                pe.wait_ge(S("w_exp"), 32)
                pe.wait_ge(S("R_lg"), NT)
                experts(0)
                with pe.Fori(1, NG, 1) as g:
                    experts(g)
                pe.wait_ge(S("F2_res"), NT * NE)

                def bias(t, p):
                    if live(t):
                        wait(pe, "B_gs", t + 1)
                        wait(pe, "B_ge", t)
                        pe.transpose(bank[6][0:NE, 0:P], small[:, p, 0:NE], ident[:, :]).then_inc(S("B_gt"), 1)
                        wait(pe, "B_ge", t + 1)
                        wait(pe, "B_res", t - 1)
                        pe.matmul(bank[2 + p][:, 0:P], gateT[:, p, :], moe_b2[:, :], start=True,
                                  stop=True).then_inc(S("B_yp"), 1)
                each_tile(pe, bias)
            if "L3" in phases:
                attention("L3")
            if "F3" in phases:
                pe.wait_ge(S("bf_used"), 2 * STAGES)
                for c in range(NC):
                    m = pe.transpose(bank[6][:, c * P:(c + 1) * P], bf_dn[:, STAGES % 2, c * P:(c + 1) * P],
                                     ident[:, :])
                m.then_inc(S("wT"), 1)
                pe.wait_ge(S("up_row"), 1)
                for c in range(NC):
                    m = pe.matmul(bank[5][:, c:c + 1], up_row[0:1, c * P:(c + 1) * P], ones[0:1, 0:1],
                                  start=True, stop=True)
                m.then_inc(S("wT"), 1)
                pe.wait_ge(S("f3_bias"), 1)

                def f3(t, p):
                    u = t + 1
                    if live(u):
                        wait(pe, "F3_xn", u + 1)
                        wait(pe, "F3_xe", u)
                        pe.transpose(bank[4][:, 0:P], xn[:, 1 - p, :], ident[:, :]).then_inc(S("F3_xt"), 1)
                        wait(pe, "F3_xe", u + 1)
                        wait(pe, "F3_ge", u - 1)
                        for c in range(NC):
                            m = pe.matmul(bank[1 - p][:, c * P:(c + 1) * P],
                                          bf_up[:, STAGES % 2, 0, c * P:(c + 1) * P], xnT[:, 1 - p, :],
                                          start=True, stop=True)
                        m.then_inc(S("F3_hp"), 1)
                    if live(t):
                        wait(pe, "F3_ge", t + 1)
                        wait(pe, "F3_res", t - 1)
                        for c in range(NC):
                            m = pe.matmul(bank[2 + p][:, 0:P], hid[:, p, c * P:(c + 1) * P], w_down[:, c, :],
                                          start=(c == 0), stop=(c == NC - 1))
                        m.then_inc(S("F3_yp"), 1)
                each_tile(pe, f3)

        @block.vector
        def _(dve):
            n_link = 0

            def link(ins):
                nonlocal n_link
                n_link += 1
                ins.then_inc(S("dve_link"), 1)
                dve.wait_ge(S("dve_link"), n_link)

            def count(ins, name, n=1):
                ins.then_inc(S(name), n)

            def tile_stats(u):
                dve.bn_stats(stats[:, bass.ds(u, 1), :].rearrange("p u s -> p (u s)"), tile_of(x, u)
                             ).then_inc(S("stats"), 1)

            def norm_stats(n, scale_by_keep=False):
                dve.wait_ge(S("stats"), NT * n)
                link(dve.tensor_tensor(var_a[:, :], stats[:, :, 2], stats[:, :, 5], ALU.add))
                link(dve.tensor_tensor(var_b[:, :], stats[:, :, 1], stats[:, :, 4], ALU.subtract))
                link(dve.scalar_tensor_tensor(out=var_b[:, :], in0=var_b[:, :], scalar=0.25, in1=var_b[:, :],
                                              op0=ALU.mult, op1=ALU.mult))
                link(dve.scalar_tensor_tensor(out=var_b[:, :], in0=var_a[:, :], scalar=1.0 / P, in1=var_b[:, :],
                                              op0=ALU.mult, op1=ALU.add))
                link(dve.tensor_scalar(var_b[:, :], var_b[:, :], EPS, None, ALU.add))
                dve.sem_inc(S("var"), 1)
                link(dve.tensor_tensor(mean[:, :], stats[:, :, 1], stats[:, :, 4], ALU.add))
                link(dve.tensor_scalar(mean[:, :], mean[:, :], 0.5, None, ALU.mult))
                dve.wait_ge(S("std"), n)
                link(dve.reciprocal(rstd[:, :], var_a[:, :]))
                if scale_by_keep:
                    link(dve.tensor_tensor(rstd[:, :], rstd[:, :], keep[:, :], ALU.mult))

            def normed(dst, u, name):
                dve.tensor_scalar(dst, tile_of(x, u), column(mean, u), column(rstd, u), ALU.subtract,
                                  ALU.mult).then_inc(S(name), 1)

            dve.wait_ge(S("pool_set"), 2)
            dve.memset(mean_mat[:, :], 1.0 / (P * HID)).then_inc(S("mean_mat"), 1)
            dve.wait_ge(S("wT"), 1)
            link(dve.tensor_copy(l0_T[:, :, :].rearrange("i n o -> i (n o)"), bank[7][:, :]))
            dve.wait_ge(S("wT"), 2)
            dve.tensor_copy(bf_dn[:, 0, :], bank[6][:, :]).then_inc(S("con_T"), 1)
            dve.wait_ge(S("keep_in"), 16)
            dve.tensor_copy(mask_f[:, :], mask_nat[:, :]).then_inc(S("mask_f"), 1)
            dve.wait_ge(S("wT"), 4)
            dve.tensor_copy(moe_b1[:, :], bank[5][:, 0:NE * NC]).then_inc(S("R_b1"), 1)
            link(dve.tensor_scalar(keep[:, :], bank[5][:, P:P + NT], 0.0, None, ALU.is_equal))
            dve.sem_inc(S("wT_out"), 1)
            dve.wait_ge(S("bias_in"), 64)
            dve.wait_ge(S("tgate"), 1)
            link(dve.tensor_scalar(bo_row[:, :], bo_row[:, :], tgate[:, 0:1], None, ALU.mult))

            def first(u):
                dve.bn_stats(stats[:, u, :], x[:, u * P:(u + 1) * P]).then_inc(S("stats"), 1)
            for u in range(NT):
                if u % 8 == 0:
                    dve.wait_ge(S("x_in"), 64)
                first(u)
            norm_stats(1)
            dve.wait_ge(S("ctx_in"), 64)

            def l0a(t, p):
                u = t
                if live(u):
                    wait(dve, "a_xt", u - 1)
                    dve.tensor_copy(ctx_one[:, p, :], tile_of(context, u)).then_inc(S("a_cc"), 1)
                    wait(dve, "a_cc", u + 1)
                    normed(xn[:, p, :], u, "a_xn")
                    wait(dve, "a_xt", u + 1)
                    wait(dve, "a_qp", u - 1)
                    wait(dve, "a_ctxT", u - 1)
                    dve.tensor_copy(oT[:, p, :], bank[4 + p][:, 0:P]).then_inc(S("a_cs"), 1)
                u = t - 1
                if live(u):
                    wait(dve, "a_qp", u + 1)
                    for stage, half, bias in ((stage_q, 0, bq_row), (stage_v, 1, bv_row)):
                        dve.tensor_tensor(stage[:, bass.ds(u, 1), :].rearrange("p u d -> p (u d)"),
                                          bank[2 + 1 - p][:, half * P:(half + 1) * P], bias[:, :],
                                          ALU.add).then_inc(S("a_qv"), 1)
            each_tile(dve, l0a)

            def attention(layer):
                wide = layer != "L2"
                gate = ATT[layer]["gate"]

                def body(t, p):
                    if live(t):
                        wait(dve, layer + "_mt", t + 1)
                        dve.tensor_tensor(qT[:, p, :, :].rearrange("c a q -> c (a q)"),
                                          qT[:, p, :, :].rearrange("c a q -> c (a q)"), bank[5][:, :],
                                          ALU.add).then_inc(S(layer + "_ma"), 1)
                    u = t + 1
                    if live(u):
                        wait(dve, layer + "_kp", u + 1)
                        wait(dve, layer + "_st", 4 * (u - 1))
                        if layer == "L0":
                            m = dve.tensor_tensor(kT[:, 1 - p, :, :],
                                                  bank[6][:, :].rearrange("c (a k) -> c a k", a=NA),
                                                  over_blocks(key_add_l0[:, :], NA), ALU.add)
                        elif wide:
                            m = dve.tensor_scalar(kT[:, 1 - p, :, :].rearrange("c a k -> c (a k)"), bank[6][:, :],
                                                  key_add[:, 0:1], None, ALU.add)
                        else:
                            m = dve.tensor_scalar(kT[:, 1 - p, 0, :], bank[6][:, 0:P], key_add[:, 0:1], None,
                                                  ALU.add)
                        m.then_inc(S(layer + "_ke"), 1)
                    u = t - 1
                    if live(u) and layer != "L0":
                        wait(dve, layer + "_yp", u + 1)
                        dve.scalar_tensor_tensor(out=tile_of(x, u), in0=bank[4][:, 384:512],
                                                 scalar=tgate[:, gate:gate + 1], in1=tile_of(x, u),
                                                 op0=ALU.mult, op1=ALU.add).then_inc(S(layer + "_res"), 1)
                    u = t + 2
                    if live(u) and layer != "L0":
                        wait(dve, layer + "_xt", u - 1)
                        normed(xn[:, p, :], u, layer + "_xn")
                    u = t + 1
                    if live(u):
                        wait(dve, layer + "_mt", u - 1)
                        if layer == "L3":
                            for j in range(NJ):
                                wait(dve, layer + "_sp", 4 * u + j + 1)
                                if j >= 1:
                                    wait(dve, layer + "_mk", 4 * u + j)
                                dve.tensor_tensor(masked[:, j % 2, :, :],
                                                  bank[j % 2][:, :].rearrange("q (a k) -> q a k", a=NA),
                                                  over_blocks(future_add[:, :], NA),
                                                  ALU.add).then_inc(S(layer + "_mk"), 1)
                                wait(dve, layer + "_mk", 4 * u + j + 1)
                                dve.tensor_reduce(nmax[:, 1 - p, :, j, DH], masked[:, j % 2, :, :], AX.X, ALU.max,
                                                  negate=True).then_inc(S(layer + "_mx"), 1)
                        else:
                            for j in range(NJ):
                                wait(dve, layer + "_sp", 4 * u + j + 1)
                                dve.tensor_reduce(nmax[:, 1 - p, :, j, DH],
                                                  bank[j % 2][:, :].rearrange("q (a k) -> q a k", a=NA), AX.X,
                                                  ALU.max, negate=True).then_inc(S(layer + "_mx"), 1)
                    u = t - 1
                    if live(u) and layer != "L0":
                        wait(dve, layer + "_res", u + 1)
                        tile_stats(u)
                    if layer == "L3" and live(t + 1):
                        wait(dve, "L3_pv", 4 * t)
                        dve.tensor_copy(hid[:, 1 - p, 0:P], tile_of(open_mask, t + 1)).then_inc(S("L3_om"), 1)
                    if live(t):
                        wait(dve, layer + "_pv", 4 * (t + 1))
                        o = bank[4][:, 0:NH * (DH + 1)].rearrange("q (h d) -> q h d", d=DH + 1)
                        dve.reciprocal(o_inv[:, p, :], o[:, :, DH]).then_inc(S(layer + "_oi"), 1)
                        wait(dve, layer + "_oi", t + 1)
                        if layer == "L0":
                            wait(dve, "L0_o_out", 16 * (t - 1))
                        else:
                            wait(dve, layer + "_ot", t - 1)
                        dve.tensor_tensor(o_tok[:, p, :].rearrange("q (h d) -> q h d", d=DH), o[:, :, 0:DH],
                                          o_inv[:, p, :].unsqueeze(2).broadcast_to([P, NH, DH]),
                                          ALU.mult).then_inc(S(layer + "_on"), 1)
                if layer != "L0":
                    each_tile(dve, body, lead=2)
                else:
                    each_tile(dve, body)

            attention("L0")

            def l0c(t, p):
                u = t + 1
                if live(u):
                    wait(dve, "L0_o_in", 16 * (u + 1))
                    wait(dve, "c_ot", u - 1)
                    dve.tensor_copy(o_tok[:, 1 - p, :], tile_of(shared, u)).then_inc(S("c_os"), 1)
                if live(t):
                    dve.tensor_tensor(tile_of(x, t), tile_of(x, t), bo_row[:, :], ALU.add).then_inc(S("c_b"), 1)
                    wait(dve, "c_b", t + 1)
                    wait(dve, "c_yp", t + 1)
                    dve.scalar_tensor_tensor(out=tile_of(x, t), in0=bank[2 + p][:, 0:P], scalar=tgate[:, 0:1],
                                             in1=tile_of(x, t), op0=ALU.mult, op1=ALU.add).then_inc(S("c_res"), 1)
                    wait(dve, "c_res", t + 1)
                    tile_stats(t)
            wait(dve, "L0_o_out", 16 * NT)
            each_tile(dve, l0c)

            def quantised_weights(which, n_sum):
                for i in which:
                    link(dve.tensor_reduce(quant_sum[:, i:i + 1], quant_src[:, i, :], AX.X, ALU.add,
                                           apply_absolute_value=True))
                dve.sem_inc(S("wsum"), 1)
                dve.wait_ge(S("wmean"), n_sum)
                link(dve.tensor_scalar(quant_scale[:, :], bank[7][:, 0:3], EPS, None, ALU.max))
                link(dve.reciprocal(quant_inv[:, :], quant_scale[:, :]))
                for i in which:
                    link(dve.tensor_scalar(quant_tmp[:, i, :], quant_src[:, i, :], quant_inv[:, i:i + 1], MAGIC,
                                           ALU.mult, ALU.add))
                    link(dve.tensor_scalar(quant_tmp[:, i, :], quant_tmp[:, i, :], MAGIC, 1.0, ALU.subtract,
                                           ALU.min))
                    dve.tensor_scalar(quant_bf[:, i, :], quant_tmp[:, i, :], -1.0, None,
                                      ALU.max).then_inc(S("wq_ready"), 1)

            def bit_ffn(layer, gated, gate):
                base = 0 if not gated else 2
                for k, i in enumerate((0, 1, 2) if gated else (0, 2)):
                    dve.wait_ge(S("wqT"), base + k + 1)
                    dve.tensor_copy(ffn_wT[:, i, :], bank[i][:, :].bitcast(BF16)[:, 0:HID]).then_inc(S("wqT_out"), 1)
                link(dve.tensor_scalar(ffn_sw[:, :], quant_scale[:, :], 1.0 / QMAX, None, ALU.mult))
                link(dve.tensor_scalar(ffn_sw[:, 2:3], ffn_sw[:, 2:3], tgate[:, gate:gate + 1], None, ALU.mult))

                LA, LB = layer + "_qa", layer + "_qb"

                def body(t, p):
                    u = t + 2
                    if live(u):
                        w = 5 * u
                        dve.tensor_scalar(xn[:, p, :], tile_of(x, u), column(mean, u), column(rstd, u),
                                          ALU.subtract, ALU.mult).then_inc(S(LA), 1)
                        wait(dve, LA, w + 1)
                        dve.tensor_reduce(small[:, p, 0:1], xn[:, p, :], AX.X, ALU.max,
                                          apply_absolute_value=True).then_inc(S(LA), 1)
                        wait(dve, LA, w + 2)
                        dve.tensor_scalar(small[:, p, 2:3], small[:, p, 0:1], EPS, None,
                                          ALU.max).then_inc(S(LA), 1)
                        wait(dve, LA, w + 3)
                        dve.reciprocal(small[:, p, 1:2], small[:, p, 2:3]).then_inc(S(LA), 1)
                        wait(dve, layer + ("_hm" if gated else "_ge"), u - 1)
                        dve.tensor_tensor(small[:, p, 3:5], ffn_sw[:, 0:2],
                                          small[:, p, 2:3].broadcast_to([P, 2]), ALU.mult)
                        wait(dve, LA, w + 4)
                        dve.tensor_scalar(small[:, p, 5:6], small[:, p, 1:2], QMAX, None,
                                          ALU.mult).then_inc(S(LA), 1)
                        wait(dve, LA, w + 5)
                        dve.tensor_scalar(xq_f[:, p, :], xn[:, p, :], small[:, p, 5:6], MAGIC, ALU.mult,
                                          ALU.add).then_inc(S(layer + "_qx"), 1)
                        wait(dve, layer + "_qx", u + 1)
                        wait(dve, layer + "_xt", u - 1)
                        dve.tensor_scalar(xq_bf[:, p, :], xq_f[:, p, :], MAGIC, QMAX, ALU.subtract,
                                          ALU.min).then_inc(S(layer + "_xn"), 1)
                    if live(t):
                        wait(dve, layer + "_yp", t + 1)
                        dve.scalar_tensor_tensor(out=tile_of(x, t), in0=bank[6 + p][:, 0:P],
                                                 scalar=small[:, p, 9:10], in1=tile_of(x, t), op0=ALU.mult,
                                                 op1=ALU.add).then_inc(S(layer + "_res"), 1)
                    u = t + 1
                    if live(u):
                        q = 1 - p
                        w = 4 * u
                        wait(dve, layer + "_ge", u + 1)
                        if gated:
                            src = hid2
                            dve.scalar_tensor_tensor(out=hid2[:, q, :], in0=bank[2 * q + 1][:, :],
                                                     scalar=small[:, q, 4:5], in1=hid[:, q, :], op0=ALU.mult,
                                                     op1=ALU.mult).then_inc(S(layer + "_hm"), 1)
                            wait(dve, layer + "_hm", u + 1)
                        else:
                            src = hid
                        dve.tensor_reduce(small[:, q, 6:7], src[:, q, :], AX.X, ALU.max,
                                          apply_absolute_value=True).then_inc(S(LB), 1)
                        wait(dve, LB, w + 1)
                        dve.tensor_scalar(small[:, q, 7:8], small[:, q, 6:7], EPS, None,
                                          ALU.max).then_inc(S(LB), 1)
                        wait(dve, LB, w + 2)
                        dve.reciprocal(small[:, q, 8:9], small[:, q, 7:8]).then_inc(S(LB), 1)
                        dve.tensor_tensor(small[:, q, 9:10], small[:, q, 7:8], ffn_sw[:, 2:3], ALU.mult)
                        wait(dve, LB, w + 3)
                        dve.tensor_scalar(small[:, q, 10:11], small[:, q, 8:9], QMAX, None,
                                          ALU.mult).then_inc(S(LB), 1)
                        wait(dve, LB, w + 4)
                        dve.tensor_scalar(src[:, q, :], src[:, q, :], small[:, q, 10:11], MAGIC, ALU.mult,
                                          ALU.add).then_inc(S(layer + "_qh"), 1)
                        wait(dve, layer + "_qh", u + 1)
                        wait(dve, layer + "_ht", u - 1)
                        dve.tensor_scalar(hid_bf[:, q, :], src[:, q, :], MAGIC, QMAX, ALU.subtract,
                                          ALU.min).then_inc(S(layer + "_hq"), 1)
                    if live(t):
                        wait(dve, layer + "_res", t + 1)
                        tile_stats(t)
                each_tile(dve, body, lead=2)

            if "F0" in phases:
                dve.wait_ge(S("w_f0"), 32)
                link(dve.memset(quant_sum[:, :], 0.0))
                quantised_weights((0, 2), 1)
                norm_stats(2)
                bit_ffn("F0", False, 4)
            if "L1" in phases:
                norm_stats(3)

                def l1(t, p):
                    u = t + 2
                    if live(u):
                        wait(dve, "L1_xt", u - 1)
                        normed(xn[:, p, :], u, "L1_xn")
                    u = t + 1
                    if live(u):
                        q = 1 - p
                        wait(dve, "L1_sp", u + 1)
                        wait(dve, "L1_ex", u - 1)
                        dve.scalar_tensor_tensor(out=hid[:, q, 0:P], in0=bank[1][:, 0:P], scalar=L1_SCALE,
                                                 in1=tile_of(add_mask, u), op0=ALU.mult,
                                                 op1=ALU.add).then_inc(S("L1_sm"), 1)
                        dve.wait_ge(S("L1_sm"), u + 1)
                        dve.tensor_reduce(small[:, q, 0:1], hid[:, q, 0:P], AX.X, ALU.max,
                                          negate=True).then_inc(S("L1_nm"), 1)
                    if live(t):
                        wait(dve, "L1_ex", t + 1)
                        dve.reciprocal(small[:, p, 2:3], small[:, p, 1:2]).then_inc(S("L1_r"), 1)
                        dve.wait_ge(S("L1_r"), 2 * t + 1)
                        dve.tensor_scalar(small[:, p, 3:4], small[:, p, 2:3], tgate[:, 1:2], None,
                                          ALU.mult).then_inc(S("L1_r"), 1)
                        dve.wait_ge(S("L1_r"), 2 * t + 2)
                        wait(dve, "L1_pv", t + 1)
                        dve.scalar_tensor_tensor(out=tile_of(x, t), in0=bank[3 + p][:, 0:P],
                                                 scalar=small[:, p, 3:4], in1=tile_of(x, t), op0=ALU.mult,
                                                 op1=ALU.add).then_inc(S("L1_res"), 1)
                        wait(dve, "L1_res", t + 1)
                        tile_stats(t)
                dve.wait_ge(S("mask_in"), 16)
                each_tile(dve, l1, lead=2)
            if "F1" in phases:
                dve.wait_ge(S("w_f1"), 48)
                quantised_weights((0, 1, 2), 2)
                norm_stats(4)
                bit_ffn("F1", True, 5)
            if "L2" in phases:
                norm_stats(5)
                attention("L2")
            if "F2" in phases:
                norm_stats(6)

                def route(t, p):
                    u = t + 1
                    if live(u):
                        wait(dve, "R_xt", u - 1)
                        normed(xn[:, 1 - p, :], u, "R_xn")
                    if live(t):
                        wait(dve, "R_xe", t + 1)
                        dve.tensor_copy(tile_of(shared, t), xnT[:, p, :]).then_inc(S("R_xd"), 1)
                        wait(dve, "R_lp", t + 1)
                        dve.tensor_tensor(logits[:, bass.ds(t, 1), :].rearrange("p u e -> p (u e)"),
                                          bank[2 + p][:, 0:NE], switch_b[:, :], ALU.add).then_inc(S("R_lg"), 1)
                each_tile(dve, route)
                dve.wait_ge(S("R_lg"), NT)

                def by_tile(i):
                    return route_m[:, i, :].unsqueeze(2).broadcast_to([P, NT, NE])

                def by_expert(ap):
                    return over_blocks(ap[:, :], NT)
                link(dve.tensor_reduce(route_m[:, 0, :], logits[:, :, :], AX.X, ALU.max))
                link(dve.tensor_tensor(route_b[:, :, :], logits[:, :, :], by_tile(0), ALU.subtract))
                dve.sem_inc(S("R_sub"), 1)
                dve.wait_ge(S("R_exp"), 1)
                link(dve.tensor_reduce(route_m[:, 1, :], route_a[:, :, :], AX.X, ALU.add))
                link(dve.reciprocal(route_m[:, 2, :], route_m[:, 1, :]))
                link(dve.tensor_scalar(route_a[:, :, :], route_b[:, :, :], 0.0, float(NE), ALU.is_lt, ALU.mult))
                link(dve.tensor_tensor(route_a[:, :, :], route_a[:, :, :], by_expert(expert_no), ALU.add))
                link(dve.tensor_reduce(route_m[:, 0, :], route_a[:, :, :], AX.X, ALU.min))
                link(dve.tensor_tensor(route_b[:, :, :], by_expert(expert_no), by_tile(0), ALU.is_equal))
                link(dve.tensor_tensor(gate_of[:, :, :], route_b[:, :, :], by_tile(2), ALU.mult))
                link(dve.tensor_scalar(gate_of[:, :, :], gate_of[:, :, :], tgate[:, 6:7], None, ALU.mult))

                def experts(g):
                    for e in range(NE):
                        for i in range(GT):
                            n = (g * NE + e) * GT + i
                            wait(dve, "F2_yt", n + 1)
                            if e > 0:
                                dve.wait_ge(S("F2_res"), n + 1 - GT)
                            xt = x[:, bass.ds(g * (GT * P) + i * P, P)]
                            dve.scalar_tensor_tensor(
                                out=xt, in0=bank[4 + i % 2][:, 0:P],
                                scalar=gate_of[:, :, e][:, bass.ds(g * GT + i, 1)],
                                in1=xt, op0=ALU.mult, op1=ALU.add).then_inc(S("F2_res"), 1)
                experts(0)
                with dve.Fori(1, NG, 1) as g:
                    experts(g)
                dve.wait_ge(S("F2_res"), NT * NE)

                def bias(t, p):
                    u = t + 1
                    if live(u):
                        wait(dve, "B_gt", u - 1)
                        dve.tensor_copy(small[:, 1 - p, 0:NE],
                                        gate_of[:, bass.ds(u, 1), :].rearrange("p u e -> p (u e)")
                                        ).then_inc(S("B_gs"), 1)
                    if live(t):
                        wait(dve, "B_gt", t + 1)
                        wait(dve, "B_yp", t - 1)
                        dve.tensor_copy(gateT[:, p, :], bank[6][0:NE, 0:P]).then_inc(S("B_ge"), 1)
                        wait(dve, "B_yp", t + 1)
                        dve.tensor_tensor(tile_of(x, t), tile_of(x, t), bank[2 + p][:, 0:P],
                                          ALU.add).then_inc(S("B_res"), 1)
                        wait(dve, "B_res", t + 1)
                        tile_stats(t)
                each_tile(dve, bias)
            if "L3" in phases:
                norm_stats(7, scale_by_keep=True)
                dve.wait_ge(S("open_in"), 16)
                dve.wait_ge(S("fut"), 5)
                dve.tensor_scalar(open_mask[:, :], open_mask[:, :].bitcast(I32), 0.0, None,
                                  ALU.not_equal).then_inc(S("open"), 1)
                dve.wait_ge(S("open"), 1)
                dve.tensor_tensor(open_mask[:, :].rearrange("k (t q) -> k t q", q=P),
                                  open_mask[:, :].rearrange("k (t q) -> k t q", q=P),
                                  over_blocks(future_one[:, :], NT), ALU.mult).then_inc(S("open"), 1)
                attention("L3")
            if "F3" in phases:
                norm_stats(8)
                dve.wait_ge(S("bf_used"), 2 * STAGES)
                link(dve.tensor_tensor(up_row[:, :], up_row[:, :], bf_up[0:1, STAGES % 2, 1, :], ALU.add))
                dve.sem_inc(S("up_row"), 1)
                dve.wait_ge(S("wT"), 6)
                link(dve.tensor_copy(w_down[:, :, :].rearrange("p c d -> p (c d)"), bank[6][:, :]))
                link(dve.tensor_copy(up_bias[:, :], bank[5][:, 0:NC]))
                dve.sem_inc(S("f3_bias"), 1)
                link(dve.tensor_tensor(con_bias[:, 0, :], con_bias[:, 0, :], con_bias[:, 1, :], ALU.add))
                link(dve.tensor_scalar(con_bias[:, 0, :], con_bias[:, 0, :], tgate[:, 7:8], None, ALU.mult))

                def f3(t, p):
                    u = t + 2
                    if live(u):
                        wait(dve, "F3_xt", u - 1)
                        normed(xn[:, p, :], u, "F3_xn")
                    if live(t):
                        dve.tensor_tensor(tile_of(x, t), tile_of(x, t), con_bias[:, 0, :],
                                          ALU.add).then_inc(S("F3_b"), 1)
                        wait(dve, "F3_b", t + 1)
                        wait(dve, "F3_yp", t + 1)
                        dve.scalar_tensor_tensor(out=tile_of(x, t), in0=bank[2 + p][:, 0:P],
                                                 scalar=tgate[:, 7:8], in1=tile_of(x, t), op0=ALU.mult,
                                                 op1=ALU.add).then_inc(S("F3_res"), 1)
                each_tile(dve, f3, lead=2)


def kernel(**inputs):
    import numpy as _np
    import concourse.bacc as _bacc
    from concourse import mybir as _mybir
    from concourse.bass_utils import run_bass_kernel_spmd as _run

    nc = _bacc.Bacc("TRN2", target_bir_lowering=False, num_devices=1)
    arrays, args = {}, {}
    for name, a in inputs.items():
        a = _np.ascontiguousarray(a)
        arrays[f"in_{name}_dram"] = a
        args[name] = nc.dram_tensor(f"in_{name}_dram", a.shape, _mybir.dt.from_np(a.dtype), kind="ExternalInput").ap()
    out = nc.dram_tensor("out_0_dram", (NT, P, P), F32, kind="ExternalOutput").ap()
    scratch = [nc.dram_tensor(f"{n}_scratch", (NT, NH, P, DH), F32).ap() for n in "qvo"]
    gated_layers(nc, args, out, *scratch)
    r = _run(nc, [arrays], core_ids=[0])
    return r.results[0]["out_0_dram"]
```

```python
from contextlib import ExitStack

import concourse.bass as bass
from concourse import mybir

ALU = mybir.AluOpType
ACT = mybir.ActivationFunctionType
AX = mybir.AxisListType
F32 = mybir.dt.float32
BF16 = mybir.dt.bfloat16
I32 = mybir.dt.int32

P = 128
NT = 32
NH, DH = 16, 8
NJ, NA = 4, 4
PG = P // NJ
HID = 512
NC = HID // P
NE = 8
NS = NT + NE
GC = 8
STAGES = 9
EPS = 1e-5
MAGIC = 1.5 * 2.0 ** 23
QMAX = 127.0
NEG = -1e9
SCORE_SCALE = DH ** -0.5
L1_SCALE = P ** -0.5
LOOP_FROM = 4

LAST_PHASE = "F3"
ORDER = ["L0", "F0", "L1", "F1", "L2", "F2", "L3", "F3"]


def gated_layers(nc, A, out, q_scratch, v_scratch, o_scratch, slot_in, slot_out):
    phases = ORDER[:ORDER.index(LAST_PHASE) + 1]
    ctx = ExitStack()
    with ctx:
        def sb(name, shape, dt=F32):
            return ctx.enter_context(nc.sbuf_tensor(name, shape, dt))

        def sem(name):
            return ctx.enter_context(nc.semaphore(name))

        bank = [ctx.enter_context(nc.psum_tensor(f"bank{i}", [P, 512], F32)) for i in range(8)]

        x = sb("x", [P, NT * P])
        context = sb("context", [P, NT * P])
        contextT = sb("contextT", [P, NT * P])
        shared = sb("shared", [P, NT * P])
        add_mask = open_mask = shared
        stats = sb("stats", [P, NT, 6])
        mean = sb("mean", [P, NT])
        rstd = sb("rstd", [P, NT])
        var_a = sb("var_a", [P, NT])
        var_b = sb("var_b", [P, NT])
        mean_mat = sb("mean_mat", [P, P])
        ident = sb("ident", [P, P])
        ident_bf = sb("ident_bf", [P, P], BF16)
        ones = sb("ones", [P, P])
        gates = sb("gates", [P, 8])
        tgate = sb("tgate", [P, 8])

        probs_space = sb("probs_space", [P, NJ * NA * P])
        probs = probs_space[:, :].rearrange("k (j a q) -> k j a q", j=NJ, a=NA)
        l0_nat = probs_space[:, 0:4 * P].rearrange("p (n d) -> p n d", d=P)
        con_nat = probs_space[:, 4 * P:8 * P].rearrange("p (n d) -> p n d", d=P)
        logits, route_a, route_b, route_c, route_d = (
            probs_space[:, i * NT * NE:(i + 1) * NT * NE].rearrange("p (t e) -> p t e", e=NE) for i in range(5))
        l0_T = sb("l0_T", [P, 4, P])
        bq_row = sb("bq_row", [P, P])
        bv_row = sb("bv_row", [P, P])
        bo_row = sb("bo_row", [P, P])
        key_add_l0 = sb("key_add_l0", [P, P])
        key_add = sb("key_add", [P, 1])
        late = sb("late", [P, 8 * HID])
        quant_src = late[:, 0:3 * HID].rearrange("p (i f) -> p i f", i=3)
        quant_tmp = late[:, 3 * HID:6 * HID].rearrange("p (i f) -> p i f", i=3)
        bf_t = late[:, 0:4 * HID].rearrange("p (i f) -> p i f", i=4)
        bf_w = late[:, 4 * HID:8 * HID].rearrange("p (i f) -> p i f", i=2)
        quant_bf = sb("quant_bf", [P, 3, HID], BF16)
        quant_sum = sb("quant_sum", [P, 3])
        quant_scale = sb("quant_scale", [P, 3])
        quant_inv = sb("quant_inv", [P, 3])
        ffn_wT = sb("ffn_wT", [P, 3, HID], BF16)
        ffn_sw = sb("ffn_sw", [P, 3])
        wq_pad = sb("wq_pad", [P, NA, NJ, PG])
        wk_pad = sb("wk_pad", [P, NA, NJ, PG])
        l2_wq = sb("l2_wq", [P, P])
        l2_wkv = sb("l2_wkv", [P, 2 * DH])
        l2_wo = sb("l2_wo", [P, P])
        l3_wq = sb("l3_wq", [P, P])
        l3_wk = sb("l3_wk", [P, P])
        l3_wv = sb("l3_wv", [P, P])
        l3_wo = sb("l3_wo", [P, P])
        future_add = sb("future_add", [P, P])
        future_one = sb("future_one", [P, P])
        mask_nat = sb("mask_nat", [NT, P], I32)
        mask_f = sb("mask_f", [NT, P])
        keep = sb("keep", [P, NT])
        switch_w = sb("switch_w", [P, NE])
        switch_b = sb("switch_b", [P, NE])
        moe_w1 = context[:, :]
        moe_b2_rows = sb("moe_b2_rows", [P, NE * P])
        moe_w2 = sb("moe_w2", [P, NE, NC, P])
        moe_b1 = sb("moe_b1", [P, NE * NC])
        moe_b1n = sb("moe_b1n", [NE * NC, P])
        con_bias = sb("con_bias", [P, 2, P])
        bf_up = sb("bf_up", [P, 2, 2, HID])
        bf_dn = sb("bf_dn", [P, 2, HID])
        up_bias = sb("up_bias", [P, NC])
        up_row = sb("up_row", [1, HID])
        w_down = sb("w_down", [P, NC, P])

        stage_q = shared[:, :].rearrange("p (b d) -> p b d", d=P)
        stage_v = moe_w2[:, :, :, :].rearrange("p e c d -> p (e c) d")

        xn = sb("xn", [P, 2, P])
        xnT = sb("xnT", [P, 2, P])
        hid_space = sb("hid_space", [P, 8 * HID // 2])
        ctx_pad = hid_space[:, 0:2 * HID].rearrange("p (b a j d) -> p b a j d", b=2, a=NA, j=NJ)
        q_rows = hid_space[:, 2 * HID:4 * HID].rearrange("p (b a j d) -> p b a j d", b=2, a=NA, j=NJ)
        hid = hid_space[:, 0:2 * HID].rearrange("p (b f) -> p b f", b=2)
        hid2 = hid_space[:, 2 * HID:4 * HID].rearrange("p (b f) -> p b f", b=2)
        ctx_one = sb("ctx_one", [P, 2, P])
        qT = sb("qT", [P, 2, NA, P])
        keys_alone = moe_w2[:, :, :, :].rearrange("p (b a) c d -> p b a c d", b=2)
        VW = P + NH
        vals = sb("vals", [P, 2, (NH + 1) * VW])
        nmax = sb("nmax", [P, 2, NA, NJ, PG])
        masked = hid2.rearrange("p b (a k) -> p b a k", a=NA)
        o_inv = sb("o_inv", [P, 2, NH])
        o_tok = sb("o_tok", [P, 2, P])
        oT = sb("oT", [P, 2, P])
        hid_bf = sb("hid_bf", [P, 2, HID], BF16)
        hidT_bf = sb("hidT_bf", [P, 2, HID], BF16)
        xq_f = sb("xq_f", [P, 2, P])
        xq_bf = sb("xq_bf", [P, 2, P], BF16)
        xqT_bf = sb("xqT_bf", [P, 2, P], BF16)
        small = sb("small", [P, 2, 16])
        route_m = sb("route_m", [P, 3, NT])
        expert_no = sb("expert_no", [P, NE])
        gate = sb("gate", [P, NT])
        earlier = sb("earlier", [P, P])
        zeros = sb("zeros", [P, P])
        expert_of = sb("expert_of", [P, NS])
        expert_int = sb("expert_int", [1, NS], I32)
        slot_no = sb("slot_no", [P, NS])
        dest_int = sb("dest_int", [P, NT], I32)
        fill = sb("fill", [P, 4, NE])

        s = {}
        FOUR_A_TILE = {"st", "sp", "ex", "mx", "mk", "pv", "qb"}
        OF_L0_TOO = {"qp", "kp", "ke", "qe", "st", "ex", "mx", "ma", "mt", "sp", "pv", "oi", "on", "cs"}

        def shared_name(name):
            phase, _, signal = name.partition("_")
            a_tile = 5 if signal == "qa" else 4 if signal in FOUR_A_TILE else 1
            if phase in ("L0", "L2", "L3") and (phase != "L0" or signal in OF_L0_TOO):
                before = {"L0": 0, "L2": 1, "L3": 2}[phase] - (signal not in OF_L0_TOO)
                if signal in ("mk", "om", "causal"):
                    before = 0
                return "att_" + signal, before * a_tile * NT
            if phase in ("F0", "F1"):
                return "bit_" + signal, (phase == "F1" and signal != "hm") * a_tile * NT
            return name, 0

        def S(name):
            name = shared_name(name)[0]
            if name not in s:
                s[name] = sem(name)
            return s[name]

        def wait(eng, name, value):
            if not isinstance(value, int) or value > 0:
                eng.wait_ge(S(name), value + shared_name(name)[1])
                if not isinstance(value, int) and eng.engine in (nc.sync.engine, nc.gpsimd.engine):
                    eng.sem_inc(S("sp_passed" if eng.engine == nc.sync.engine else "pool_passed"), 1)

        def live(u, n=NT):
            return not isinstance(u, int) or 0 <= u < n

        def each_tile(eng, body, lead=1, tail=1, n=NT):
            for t in range(-lead, LOOP_FROM):
                body(t, t % 2)
            with eng.Fori(LOOP_FROM, n - 3, 2) as i:
                body(i, 0)
                body(i + 1, 1)
            for t in range(n - 2, n + tail):
                body(t, t % 2)

        def values_of(p, h=None):
            if h is None:
                return vals[:, p, 0:NH * (VW + DH)].rearrange("k (h c) -> k h c", h=NH)[:, :, 0:DH]
            return vals[:, p, h * VW:(h + 1) * VW]

        def tile_of(buf, t):
            return buf[:, bass.ds(t * P, P)]

        def column(buf, t):
            return buf[:, bass.ds(t, 1)]

        def over_blocks(ap, n):
            return ap.unsqueeze(1).broadcast_to([ap.shape[0], n, ap.shape[1]])

        ATT = {
            "L0": dict(gate=0), "L2": dict(gate=2), "L3": dict(gate=3),
        }

        def pad_weights(pool, layer):
            pool.wait_ge(S("w_att"), 16 * 7)
            if layer == "L2":
                pool.memset(wq_pad[:, :, :, :], 0.0).then_inc(S("pad"), 1)
                pool.memset(wk_pad[:, :, :, :], 0.0).then_inc(S("pad"), 1)
                pool.wait_ge(S("pad"), 2)
                pool.tensor_copy(wq_pad[:, :, :, 0:DH].rearrange("i a j d -> i (a j) d"),
                                 l2_wq[:, :].rearrange("i (h d) -> i h d", d=DH)).then_inc(S("pad"), 1)
                pool.tensor_copy(wk_pad[:, 0, :, 0:DH], over_blocks(l2_wkv[:, 0:DH], NJ)).then_inc(S("pad"), 1)
            else:
                wait(pool, "L2_qp", NT)
                wait(pool, "L2_kp", NT)
                pool.tensor_copy(wq_pad[:, :, :, 0:DH].rearrange("i a j d -> i (a j) d"),
                                 l3_wq[:, :].rearrange("i (h d) -> i h d", d=DH)).then_inc(S("pad"), 1)
                pool.tensor_copy(wk_pad[:, :, :, 0:DH].rearrange("i a j d -> i (a j) d"),
                                 l3_wk[:, :].rearrange("i (h d) -> i h d", d=DH)).then_inc(S("pad"), 1)

        block = ctx.enter_context(nc.Block())

        @block.sync
        def _(sp):
            tok = "b s d -> s b d"
            for c in range(4):
                b = slice(8 * c, 8 * c + 8)
                sp.dma_start(x[:, 1024 * c:1024 * c + 1024].rearrange("p (b d) -> p b d", d=P),
                             A["x"][b].rearrange(tok)).then_inc(S("x_in"), 16)
                if c == 0:
                    sp.dma_start(l0_nat[:, 0, :], A["L0_xattn_wq"]).then_inc(S("w_l0"), 16)
                    sp.dma_start(l0_nat[:, 1, :], A["L0_xattn_wk"]).then_inc(S("w_l0"), 16)
                    sp.dma_start(l0_nat[:, 2, :], A["L0_xattn_wv"]).then_inc(S("w_l0"), 16)
                    sp.dma_start(l0_nat[:, 3, :], A["L0_xattn_wo"]).then_inc(S("w_l0"), 16)
            for c in range(4):
                b = slice(8 * c, 8 * c + 8)
                sp.dma_start(context[:, 1024 * c:1024 * c + 1024].rearrange("p (b d) -> p b d", d=P),
                             A["ctx_1024"][b].rearrange(tok)).then_inc(S("ctx_in"), 16)

            def l0b(t, p):
                u = t + 2
                if live(u):
                    wait(sp, "L0_q_in", 16 * u)
                    wait(sp, "L0_qp", u - 1)
                    sp.dma_start(q_rows[:, p, :, :, 0:DH].rearrange("i a j d -> i (a j) d"),
                                 q_scratch[bass.ds(u, 1)].rearrange("u h i d -> i (u h) d")).then_inc(S("L0_q_in"), 16)
                    wait(sp, "L0_v_in", 16 * u)
                    wait(sp, "L0_pv", 4 * (u - 1))
                    sp.dma_start(values_of(p),
                                 v_scratch[bass.ds(u, 1)].rearrange("u h i d -> i (u h) d")).then_inc(S("L0_v_in"), 16)
                u = t - 1
                if live(u):
                    wait(sp, "L0_o_out", 16 * u)
                    wait(sp, "L0_on", u + 1)
                    sp.dma_start(o_scratch[bass.ds(u, 1)].rearrange("u h i d -> i (u h) d"),
                                 o_tok[:, 1 - p, :].rearrange("i (h d) -> i h d", d=DH)).then_inc(S("L0_o_out"), 16)
                u = t - 2
                if live(u):
                    wait(sp, "L0_o_out", 16 * (u + 1))
                    wait(sp, "L0_o_in", 16 * u)
                    sp.dma_start(tile_of(shared, u),
                                 o_scratch[bass.ds(u, 1)].rearrange("u h (r c) d -> (u h r) (c d)", r=8)
                                 ).then_inc(S("L0_o_in"), 16)

            for c in range(4):
                sp.wait_ge(S("a_qv"), 2 * 8 * (c + 1))
                for scratch, stage in ((q_scratch, stage_q), (v_scratch, stage_v)):
                    sp.dma_start(scratch[8 * c:8 * c + 8].rearrange("u h (r c) d -> (h r) u (c d)", r=8),
                                 stage[:, 8 * c:8 * c + 8, :]).then_inc(S("l0a_stored"), 16)
            sp.wait_ge(S("l0a_stored"), 16 * 8)
            sp.wait_ge(S("pool_set"), 13)
            each_tile(sp, l0b, lead=2, tail=2)

            sp.wait_ge(S("c_os"), NT)
            sp.dma_start(add_mask[:, :].rearrange("p (b d) -> p b d", d=P),
                         A["mask_BxSxS2_ff0"].rearrange(tok)).then_inc(S("mask_in"), 16)
            sp.wait_ge(S("zero_set"), 1)
            sp.dma_start(slot_in.rearrange("(s p) d -> p s d", p=P), over_blocks(zeros[:, :], NS)
                         ).then_inc(S("zeroed"), 16)
            if "F1" in phases:
                sp.wait_ge(S("wq_ready"), 2)
                for i, name in enumerate(("L1_ffn_w_gate", "L1_ffn_w_up")):
                    sp.dma_start(quant_src[:, i, :].rearrange("p (c d) -> p c d", d=P),
                                 A[name].rearrange("(c p) d -> p c d", p=P)).then_inc(S("w_f1"), 16)
                sp.dma_start(quant_src[:, 2, :], A["L1_ffn_w_down"]).then_inc(S("w_f1"), 16)
            if "L2" in phases:
                sp.wait_ge(S("L1_pv"), NT)
                sp.dma_start(moe_w1.rearrange("d (e f) -> d e f", e=NE), A["L2_ffn_w1"].rearrange("e d f -> d e f")
                             ).then_inc(S("w_exp"), 16)
            if "F3" in phases:
                for n in range(2 * STAGES):
                    src = A["L3_ffn_up_weights"][n] if n < STAGES else A["L3_ffn_down_weights"][2 * STAGES - 1 - n]
                    if n >= 2:
                        wait(sp, "bf_used", n - 1)
                    else:
                        sp.wait_ge(S("wq_ready"), 5)
                    wait(sp, "bf_in", 16 * n)
                    sp.dma_start(bf_w[:, n % 2, :],
                                 src.rearrange("k i j -> (k i j)").unsqueeze(0).broadcast_to([P, 1024])
                                 ).then_inc(S("bf_in"), 16)

            if "F2" in phases:
                wait(sp, "L2_st", 4 * NT)
                sp.dma_start(moe_w2[:, :, :, :].rearrange("p e c d -> p (e c) d"),
                             A["L2_ffn_w2"].rearrange("e (c p) d -> p (e c) d", p=P)).then_inc(S("w_exp"), 16)
                sp.wait_ge(S("scattered"), 16 * NT)

                def slots(t, p):
                    u = t + 2
                    if live(u, NS):
                        wait(sp, "G_in", 16 * u)
                        wait(sp, "G_xt", u - 1)
                        sp.dma_start(xn[:, p, :], slot_in[bass.ds(u * P, P), :]).then_inc(S("G_in"), 16)
                    u = t - 1
                    if live(u, NS):
                        wait(sp, "G_out", 16 * u)
                        wait(sp, "G_yo", u + 1)
                        sp.dma_start(slot_out[bass.ds(u * P, P), :], o_tok[:, 1 - p, :]).then_inc(S("G_out"), 16)
                each_tile(sp, slots, lead=2, n=NS)
            if "L3" in phases:
                sp.wait_ge(S("B_res"), NT)
                sp.dma_start(open_mask[:, :].bitcast(I32),
                             A["mask_BxS2_ik0"].rearrange("b s -> (b s)").unsqueeze(0).broadcast_to([P, NT * P])
                             ).then_inc(S("open_in"), 16)
            done = {"L0": "c_res", "F0": "F0_res", "L1": "L1_res", "F1": "F1_res", "L2": "L2_res",
                    "F2": "B_res", "L3": "L3_res", "F3": "F3_res"}[LAST_PHASE]

            def store(t, p):
                u = t - 1
                if live(u):
                    wait(sp, done, u + 1)
                    sp.dma_start(out[bass.ds(u, 1)].rearrange("u s d -> (u s) d"),
                                 tile_of(x, u)).then_inc(S("stored"), 16)
            each_tile(sp, store)
            sp.wait_ge(S("stored"), 16 * NT)
            wait(sp, "L0_o_in", 16 * NT)

        @block.gpsimd
        def _(pool):
            n_set = 0

            def const(ins):
                nonlocal n_set
                n_set += 1
                ins.then_inc(S("pool_set"), 1)

            def settle():
                pool.wait_ge(S("pool_set"), n_set)

            const(pool.memset(ident[:, :], 0.0))
            const(pool.memset(ones[:, :], 1.0))
            settle()
            const(pool.affine_select(out=ident[:, :], in_=ident[:, :], compare_op=ALU.not_equal, fill=1.0,
                                     base=0, pattern=[[-1, P]], channel_multiplier=1))
            settle()
            const(pool.tensor_copy(ident_bf[:, :], ident[:, :]))
            settle()
            const(pool.memset(key_add[:, :], 0.0))
            const(pool.memset(ctx_pad[:, :, :, :, :], 0.0))
            const(pool.memset(q_rows[:, :, :, :, :], 0.0))
            const(pool.memset(nmax[:, :, :, :, :], 0.0))
            const(pool.memset(vals[:, :, :], 0.0))
            settle()
            for b in range(2):
                const(pool.memset(vals[:, b, P:P + NH * (VW + 1):VW + 1], 1.0))
                const(pool.memset(vals[:, b, NH * VW + P:(NH + 1) * VW], 1.0))
            settle()
            for j in range(NJ):
                const(pool.affine_select(out=key_add[:, :], in_=key_add[:, :], compare_op=ALU.not_equal,
                                         fill=1.0, base=-(PG * j + DH), pattern=[[0, 1]], channel_multiplier=1))
                settle()
            pool.wait_ge(S("bias_in"), 16 * 4)
            const(pool.affine_select(out=key_add_l0[:, :].rearrange("p n -> p n"), in_=key_add_l0[:, :],
                                     compare_op=ALU.not_equal, fill=1.0, base=-DH, pattern=[[0, P]],
                                     channel_multiplier=1))
            settle()
            for j in range(1, NJ):
                const(pool.affine_select(out=key_add_l0[:, :], in_=key_add_l0[:, :],
                                         compare_op=ALU.not_equal, fill=1.0, base=-(PG * j + DH),
                                         pattern=[[0, P]], channel_multiplier=1))
                settle()
            pool.memset(future_add[:, :], 0.0).then_inc(S("fut"), 1)
            pool.memset(future_one[:, :], 0.0).then_inc(S("fut"), 1)
            pool.wait_ge(S("fut"), 2)
            pool.affine_select(out=future_add[:, :], in_=future_add[:, :], compare_op=ALU.is_ge, fill=NEG,
                               base=0, pattern=[[-1, P]], channel_multiplier=1).then_inc(S("fut"), 1)
            pool.affine_select(out=future_one[:, :], in_=future_one[:, :], compare_op=ALU.is_ge, fill=1.0,
                               base=0, pattern=[[1, P]], channel_multiplier=-1).then_inc(S("fut"), 1)
            pool.memset(zeros[:, :], 0.0).then_inc(S("zero_set"), 1)
            pool.iota(slot_no[:, :], [[1, NS]], base=0, channel_multiplier=0,
                      allow_small_or_imprecise_dtypes=True).then_inc(S("fut"), 1)
            pool.affine_select(out=earlier[:, :], in_=ones[:, :], compare_op=ALU.is_gt, fill=0.0,
                               base=0, pattern=[[1, P]], channel_multiplier=-1).then_inc(S("fut"), 1)
            pool.iota(expert_no[:, :], [[1, NE]], base=0, channel_multiplier=0,
                      allow_small_or_imprecise_dtypes=True).then_inc(S("fut"), 1)

            def ctx_copy(layer, padded):
                def body(t, p):
                    u = t + 1
                    if live(u):
                        if padded:
                            wait(pool, layer + "_kp", u - 1)
                            pool.tensor_copy(ctx_pad[:, 1 - p, :, :, 0:DH].rearrange("i a j d -> i (a j) d"),
                                             tile_of(contextT, u).rearrange("i (h d) -> i h d", d=DH)
                                             ).then_inc(S(layer + "_cs"), 1)
                        else:
                            wait(pool, layer + "_vp", u - 1)
                            pool.tensor_copy(ctx_one[:, 1 - p, :], tile_of(contextT, u)
                                             ).then_inc(S(layer + "_cs"), 1)
                    if layer == "L3" and live(t):
                        for j in range(NJ):
                            wait(pool, "L3_ex", 4 * t + j + 1)
                            pool.affine_select(out=probs[:, j, :, :], in_=probs[:, j, :, :],
                                               compare_op=ALU.is_ge, fill=0.0, base=0,
                                               pattern=[[0, NA], [1, P]],
                                               channel_multiplier=-1).then_inc(S("L3_causal"), 1)
                each_tile(pool, body)


            def keep_ctxT(t, p):
                if live(t):
                    wait(pool, "a_cs", t + 1)
                    pool.tensor_copy(tile_of(contextT, t), oT[:, p, :]).then_inc(S("a_ctxT"), 1)
            each_tile(pool, keep_ctxT)
            ctx_copy("L0", True)
            if "L2" in phases:
                pad_weights(pool, "L2")

            if "L2" in phases:
                ctx_copy("L2", False)
            if "F3" in phases:
                pool.wait_ge(S("w_f3"), 16 * 2)
                pool.wait_ge(S("con_T"), 1)
                pool.wait_ge(S("wq_ready"), 5)
                step = 0
                for n in range(2 * STAGES):
                    up = n < STAGES
                    k = n if up else 2 * STAGES - 1 - n
                    w_n = 2 ** k
                    src, dst = n % 2, (n + 1) % 2
                    pool.wait_ge(S("bf_in"), 16 * (n + 1))
                    wv = bf_w[:, n % 2, :].rearrange("p (n s c) -> p c n s", s=w_n, c=4)
                    if up:
                        m = 2

                        def half(buf, i):
                            return buf.rearrange("p m (n two s) -> p two m n s", two=2, s=w_n)[:, i]

                        def tmp(i):
                            return bf_t[:, i, :].rearrange("p (m n s) -> p m n s", m=m, s=w_n)

                        def wgt(c):
                            return wv[:, c].unsqueeze(1).broadcast_to([P, m, HID // 2 // w_n, w_n])
                        a_in, b_in = half(bf_up[:, src], 0), half(bf_up[:, src], 1)
                        a_out, b_out = half(bf_up[:, dst], 0), half(bf_up[:, dst], 1)
                        order = (0, 1, 2, 3)
                    else:
                        src, dst = (n - STAGES) % 2, (n - STAGES + 1) % 2

                        def half(buf, i):
                            return buf.rearrange("p (n two s) -> p two n s", two=2, s=w_n)[:, i]

                        def tmp(i):
                            return bf_t[:, i, 0:HID // 2].rearrange("p (n s) -> p n s", s=w_n)

                        def wgt(c):
                            return wv[:, c]
                        a_in, b_in = half(bf_dn[:, src], 0), half(bf_dn[:, src], 1)
                        a_out, b_out = half(bf_dn[:, dst], 0), half(bf_dn[:, dst], 1)
                        order = (0, 2, 1, 3)
                    for i, (c, d) in enumerate(zip(order, (a_in, b_in, a_in, b_in))):
                        last = pool.tensor_tensor(tmp(i), d, wgt(c), ALU.mult)
                        last.then_inc(S("bf_step"), 1)
                    step += 4
                    pool.wait_ge(S("bf_step"), step)
                    pool.tensor_tensor(a_out, tmp(0), tmp(1), ALU.add).then_inc(S("bf_step"), 1)
                    pool.tensor_tensor(b_out, tmp(2), tmp(3), ALU.add).then_inc(S("bf_step"), 1)
                    step += 2
                    pool.wait_ge(S("bf_step"), step)
                    pool.sem_inc(S("bf_used"), 1)
            if "F2" in phases:
                pool.wait_ge(S("zeroed"), 16)
                pool.wait_ge(S("R_dest"), 1)
                for t in range(NT):
                    pool.indirect_dma_start(
                        out=slot_in, out_offset=bass.IndirectOffsetOnAxis(ap=dest_int[:, t:t + 1], axis=0),
                        in_=shared[:, t * P:(t + 1) * P], in_offset=None).then_inc(S("scattered"), 16)
                pool.wait_ge(S("scattered"), 16 * NT)
                pool.wait_ge(S("G_out"), 16 * NS)
                for t in range(NT):
                    pool.indirect_dma_start(
                        out=shared[:, t * P:(t + 1) * P], out_offset=None, in_=slot_out,
                        in_offset=bass.IndirectOffsetOnAxis(ap=dest_int[:, t:t + 1], axis=0)
                    ).then_inc(S(f"gathered_{t // GC}"), 16)
            if "L3" in phases:
                pad_weights(pool, "L3")
                ctx_copy("L3", False)

        @block.scalar
        def _(act):
            def row(name):
                return A[name].unsqueeze(0).broadcast_to([P, A[name].shape[0]])
            act.dma_start(gates[:, 0:4], row("g_xattn")).then_inc(S("gates_in"), 16)
            act.dma_start(gates[:, 4:8], row("g_ffn")).then_inc(S("gates_in"), 16)
            act.dma_start(bq_row[:, :], row("L0_xattn_bq")).then_inc(S("bias_in"), 16)
            act.dma_start(bv_row[:, :], row("L0_xattn_bv")).then_inc(S("bias_in"), 16)
            act.dma_start(bo_row[:, :], row("L0_xattn_bo")).then_inc(S("bias_in"), 16)
            act.dma_start(key_add_l0[:, :], row("L0_xattn_bk")).then_inc(S("bias_in"), 16)
            act.dma_start(quant_src[:, 0, :].rearrange("p (c d) -> p c d", d=P),
                          A["L0_ffn_w1"].rearrange("(c p) d -> p c d", p=P)).then_inc(S("w_f0"), 16)
            act.dma_start(quant_src[:, 2, :], A["L0_ffn_w2"]).then_inc(S("w_f0"), 16)
            act.dma_start(l2_wq[:, :], A["L2_xattn_w_q"]).then_inc(S("w_att"), 16)
            act.dma_start(l2_wkv[:, :], A["L2_xattn_w_kv"]).then_inc(S("w_att"), 16)
            act.dma_start(l2_wo[:, :], A["L2_xattn_w_concat"]).then_inc(S("w_att"), 16)
            act.dma_start(l3_wq[:, :], A["L3_xattn_WQ"]).then_inc(S("w_att"), 16)
            act.dma_start(l3_wk[:, :], A["L3_xattn_WK"]).then_inc(S("w_att"), 16)
            act.dma_start(l3_wv[:, :], A["L3_xattn_WV"]).then_inc(S("w_att"), 16)
            act.dma_start(l3_wo[:, :], A["L3_xattn_WO"]).then_inc(S("w_att"), 16)
            act.dma_start(switch_w[:, :], A["L2_ffn_switch_w"]).then_inc(S("w_moe"), 16)
            act.dma_start(switch_b[:, :], row("L2_ffn_switch_b")).then_inc(S("w_moe"), 16)
            act.dma_start(moe_b1n[:, :], A["L2_ffn_b1"].rearrange("e (c p) -> (e c) p", p=P)).then_inc(S("w_moe"), 16)
            act.dma_start(moe_b2_rows[:, :], A["L2_ffn_b2"].rearrange("e d -> (e d)").unsqueeze(0).broadcast_to([P, NE * P])
                          ).then_inc(S("w_moe"), 16)
            act.dma_start(con_nat[:, :, :], A["L3_ffn_W_con"].rearrange("(c p) d -> p c d", p=P)).then_inc(S("w_con"), 16)
            act.dma_start(con_bias[:, 0, :], row("L3_ffn_b_con")).then_inc(S("w_con"), 16)
            act.dma_start(con_bias[:, 1, :], row("L3_ffn_down_bias")).then_inc(S("w_con"), 16)
            act.dma_start(up_row[:, :], A["L3_ffn_up_bias"].unsqueeze(0)).then_inc(S("w_con"), 16)
            act.dma_start(bf_up[:, 0, 0, :], A["L3_ffn_W_exp"]).then_inc(S("w_f3"), 16)
            act.dma_start(bf_up[:, 0, 1, :], row("L3_ffn_b_exp")).then_inc(S("w_f3"), 16)
            act.dma_start(mask_nat[:, :], A["mask_BxS2_ik0"]).then_inc(S("keep_in"), 16)

            act.wait_ge(S("gates_in"), 32)
            act.activation(tgate[:, :], gates[:, :], ACT.Tanh).then_inc(S("tgate"), 1)

            def root(n):
                act.wait_ge(S("var"), n)
                act.activation(var_a[:, :], var_b[:, :], ACT.Sqrt).then_inc(S("std"), 1)

            root(1)

            def l0a(t, p):
                u = t
                if live(u):
                    wait(act, "a_xt", u + 1)
                    wait(act, "a_qp", u - 1)
                    act.activation(xnT[:, p, :], bank[p][:, 0:P], ACT.Copy).then_inc(S("a_xe"), 1)
            each_tile(act, l0a)

            def attention(layer):
                wide = layer != "L2"

                def body(t, p):
                    u = t - 1
                    if live(u) and layer != "L0":
                        wait(act, layer + "_ot", u + 1)
                        wait(act, layer + "_yp", u - 1)
                        act.activation(oT[:, 1 - p, :], bank[4][:, 256:384], ACT.Copy).then_inc(S(layer + "_oe"), 1)
                    u = t + 1
                    if live(u):
                        if layer != "L0":
                            wait(act, layer + "_xt", u + 1)
                            wait(act, layer + "_qp", u - 1)
                            act.activation(xnT[:, 1 - p, :], bank[7][:, 0:P], ACT.Copy).then_inc(S(layer + "_xe"), 1)
                            wait(act, layer + "_vp", u + 1)
                            wait(act, layer + "_pv", 4 * (u - 1))
                            if wide:
                                act.activation(values_of(1 - p, NH)[:, 0:P], bank[7][:, P:2 * P], ACT.Copy)
                                act.activation(values_of(1 - p),
                                               bank[7][:, P:2 * P].rearrange("k (h d) -> k h d", d=DH),
                                               ACT.Copy).then_inc(S(layer + "_ve"), 1)
                            else:
                                act.activation(values_of(1 - p), over_blocks(bank[7][:, P:P + DH], NH),
                                               ACT.Copy).then_inc(S(layer + "_ve"), 1)
                        wait(act, layer + "_qp", u + 1)
                        wait(act, layer + "_st", 4 * (u - 1))
                        act.activation(qT[:, 1 - p, :, :].rearrange("c a q -> c (a q)"), bank[5][:, :], ACT.Copy,
                                       scale=SCORE_SCALE).then_inc(S(layer + "_qe"), 1)
                    if live(t):
                        for j in range(NJ):
                            wait(act, layer + "_st", 4 * t + j + 1)
                            wait(act, layer + "_pv", 4 * (t - 1) + j + 1)
                            act.activation(probs[:, j, :, :].rearrange("k a q -> k (a q)"), bank[2 + j % 2][:, :],
                                           ACT.Exp).then_inc(S(layer + "_ex"), 1)
                each_tile(act, body)

            attention("L0")

            def l0c(t, p):
                if live(t):
                    wait(act, "c_ot", t + 1)
                    wait(act, "c_yp", t - 1)
                    act.activation(oT[:, p, :], bank[p][:, 0:P], ACT.Copy).then_inc(S("c_oe"), 1)
            each_tile(act, l0c)

            def bit_ffn(layer, gated):
                def body(t, p):
                    u = t + 1
                    if live(u):
                        wait(act, layer + "_xt", u + 1)
                        wait(act, layer + "_hp", u - 1)
                        act.activation(xqT_bf[:, 1 - p, :], bank[5][:, :].bitcast(BF16)[:, 0:P],
                                       ACT.Copy).then_inc(S(layer + "_xe"), 1)
                        wait(act, layer + "_hp", u + 1)
                        wait(act, layer + "_hq", u - 1)
                        act.activation(hid[:, 1 - p, :], bank[2 * (1 - p)][:, :], ACT.Silu if gated else ACT.Gelu,
                                       scale=small[:, 1 - p, 3:4]).then_inc(S(layer + "_ge"), 1)
                    if live(t):
                        wait(act, layer + "_ht", t + 1)
                        wait(act, layer + "_yp", t - 1)
                        act.activation(hidT_bf[:, p, :], bank[4][:, :].bitcast(BF16)[:, 0:HID],
                                       ACT.Copy).then_inc(S(layer + "_he"), 1)
                each_tile(act, body)

            if "F0" in phases:
                root(2)
                bit_ffn("F0", False)
            if "L1" in phases:
                root(3)

                def l1(t, p):
                    u = t + 1
                    if live(u):
                        wait(act, "L1_xt", u + 1)
                        wait(act, "L1_sp", u - 1)
                        act.activation(xnT[:, 1 - p, :], bank[0][:, 0:P], ACT.Copy).then_inc(S("L1_xe"), 1)
                        wait(act, "L1_nm", u + 1)
                        wait(act, "L1_tp", u - 1)
                        act.activation(hid2[:, 1 - p, 0:P], hid[:, 1 - p, 0:P], ACT.Exp,
                                       bias=small[:, 1 - p, 0:1],
                                       accum_out=small[:, 1 - p, 1:2]).then_inc(S("L1_ex"), 1)
                    if live(t):
                        wait(act, "L1_tp", t + 1)
                        wait(act, "L1_pv", t - 1)
                        act.activation(oT[:, p, :], bank[2][:, 0:P], ACT.Copy).then_inc(S("L1_te"), 1)
                each_tile(act, l1)
            if "F1" in phases:
                root(4)
                bit_ffn("F1", True)
            if "L2" in phases:
                root(5)
                attention("L2")
            if "F2" in phases:
                root(6)

                def route(t, p):
                    if live(t):
                        wait(act, "R_xt", t + 1)
                        wait(act, "R_lp", t - 1)
                        act.activation(xnT[:, p, :], bank[p][:, 0:P], ACT.Copy).then_inc(S("R_xe"), 1)
                each_tile(act, route)
                act.wait_ge(S("R_sub"), 1)
                act.activation(route_a[:, :, :], route_b[:, :, :], ACT.Exp).then_inc(S("R_exp"), 1)

                act.wait_ge(S("R_slots"), 1)

                def slots(t, p):
                    u = t + 1
                    if live(u, NS):
                        wait(act, "G_xt", u + 1)
                        wait(act, "G_hp", u - 1)
                        act.activation(xnT[:, 1 - p, :], bank[4][:, 0:P], ACT.Copy).then_inc(S("G_xe"), 1)
                    if live(t, NS):
                        e = act.value_load(expert_int[0:1, bass.ds(t, 1)], min_val=0, max_val=NE - 1)
                        wait(act, "G_ht", t + 1)
                        wait(act, "G_yp", t - 1)
                        for c in range(NC):
                            m = act.activation(hid2[:, p, c * P:(c + 1) * P], bank[2 + p][:, c * P:(c + 1) * P],
                                               ACT.Gelu_apprx_tanh, bias=moe_b1[:, bass.ds(e * NC + c, 1)])
                        m.then_inc(S("G_ge"), 1)
                act.wait_ge(S("R_b1"), 1)
                each_tile(act, slots, n=NS)
            if "L3" in phases:
                root(7)
                attention("L3")
            if "F3" in phases:
                root(8)
                act.wait_ge(S("f3_bias"), 1)

                def f3(t, p):
                    u = t + 1
                    if live(u):
                        wait(act, "F3_xt", u + 1)
                        wait(act, "F3_hp", u - 1)
                        act.activation(xnT[:, 1 - p, :], bank[4][:, 0:P], ACT.Copy).then_inc(S("F3_xe"), 1)
                        wait(act, "F3_hp", u + 1)
                        wait(act, "F3_yp", u - 1)
                        for c in range(NC):
                            g = act.activation(hid[:, 1 - p, c * P:(c + 1) * P], bank[1 - p][:, c * P:(c + 1) * P],
                                               ACT.Gelu, bias=up_bias[:, c:c + 1])
                        g.then_inc(S("F3_ge"), 1)
                each_tile(act, f3)

        @block.tensor
        def _(pe):
            pe.wait_ge(S("pool_set"), 4)
            pe.wait_ge(S("w_l0"), 64)
            for i in range(4):
                m = pe.transpose(bank[7][:, i * P:(i + 1) * P], l0_nat[:, i, :], ident[:, :])
            m.then_inc(S("wT"), 1)
            pe.wait_ge(S("w_con"), 64)
            for i in range(NC):
                m = pe.transpose(bank[6][:, i * P:(i + 1) * P], con_nat[:, i, :], ident[:, :])
            m.then_inc(S("wT"), 1)
            pe.wait_ge(S("w_moe"), 16 * 4)
            pe.transpose(bank[5][:, 0:NE * NC], moe_b1n[:, :], ident[0:NE * NC, 0:NE * NC]).then_inc(S("wT"), 1)
            pe.wait_ge(S("mask_f"), 1)
            pe.transpose(bank[5][:, P:P + NT], mask_f[:, :], ident[0:NT, 0:NT]).then_inc(S("wT"), 1)
            pe.wait_ge(S("wT_out"), 1)

            def l0a(t, p):
                u = t
                if live(u):
                    wait(pe, "a_xn", u + 1)
                    wait(pe, "a_xe", u - 1)
                    wait(pe, "a_cs", u - 1)
                    pe.transpose(bank[p][:, 0:P], xn[:, p, :], ident[:, :])
                    pe.transpose(bank[4 + p][:, 0:P], ctx_one[:, p, :], ident[:, :]).then_inc(S("a_xt"), 1)
                    wait(pe, "a_xe", u + 1)
                    wait(pe, "a_cs", u + 1)
                    wait(pe, "a_qv", 2 * (u - 1))
                    pe.matmul(bank[2 + p][:, 0:P], xnT[:, p, :], l0_T[:, 0, :], start=True, stop=True)
                    pe.matmul(bank[2 + p][:, P:2 * P], oT[:, p, :], l0_T[:, 2, :], start=True,
                              stop=True).then_inc(S("a_qp"), 1)
            each_tile(pe, l0a)

            def attention(layer):
                wide = layer != "L2"
                if layer == "L0":
                    pe.wait_ge(S("pool_set"), 21)
                else:
                    pe.wait_ge(S("pad"), 4 if layer == "L2" else 6)

                def tokens(u, p):
                    wait(pe, layer + "_xn", u + 1)
                    wait(pe, layer + "_ve", u)
                    pe.transpose(bank[7][:, 0:P], xn[:, p, :], ident[:, :]).then_inc(S(layer + "_xt"), 1)

                def own_values(u, p):
                    wait(pe, layer + "_xe", u + 1)
                    if wide:
                        m = pe.matmul(bank[7][:, P:2 * P], ctx_one[:, p, :], l3_wv[:, :], start=True, stop=True)
                    else:
                        m = pe.matmul(bank[7][:, P:P + DH], ctx_one[:, p, :], l2_wkv[:, DH:2 * DH],
                                      start=True, stop=True)
                    m.then_inc(S(layer + "_vp"), 1)

                def keys(u, p):
                    wait(pe, layer + "_cs", u + 1)
                    wait(pe, layer + "_ke", u)
                    for a in range(NA if wide else 1):
                        o = bank[6][:, a * P:(a + 1) * P]
                        if layer == "L0":
                            m = pe.matmul(o, ctx_pad[:, p, a, :, :].rearrange("i j d -> i (j d)"), l0_T[:, 1, :],
                                          start=True, stop=True)
                        else:
                            m = pe.matmul(o, wk_pad[:, a, :, :].rearrange("i j d -> i (j d)"),
                                          tile_of(contextT, u), start=True, stop=True)
                    m.then_inc(S(layer + "_kp"), 1)

                def queries(u, p):
                    wait(pe, layer + "_ma", u)
                    if layer == "L0":
                        wait(pe, "L0_q_in", 16 * (u + 1))
                    else:
                        wait(pe, layer + "_xe", u + 1)
                    for a in range(NA):
                        o = bank[5][:, a * P:(a + 1) * P]
                        if layer == "L0":
                            m = pe.transpose(o, q_rows[:, p, a, :, :].rearrange("i j d -> i (j d)"), ident[:, :])
                        else:
                            m = pe.matmul(o, wq_pad[:, a, :, :].rearrange("i j d -> i (j d)"), xnT[:, p, :],
                                          start=True, stop=True)
                    m.then_inc(S(layer + "_qp"), 1)

                def keys_of(p, a):
                    return keys_alone[:, p, a if wide else 0, :, :]

                def scores(u, p, a):
                    if a == 0:
                        wait(pe, layer + "_qe", u + 1)
                        wait(pe, layer + "_ke", u + 1)
                    wait(pe, layer + "_mx", 4 * u + a - 1)
                    pe.matmul(bank[a % 2][:, :], qT[:, p, a, :],
                              keys_of(p, a).rearrange("c j k -> c (j k)"), start=True,
                              stop=True).then_inc(S(layer + "_sp"), 1)

                def scores_by_key(t, p, j):
                    if j == 0:
                        wait(pe, layer + "_ma", t + 1)
                    wait(pe, layer + "_ex", 4 * t + j - 1)
                    for a in range(NA):
                        m = pe.matmul(bank[2 + j % 2][:, a * P:(a + 1) * P], keys_of(p, a)[:, j, :],
                                      qT[:, p, a, :], start=True, stop=True)
                    m.then_inc(S(layer + "_st"), 1)

                def values(t, p, j):
                    if j == 0:
                        wait(pe, layer + ("_on" if layer == "L0" else "_res"), t)
                        if layer == "L0":
                            wait(pe, "L0_v_in", 16 * (t + 1))
                        else:
                            wait(pe, layer + "_ve", t + 1)
                        if layer == "L3":
                            wait(pe, "L3_om", t + 1)
                            pe.matmul(bank[4][:, 0:VW], hid[:, p, 0:P], values_of(p, NH), start=True,
                                      stop=False)
                    wait(pe, "L3_causal" if layer == "L3" else layer + "_ex", 4 * t + j + 1)
                    for a in range(NA):
                        m = pe.matmul(bank[4][:, 0:VW], probs[:, j, a, :], values_of(p, NJ * a + j),
                                      start=(layer != "L3" and j == 0 and a == 0),
                                      stop=(j == NJ - 1 and a == NA - 1))
                    m.then_inc(S(layer + "_pv"), 1)

                def body(t, p):
                    if live(t):
                        wait(pe, layer + "_mx", 4 * (t + 1))
                        for a in range(NA):
                            m = pe.transpose(bank[5][:, a * P:(a + 1) * P],
                                             nmax[:, p, a, :, :].rearrange("q j d -> q (j d)"), ident[:, :])
                        m.then_inc(S(layer + "_mt"), 1)
                    if live(t - 1) and layer != "L0":
                        wait(pe, layer + "_on", t)
                        wait(pe, layer + "_oe", t - 1)
                        pe.transpose(bank[4][:, 256:384], o_tok[:, 1 - p, :], ident[:, :]).then_inc(S(layer + "_ot"), 1)
                    if live(t + 1):
                        if layer != "L0":
                            tokens(t + 1, 1 - p)
                        keys(t + 1, 1 - p)
                    if live(t - 1) and layer != "L0":
                        wait(pe, layer + "_oe", t)
                        wait(pe, layer + "_res", t - 1)
                        pe.matmul(bank[4][:, 384:512], oT[:, 1 - p, :], (l2_wo if layer == "L2" else l3_wo)[:, :],
                                  start=True, stop=True).then_inc(S(layer + "_yp"), 1)
                    if live(t + 1):
                        if layer != "L0":
                            own_values(t + 1, 1 - p)
                        queries(t + 1, 1 - p)
                    for j in range(NJ):
                        if live(t):
                            scores_by_key(t, p, j)
                        if live(t + 1):
                            scores(t + 1, 1 - p, j)
                        if live(t) and j > 0:
                            values(t, p, j - 1)
                    if live(t):
                        values(t, p, NJ - 1)
                each_tile(pe, body)

            attention("L0")

            def l0c(t, p):
                u = t + 1
                if live(u):
                    wait(pe, "c_os", u + 1)
                    wait(pe, "c_oe", u - 1)
                    pe.transpose(bank[1 - p][:, 0:P], o_tok[:, 1 - p, :], ident[:, :]).then_inc(S("c_ot"), 1)
                if live(t):
                    wait(pe, "c_oe", t + 1)
                    wait(pe, "c_res", t - 1)
                    pe.matmul(bank[2 + p][:, 0:P], oT[:, p, :], l0_T[:, 3, :], start=True,
                              stop=True).then_inc(S("c_yp"), 1)
            each_tile(pe, l0c)

            def bit_ffn(layer, gated):
                for i in (0, 1, 2):
                    if i == 1 and not gated:
                        continue
                    n = {("F0", 0): 1, ("F0", 2): 2, ("F1", 0): 3, ("F1", 1): 4, ("F1", 2): 5}[layer, i]
                    pe.wait_ge(S("wq_ready"), n)
                    for c in range(NC):
                        m = pe.transpose(bank[i][:, :].bitcast(BF16)[:, c * P:(c + 1) * P],
                                         quant_bf[:, i, c * P:(c + 1) * P], ident_bf[:, :])
                    m.then_inc(S("wqT"), 1)
                pe.wait_ge(S("wqT_out"), 2 if not gated else 5)

                def body(t, p):
                    u = t + 1
                    if live(u):
                        wait(pe, layer + "_xn", u + 1)
                        wait(pe, layer + "_xe", u)
                        pe.transpose(bank[5][:, :].bitcast(BF16)[:, 0:P], xq_bf[:, 1 - p, :],
                                     ident_bf[:, :]).then_inc(S(layer + "_xt"), 1)
                        wait(pe, layer + "_xe", u + 1)
                        wait(pe, layer + "_hm" if gated else layer + "_ge", u - 1)
                        m = pe.matmul(bank[2 * (1 - p)][:, :], xqT_bf[:, 1 - p, :], ffn_wT[:, 0, :],
                                      start=True, stop=True)
                        if gated:
                            m = pe.matmul(bank[2 * (1 - p) + 1][:, :], xqT_bf[:, 1 - p, :], ffn_wT[:, 1, :],
                                          start=True, stop=True)
                        m.then_inc(S(layer + "_hp"), 1)
                    if live(t):
                        wait(pe, layer + "_hq", t + 1)
                        wait(pe, layer + "_he", t)
                        for c in range(NC):
                            m = pe.transpose(bank[4][:, :].bitcast(BF16)[:, c * P:(c + 1) * P],
                                             hid_bf[:, p, c * P:(c + 1) * P], ident_bf[:, :])
                        m.then_inc(S(layer + "_ht"), 1)
                    if live(t):
                        wait(pe, layer + "_he", t + 1)
                        wait(pe, layer + "_res", t - 1)
                        for c in range(NC):
                            m = pe.matmul(bank[6 + p][:, 0:P], hidT_bf[:, p, c * P:(c + 1) * P],
                                          ffn_wT[:, 2, c * P:(c + 1) * P], start=(c == 0), stop=(c == NC - 1))
                        m.then_inc(S(layer + "_yp"), 1)
                each_tile(pe, body)

            if "F0" in phases:
                pe.wait_ge(S("wsum"), 1)
                pe.matmul(bank[7][:, 0:3], mean_mat[:, :], quant_sum[:, 0:3], start=True,
                          stop=True).then_inc(S("wmean"), 1)
                bit_ffn("F0", False)
            if "L1" in phases:
                def l1(t, p):
                    u = t + 1
                    if live(u):
                        wait(pe, "L1_xn", u + 1)
                        wait(pe, "L1_xe", u)
                        pe.transpose(bank[0][:, 0:P], xn[:, 1 - p, :], ident[:, :]).then_inc(S("L1_xt"), 1)
                        wait(pe, "L1_xe", u + 1)
                        wait(pe, "L1_sm", u)
                        pe.matmul(bank[1][:, 0:P], xnT[:, 1 - p, :], tile_of(contextT, u), start=True,
                                  stop=True).then_inc(S("L1_sp"), 1)
                    if live(t):
                        wait(pe, "L1_te", t + 1)
                        wait(pe, "L1_res", t - 1)
                        pe.matmul(bank[3 + p][:, 0:P], oT[:, p, :], tile_of(context, t), start=True,
                                  stop=True).then_inc(S("L1_pv"), 1)
                    if live(u):
                        wait(pe, "L1_ex", u + 1)
                        wait(pe, "L1_te", u)
                        pe.transpose(bank[2][:, 0:P], hid2[:, 1 - p, 0:P], ident[:, :]).then_inc(S("L1_tp"), 1)
                each_tile(pe, l1)
            if "F1" in phases:
                pe.wait_ge(S("wsum"), 2)
                pe.matmul(bank[7][:, 0:3], mean_mat[:, :], quant_sum[:, 0:3], start=True,
                          stop=True).then_inc(S("wmean"), 1)
                bit_ffn("F1", True)
            if "L2" in phases:
                attention("L2")
            if "F2" in phases:
                def route(t, p):
                    if live(t):
                        wait(pe, "R_xn", t + 1)
                        wait(pe, "R_xe", t - 1)
                        pe.transpose(bank[p][:, 0:P], xn[:, p, :], ident[:, :]).then_inc(S("R_xt"), 1)
                        wait(pe, "R_xe", t + 1)
                        wait(pe, "R_lg", t - 1)
                        pe.matmul(bank[2 + p][:, 0:NE], xnT[:, p, :], switch_w[:, :], start=True,
                                  stop=True).then_inc(S("R_lp"), 1)
                each_tile(pe, route)

                pe.wait_ge(S("R_hot"), 1)
                hot = route_b[:, :, :].rearrange("p t e -> p (t e)")
                pe.matmul(bank[0][:, 0:NT * NE], earlier[:, :], hot, start=True, stop=True)
                pe.matmul(bank[1][:, 0:NT * NE], ones[:, :], hot, start=True, stop=True).then_inc(S("R_rank"), 1)

                def slots(t, p):
                    u = t + 1
                    if live(u, NS):
                        wait(pe, "G_in", 16 * (u + 1))
                        wait(pe, "G_xe", u)
                        pe.transpose(bank[4][:, 0:P], xn[:, 1 - p, :], ident[:, :]).then_inc(S("G_xt"), 1)
                    if live(t, NS):
                        wait(pe, "G_hs", t + 1)
                        wait(pe, "G_ge", t - 1)
                        for c in range(NC):
                            m = pe.transpose(bank[2 + p][:, c * P:(c + 1) * P], hid[:, p, c * P:(c + 1) * P],
                                             ident[:, :])
                        m.then_inc(S("G_ht"), 1)
                    if live(u, NS):
                        e = pe.value_load(expert_int[0:1, bass.ds(u, 1)], min_val=0, max_val=NE - 1)
                        wait(pe, "G_xe", u + 1)
                        wait(pe, "G_hs", u - 1)
                        pe.matmul(bank[1 - p][:, :], xnT[:, 1 - p, :], moe_w1[:, bass.ds(e * HID, HID)],
                                  start=True, stop=True).then_inc(S("G_hp"), 1)
                    if live(t, NS):
                        e = pe.value_load(expert_int[0:1, bass.ds(t, 1)], min_val=0, max_val=NE - 1)
                        wait(pe, "G_ge", t + 1)
                        wait(pe, "G_yo", t - 1)
                        w2 = moe_w2[:, :, :, :].rearrange("f e c d -> f (e c d)")
                        for c in range(NC):
                            m = pe.matmul(bank[5 + p][:, 0:P], hid2[:, p, c * P:(c + 1) * P],
                                          w2[:, bass.ds(e * HID + c * P, P)], start=(c == 0), stop=(c == NC - 1))
                        m.then_inc(S("G_yp"), 1)
                pe.wait_ge(S("w_exp"), 32)
                pe.wait_ge(S("R_slots"), 1)
                each_tile(pe, slots, n=NS)
            if "L3" in phases:
                attention("L3")
            if "F3" in phases:
                pe.wait_ge(S("bf_used"), 2 * STAGES)
                for c in range(NC):
                    m = pe.transpose(bank[6][:, c * P:(c + 1) * P], bf_dn[:, STAGES % 2, c * P:(c + 1) * P],
                                     ident[:, :])
                m.then_inc(S("wT"), 1)
                pe.wait_ge(S("up_row"), 1)
                for c in range(NC):
                    m = pe.matmul(bank[5][:, c:c + 1], up_row[0:1, c * P:(c + 1) * P], ones[0:1, 0:1],
                                  start=True, stop=True)
                m.then_inc(S("wT"), 1)
                pe.wait_ge(S("f3_bias"), 1)

                def f3(t, p):
                    u = t + 1
                    if live(u):
                        wait(pe, "F3_xn", u + 1)
                        wait(pe, "F3_xe", u)
                        pe.transpose(bank[4][:, 0:P], xn[:, 1 - p, :], ident[:, :]).then_inc(S("F3_xt"), 1)
                        wait(pe, "F3_xe", u + 1)
                        wait(pe, "F3_ge", u - 1)
                        for c in range(NC):
                            m = pe.matmul(bank[1 - p][:, c * P:(c + 1) * P],
                                          bf_up[:, STAGES % 2, 0, c * P:(c + 1) * P], xnT[:, 1 - p, :],
                                          start=True, stop=True)
                        m.then_inc(S("F3_hp"), 1)
                    if live(t):
                        wait(pe, "F3_ge", t + 1)
                        wait(pe, "F3_res", t - 1)
                        for c in range(NC):
                            m = pe.matmul(bank[2 + p][:, 0:P], hid[:, p, c * P:(c + 1) * P], w_down[:, c, :],
                                          start=(c == 0), stop=(c == NC - 1))
                        m.then_inc(S("F3_yp"), 1)
                each_tile(pe, f3)

        @block.vector
        def _(dve):
            n_link = 0

            def link(ins):
                nonlocal n_link
                n_link += 1
                ins.then_inc(S("dve_link"), 1)
                dve.wait_ge(S("dve_link"), n_link)

            def count(ins, name, n=1):
                ins.then_inc(S(name), n)

            def tile_stats(u):
                if isinstance(u, int):
                    dve.bn_stats(stats[:, u, :], x[:, u * P:(u + 1) * P]).then_inc(S("stats"), 1)
                    return
                dve.bn_stats(stats[:, bass.ds(u, 1), :].rearrange("p u s -> p (u s)"), tile_of(x, u)
                             ).then_inc(S("stats"), 1)

            def norm_stats(n, scale_by_keep=False):
                dve.wait_ge(S("stats"), NT * n)
                link(dve.tensor_tensor(var_a[:, :], stats[:, :, 2], stats[:, :, 5], ALU.add))
                link(dve.tensor_tensor(var_b[:, :], stats[:, :, 1], stats[:, :, 4], ALU.subtract))
                link(dve.scalar_tensor_tensor(out=var_b[:, :], in0=var_b[:, :], scalar=0.25, in1=var_b[:, :],
                                              op0=ALU.mult, op1=ALU.mult))
                link(dve.scalar_tensor_tensor(out=var_b[:, :], in0=var_a[:, :], scalar=1.0 / P, in1=var_b[:, :],
                                              op0=ALU.mult, op1=ALU.add))
                link(dve.tensor_scalar(var_b[:, :], var_b[:, :], EPS, None, ALU.add))
                dve.sem_inc(S("var"), 1)
                link(dve.tensor_tensor(mean[:, :], stats[:, :, 1], stats[:, :, 4], ALU.add))
                link(dve.tensor_scalar(mean[:, :], mean[:, :], 0.5, None, ALU.mult))
                dve.wait_ge(S("std"), n)
                link(dve.reciprocal(rstd[:, :], var_a[:, :]))
                if scale_by_keep:
                    link(dve.tensor_tensor(rstd[:, :], rstd[:, :], keep[:, :], ALU.mult))

            def normed(dst, u, name):
                dve.tensor_scalar(dst, tile_of(x, u), column(mean, u), column(rstd, u), ALU.subtract,
                                  ALU.mult).then_inc(S(name), 1)

            dve.wait_ge(S("pool_set"), 2)
            dve.memset(mean_mat[:, :], 1.0 / (P * HID)).then_inc(S("mean_mat"), 1)
            dve.wait_ge(S("wT"), 1)
            link(dve.tensor_copy(l0_T[:, :, :].rearrange("i n o -> i (n o)"), bank[7][:, :]))
            dve.wait_ge(S("wT"), 2)
            dve.tensor_copy(bf_dn[:, 0, :], bank[6][:, :]).then_inc(S("con_T"), 1)
            dve.wait_ge(S("keep_in"), 16)
            dve.tensor_copy(mask_f[:, :], mask_nat[:, :]).then_inc(S("mask_f"), 1)
            dve.wait_ge(S("wT"), 4)
            dve.tensor_copy(moe_b1[:, :], bank[5][:, 0:NE * NC]).then_inc(S("R_b1"), 1)
            link(dve.tensor_scalar(keep[:, :], bank[5][:, P:P + NT], 0.0, None, ALU.is_equal))
            dve.sem_inc(S("wT_out"), 1)
            dve.wait_ge(S("bias_in"), 64)
            dve.wait_ge(S("tgate"), 1)
            link(dve.tensor_scalar(bo_row[:, :], bo_row[:, :], tgate[:, 0:1], None, ALU.mult))

            def first(u):
                dve.bn_stats(stats[:, u, :], x[:, u * P:(u + 1) * P]).then_inc(S("stats"), 1)
            for u in range(NT):
                if u % 8 == 0:
                    dve.wait_ge(S("x_in"), 64)
                first(u)
            norm_stats(1)
            dve.wait_ge(S("ctx_in"), 64)

            def l0a(t, p):
                u = t
                if live(u):
                    wait(dve, "a_xt", u - 1)
                    dve.tensor_copy(ctx_one[:, p, :], tile_of(context, u)).then_inc(S("a_cc"), 1)
                    wait(dve, "a_cc", u + 1)
                    normed(xn[:, p, :], u, "a_xn")
                    wait(dve, "a_xt", u + 1)
                    wait(dve, "a_qp", u - 1)
                    wait(dve, "a_ctxT", u - 1)
                    dve.tensor_copy(oT[:, p, :], bank[4 + p][:, 0:P]).then_inc(S("a_cs"), 1)
                u = t - 1
                if live(u):
                    wait(dve, "a_qp", u + 1)
                    for stage, half, bias in ((stage_q, 0, bq_row), (stage_v, 1, bv_row)):
                        dve.tensor_tensor(stage[:, bass.ds(u, 1), :].rearrange("p u d -> p (u d)"),
                                          bank[2 + 1 - p][:, half * P:(half + 1) * P], bias[:, :],
                                          ALU.add).then_inc(S("a_qv"), 1)
            each_tile(dve, l0a)

            def attention(layer):
                wide = layer != "L2"
                gate = ATT[layer]["gate"]

                def body(t, p):
                    if live(t):
                        wait(dve, layer + "_mt", t + 1)
                        dve.tensor_tensor(qT[:, p, :, :].rearrange("c a q -> c (a q)"),
                                          qT[:, p, :, :].rearrange("c a q -> c (a q)"), bank[5][:, :],
                                          ALU.add).then_inc(S(layer + "_ma"), 1)
                    u = t + 1
                    if live(u):
                        wait(dve, layer + "_kp", u + 1)
                        wait(dve, layer + "_st", 4 * (u - 1))
                        for j in range(NJ):
                            c = slice(PG * j, PG * (j + 1))
                            new = bank[6][c, :].rearrange("c (a k) -> c a k", a=NA)
                            if layer == "L0":
                                m = dve.tensor_tensor(keys_alone[c, 1 - p, :, j, :], new,
                                                      over_blocks(key_add_l0[c, :], NA), ALU.add)
                            elif wide:
                                m = dve.tensor_scalar(keys_alone[c, 1 - p, :, j, :], new, key_add[c, 0:1], None,
                                                      ALU.add)
                            else:
                                m = dve.tensor_scalar(keys_alone[c, 1 - p, 0, j, :], new[:, 0, :],
                                                      key_add[c, 0:1], None, ALU.add)
                        m.then_inc(S(layer + "_ke"), 1)
                    u = t - 1
                    if live(u) and layer != "L0":
                        wait(dve, layer + "_yp", u + 1)
                        dve.scalar_tensor_tensor(out=tile_of(x, u), in0=bank[4][:, 384:512],
                                                 scalar=tgate[:, gate:gate + 1], in1=tile_of(x, u),
                                                 op0=ALU.mult, op1=ALU.add).then_inc(S(layer + "_res"), 1)
                    u = t + 2
                    if live(u) and layer != "L0":
                        wait(dve, layer + "_xt", u - 1)
                        normed(xn[:, p, :], u, layer + "_xn")
                    u = t + 1
                    if live(u):
                        wait(dve, layer + "_mt", u - 1)
                        if layer == "L3":
                            for j in range(NJ):
                                wait(dve, layer + "_sp", 4 * u + j + 1)
                                if j >= 1:
                                    wait(dve, layer + "_mk", 4 * u + j)
                                dve.tensor_tensor(masked[:, j % 2, :, :],
                                                  bank[j % 2][:, :].rearrange("q (a k) -> q a k", a=NA),
                                                  over_blocks(future_add[:, :], NA),
                                                  ALU.add).then_inc(S(layer + "_mk"), 1)
                                wait(dve, layer + "_mk", 4 * u + j + 1)
                                dve.tensor_reduce(nmax[:, 1 - p, j, :, DH], masked[:, j % 2, :, :], AX.X, ALU.max,
                                                  negate=True).then_inc(S(layer + "_mx"), 1)
                        else:
                            for j in range(NJ):
                                wait(dve, layer + "_sp", 4 * u + j + 1)
                                dve.tensor_reduce(nmax[:, 1 - p, j, :, DH],
                                                  bank[j % 2][:, :].rearrange("q (a k) -> q a k", a=NA), AX.X,
                                                  ALU.max, negate=True).then_inc(S(layer + "_mx"), 1)
                    u = t - 1
                    if live(u) and layer != "L0":
                        wait(dve, layer + "_res", u + 1)
                        tile_stats(u)
                    if layer == "L3" and live(t + 1):
                        wait(dve, "L3_pv", 4 * t)
                        dve.tensor_copy(hid[:, 1 - p, 0:P], tile_of(open_mask, t + 1)).then_inc(S("L3_om"), 1)
                    if live(t):
                        wait(dve, layer + "_pv", 4 * (t + 1))
                        dve.reciprocal(o_inv[:, p, :], bank[4][:, P:VW]).then_inc(S(layer + "_oi"), 1)
                        wait(dve, layer + "_oi", t + 1)
                        if layer == "L0":
                            wait(dve, "L0_o_out", 16 * (t - 1))
                        else:
                            wait(dve, layer + "_ot", t - 1)
                        dve.tensor_tensor(o_tok[:, p, :].rearrange("q (h d) -> q h d", d=DH),
                                          bank[4][:, 0:P].rearrange("q (h d) -> q h d", d=DH),
                                          o_inv[:, p, :].unsqueeze(2).broadcast_to([P, NH, DH]),
                                          ALU.mult).then_inc(S(layer + "_on"), 1)
                if layer == "L0":
                    dve.wait_ge(S("l0a_stored"), 16 * 8)
                if layer != "L2":
                    for p in range(2):
                        link(dve.memset(keys_alone[:, p, :, :, :].rearrange("c a j k -> c (a j k)"), 0.0))
                each_tile(dve, body, lead=1 if layer == "L0" else 2)

            attention("L0")

            def l0c(t, p):
                u = t + 1
                if live(u):
                    wait(dve, "L0_o_in", 16 * (u + 1))
                    wait(dve, "c_ot", u - 1)
                    dve.tensor_copy(o_tok[:, 1 - p, :], tile_of(shared, u)).then_inc(S("c_os"), 1)
                if live(t):
                    dve.tensor_tensor(tile_of(x, t), tile_of(x, t), bo_row[:, :], ALU.add).then_inc(S("c_b"), 1)
                    wait(dve, "c_b", t + 1)
                    wait(dve, "c_yp", t + 1)
                    dve.scalar_tensor_tensor(out=tile_of(x, t), in0=bank[2 + p][:, 0:P], scalar=tgate[:, 0:1],
                                             in1=tile_of(x, t), op0=ALU.mult, op1=ALU.add).then_inc(S("c_res"), 1)
                    wait(dve, "c_res", t + 1)
                    tile_stats(t)
            wait(dve, "L0_o_out", 16 * NT)
            each_tile(dve, l0c)

            def quantised_weights(which, n_sum):
                for i in which:
                    link(dve.tensor_reduce(quant_sum[:, i:i + 1], quant_src[:, i, :], AX.X, ALU.add,
                                           apply_absolute_value=True))
                dve.sem_inc(S("wsum"), 1)
                dve.wait_ge(S("wmean"), n_sum)
                link(dve.tensor_scalar(quant_scale[:, :], bank[7][:, 0:3], EPS, None, ALU.max))
                link(dve.reciprocal(quant_inv[:, :], quant_scale[:, :]))
                for i in which:
                    link(dve.tensor_scalar(quant_tmp[:, i, :], quant_src[:, i, :], quant_inv[:, i:i + 1], MAGIC,
                                           ALU.mult, ALU.add))
                    link(dve.tensor_scalar(quant_tmp[:, i, :], quant_tmp[:, i, :], MAGIC, 1.0, ALU.subtract,
                                           ALU.min))
                    dve.tensor_scalar(quant_bf[:, i, :], quant_tmp[:, i, :], -1.0, None,
                                      ALU.max).then_inc(S("wq_ready"), 1)

            def bit_ffn(layer, gated, gate):
                base = 0 if not gated else 2
                for k, i in enumerate((0, 1, 2) if gated else (0, 2)):
                    dve.wait_ge(S("wqT"), base + k + 1)
                    dve.tensor_copy(ffn_wT[:, i, :], bank[i][:, :].bitcast(BF16)[:, 0:HID]).then_inc(S("wqT_out"), 1)
                link(dve.tensor_scalar(ffn_sw[:, :], quant_scale[:, :], 1.0 / QMAX, None, ALU.mult))
                link(dve.tensor_scalar(ffn_sw[:, 2:3], ffn_sw[:, 2:3], tgate[:, gate:gate + 1], None, ALU.mult))

                LA, LB = layer + "_qa", layer + "_qb"

                def body(t, p):
                    u = t + 2
                    if live(u):
                        w = 5 * u
                        dve.tensor_scalar(xn[:, p, :], tile_of(x, u), column(mean, u), column(rstd, u),
                                          ALU.subtract, ALU.mult).then_inc(S(LA), 1)
                        wait(dve, LA, w + 1)
                        dve.tensor_reduce(small[:, p, 0:1], xn[:, p, :], AX.X, ALU.max,
                                          apply_absolute_value=True).then_inc(S(LA), 1)
                        wait(dve, LA, w + 2)
                        dve.tensor_scalar(small[:, p, 2:3], small[:, p, 0:1], EPS, None,
                                          ALU.max).then_inc(S(LA), 1)
                        wait(dve, LA, w + 3)
                        dve.reciprocal(small[:, p, 1:2], small[:, p, 2:3]).then_inc(S(LA), 1)
                        wait(dve, layer + ("_hm" if gated else "_ge"), u - 1)
                        dve.tensor_tensor(small[:, p, 3:5], ffn_sw[:, 0:2],
                                          small[:, p, 2:3].broadcast_to([P, 2]), ALU.mult)
                        wait(dve, LA, w + 4)
                        dve.tensor_scalar(small[:, p, 5:6], small[:, p, 1:2], QMAX, None,
                                          ALU.mult).then_inc(S(LA), 1)
                        wait(dve, LA, w + 5)
                        dve.tensor_scalar(xq_f[:, p, :], xn[:, p, :], small[:, p, 5:6], MAGIC, ALU.mult,
                                          ALU.add).then_inc(S(layer + "_qx"), 1)
                        wait(dve, layer + "_qx", u + 1)
                        wait(dve, layer + "_xt", u - 1)
                        dve.tensor_scalar(xq_bf[:, p, :], xq_f[:, p, :], MAGIC, QMAX, ALU.subtract,
                                          ALU.min).then_inc(S(layer + "_xn"), 1)
                    if live(t):
                        wait(dve, layer + "_yp", t + 1)
                        dve.scalar_tensor_tensor(out=tile_of(x, t), in0=bank[6 + p][:, 0:P],
                                                 scalar=small[:, p, 9:10], in1=tile_of(x, t), op0=ALU.mult,
                                                 op1=ALU.add).then_inc(S(layer + "_res"), 1)
                    u = t + 1
                    if live(u):
                        q = 1 - p
                        w = 4 * u
                        wait(dve, layer + "_ge", u + 1)
                        if gated:
                            src = hid2
                            dve.scalar_tensor_tensor(out=hid2[:, q, :], in0=bank[2 * q + 1][:, :],
                                                     scalar=small[:, q, 4:5], in1=hid[:, q, :], op0=ALU.mult,
                                                     op1=ALU.mult).then_inc(S(layer + "_hm"), 1)
                            wait(dve, layer + "_hm", u + 1)
                        else:
                            src = hid
                        dve.tensor_reduce(small[:, q, 6:7], src[:, q, :], AX.X, ALU.max,
                                          apply_absolute_value=True).then_inc(S(LB), 1)
                        wait(dve, LB, w + 1)
                        dve.tensor_scalar(small[:, q, 7:8], small[:, q, 6:7], EPS, None,
                                          ALU.max).then_inc(S(LB), 1)
                        wait(dve, LB, w + 2)
                        dve.reciprocal(small[:, q, 8:9], small[:, q, 7:8]).then_inc(S(LB), 1)
                        dve.tensor_tensor(small[:, q, 9:10], small[:, q, 7:8], ffn_sw[:, 2:3], ALU.mult)
                        wait(dve, LB, w + 3)
                        dve.tensor_scalar(small[:, q, 10:11], small[:, q, 8:9], QMAX, None,
                                          ALU.mult).then_inc(S(LB), 1)
                        wait(dve, LB, w + 4)
                        dve.tensor_scalar(src[:, q, :], src[:, q, :], small[:, q, 10:11], MAGIC, ALU.mult,
                                          ALU.add).then_inc(S(layer + "_qh"), 1)
                        wait(dve, layer + "_qh", u + 1)
                        wait(dve, layer + "_ht", u - 1)
                        dve.tensor_scalar(hid_bf[:, q, :], src[:, q, :], MAGIC, QMAX, ALU.subtract,
                                          ALU.min).then_inc(S(layer + "_hq"), 1)
                    if live(t):
                        wait(dve, layer + "_res", t + 1)
                        tile_stats(t)
                each_tile(dve, body, lead=2)

            if "F0" in phases:
                dve.wait_ge(S("w_f0"), 32)
                link(dve.memset(quant_sum[:, :], 0.0))
                quantised_weights((0, 2), 1)
                norm_stats(2)
                bit_ffn("F0", False, 4)
            if "L1" in phases:
                norm_stats(3)

                def l1(t, p):
                    u = t + 2
                    if live(u):
                        wait(dve, "L1_xt", u - 1)
                        normed(xn[:, p, :], u, "L1_xn")
                    u = t + 1
                    if live(u):
                        q = 1 - p
                        wait(dve, "L1_sp", u + 1)
                        wait(dve, "L1_ex", u - 1)
                        dve.scalar_tensor_tensor(out=hid[:, q, 0:P], in0=bank[1][:, 0:P], scalar=L1_SCALE,
                                                 in1=tile_of(add_mask, u), op0=ALU.mult,
                                                 op1=ALU.add).then_inc(S("L1_sm"), 1)
                        dve.wait_ge(S("L1_sm"), u + 1)
                        dve.tensor_reduce(small[:, q, 0:1], hid[:, q, 0:P], AX.X, ALU.max,
                                          negate=True).then_inc(S("L1_nm"), 1)
                    if live(t):
                        wait(dve, "L1_ex", t + 1)
                        dve.reciprocal(small[:, p, 2:3], small[:, p, 1:2]).then_inc(S("L1_r"), 1)
                        dve.wait_ge(S("L1_r"), 2 * t + 1)
                        dve.tensor_scalar(small[:, p, 3:4], small[:, p, 2:3], tgate[:, 1:2], None,
                                          ALU.mult).then_inc(S("L1_r"), 1)
                        dve.wait_ge(S("L1_r"), 2 * t + 2)
                        wait(dve, "L1_pv", t + 1)
                        dve.scalar_tensor_tensor(out=tile_of(x, t), in0=bank[3 + p][:, 0:P],
                                                 scalar=small[:, p, 3:4], in1=tile_of(x, t), op0=ALU.mult,
                                                 op1=ALU.add).then_inc(S("L1_res"), 1)
                        wait(dve, "L1_res", t + 1)
                        tile_stats(t)
                dve.wait_ge(S("mask_in"), 16)
                each_tile(dve, l1, lead=2)
            if "F1" in phases:
                dve.wait_ge(S("w_f1"), 48)
                quantised_weights((0, 1, 2), 2)
                norm_stats(4)
                bit_ffn("F1", True, 5)
            if "L2" in phases:
                norm_stats(5)
                attention("L2")
            if "F2" in phases:
                norm_stats(6)

                def route(t, p):
                    u = t + 1
                    if live(u):
                        wait(dve, "R_xt", u - 1)
                        wait(dve, "R_xd", u - 1)
                        normed(xn[:, 1 - p, :], u, "R_xn")
                    if live(t):
                        wait(dve, "R_xn", t + 1)
                        dve.tensor_copy(tile_of(shared, t), xn[:, p, :]).then_inc(S("R_xd"), 1)
                        wait(dve, "R_lp", t + 1)
                        dve.tensor_tensor(logits[:, bass.ds(t, 1), :].rearrange("p u e -> p (u e)"),
                                          bank[2 + p][:, 0:NE], switch_b[:, :], ALU.add).then_inc(S("R_lg"), 1)
                each_tile(dve, route)
                dve.wait_ge(S("R_lg"), NT)

                def by_tile(i):
                    return route_m[:, i, :].unsqueeze(2).broadcast_to([P, NT, NE])

                def by_expert(ap):
                    return over_blocks(ap, NT)
                link(dve.tensor_reduce(route_m[:, 0, :], logits[:, :, :], AX.X, ALU.max))
                link(dve.tensor_tensor(route_b[:, :, :], logits[:, :, :], by_tile(0), ALU.subtract))
                dve.sem_inc(S("R_sub"), 1)
                dve.wait_ge(S("R_exp"), 1)
                link(dve.tensor_reduce(route_m[:, 1, :], route_a[:, :, :], AX.X, ALU.add))
                link(dve.reciprocal(route_m[:, 2, :], route_m[:, 1, :]))
                link(dve.tensor_scalar(route_a[:, :, :], route_b[:, :, :], 0.0, float(NE), ALU.is_lt, ALU.mult))
                link(dve.tensor_tensor(route_a[:, :, :], route_a[:, :, :], by_expert(expert_no[:, :]), ALU.add))
                link(dve.tensor_reduce(route_m[:, 0, :], route_a[:, :, :], AX.X, ALU.min))
                link(dve.tensor_tensor(route_b[:, :, :], by_expert(expert_no[:, :]), by_tile(0), ALU.is_equal))
                dve.sem_inc(S("R_hot"), 1)
                link(dve.tensor_scalar(gate[:, :], route_m[:, 2, :], tgate[:, 6:7], None, ALU.mult))
                dve.wait_ge(S("R_rank"), 1)
                here, upto, other = (bank[1][:, 0:NT * NE].rearrange("p (t e) -> p t e", e=NE), route_c, route_d)
                link(dve.tensor_copy(upto[:, :, :], here))
                back = 1
                while back < NT:
                    dve.tensor_copy(other[:, 0:back, :], upto[:, 0:back, :])
                    link(dve.tensor_tensor(other[:, back:NT, :], upto[:, back:NT, :], upto[:, 0:NT - back, :],
                                           ALU.add))
                    upto, other = other, upto
                    back *= 2
                link(dve.tensor_scalar(fill[:, 0, :], upto[:, NT - 1, :], 1.0 / P, (P - 1) / P - 0.498,
                                       ALU.mult, ALU.add))
                link(dve.tensor_scalar(fill[:, 0, :], fill[:, 0, :], MAGIC, None, ALU.add))
                link(dve.tensor_scalar(fill[:, 0, :], fill[:, 0, :], MAGIC, None, ALU.subtract))
                link(dve.tensor_copy(fill[:, 1, :], fill[:, 0, :]))
                now, then = 1, 2
                back = 1
                while back < NE:
                    dve.tensor_copy(fill[:, then, 0:back], fill[:, now, 0:back])
                    link(dve.tensor_tensor(fill[:, then, back:NE], fill[:, now, back:NE],
                                           fill[:, now, 0:NE - back], ALU.add))
                    now, then = then, now
                    back *= 2
                link(dve.tensor_scalar(expert_of[:, :], slot_no[:, :], fill[:, now, 0:1], None, ALU.is_ge))
                for e in range(1, NE - 1):
                    link(dve.scalar_tensor_tensor(out=expert_of[:, :], in0=slot_no[:, :],
                                                  scalar=fill[:, now, e:e + 1], in1=expert_of[:, :],
                                                  op0=ALU.is_ge, op1=ALU.add))
                dve.tensor_copy(expert_int[:, :], expert_of[0:1, :]).then_inc(S("R_slots"), 1)
                link(dve.tensor_tensor(fill[:, 3, :], fill[:, now, :], fill[:, 0, :], ALU.subtract))
                link(dve.tensor_scalar(fill[:, 3, :], fill[:, 3, :], float(P), None, ALU.mult))
                link(dve.tensor_tensor(upto[:, :, :], upto[:, :, :], here, ALU.subtract))
                link(dve.tensor_tensor(upto[:, :, :], upto[:, :, :],
                                       bank[0][:, 0:NT * NE].rearrange("p (t e) -> p t e", e=NE), ALU.add))
                link(dve.tensor_tensor(upto[:, :, :], upto[:, :, :], by_expert(fill[:, 3, :]), ALU.add))
                link(dve.tensor_tensor(upto[:, :, :], upto[:, :, :], route_b[:, :, :], ALU.mult))
                link(dve.tensor_reduce(route_m[:, 0, :], upto[:, :, :], AX.X, ALU.add))
                dve.tensor_copy(dest_int[:, :], route_m[:, 0, :]).then_inc(S("R_dest"), 1)

                def slots(t, p):
                    u = t + 1
                    if live(u, NS):
                        wait(dve, "G_hp", u + 1)
                        wait(dve, "G_ht", u - 1)
                        dve.tensor_copy(hid[:, 1 - p, :], bank[1 - p][:, :]).then_inc(S("G_hs"), 1)
                    if live(t, NS):
                        e = dve.value_load(expert_int[0:1, bass.ds(t, 1)], min_val=0, max_val=NE - 1)
                        wait(dve, "G_yp", t + 1)
                        wait(dve, "G_out", 16 * (t - 1))
                        dve.tensor_tensor(o_tok[:, p, :], bank[5 + p][:, 0:P], moe_b2_rows[:, bass.ds(e * P, P)],
                                          ALU.add).then_inc(S("G_yo"), 1)
                dve.wait_ge(S("R_slots"), 1)
                each_tile(dve, slots, n=NS)

                for c in range(NT // GC):
                    dve.wait_ge(S(f"gathered_{c}"), 16 * GC)
                    for t in range(c * GC, (c + 1) * GC):
                        dve.scalar_tensor_tensor(out=x[:, t * P:(t + 1) * P], in0=shared[:, t * P:(t + 1) * P],
                                                 scalar=gate[:, t:t + 1], in1=x[:, t * P:(t + 1) * P],
                                                 op0=ALU.mult, op1=ALU.add).then_inc(S("B_res"), 1)
                    dve.wait_ge(S("B_res"), (c + 1) * GC)
                    for t in range(c * GC, (c + 1) * GC):
                        tile_stats(t)
            if "L3" in phases:
                norm_stats(7, scale_by_keep=True)
                dve.wait_ge(S("open_in"), 16)
                dve.wait_ge(S("fut"), 7)
                dve.tensor_scalar(open_mask[:, :], open_mask[:, :].bitcast(I32), 0.0, None,
                                  ALU.not_equal).then_inc(S("open"), 1)
                dve.wait_ge(S("open"), 1)
                dve.tensor_tensor(open_mask[:, :].rearrange("k (t q) -> k t q", q=P),
                                  open_mask[:, :].rearrange("k (t q) -> k t q", q=P),
                                  over_blocks(future_one[:, :], NT), ALU.mult).then_inc(S("open"), 1)
                attention("L3")
            if "F3" in phases:
                norm_stats(8)
                dve.wait_ge(S("bf_used"), 2 * STAGES)
                link(dve.tensor_tensor(up_row[:, :], up_row[:, :], bf_up[0:1, STAGES % 2, 1, :], ALU.add))
                dve.sem_inc(S("up_row"), 1)
                dve.wait_ge(S("wT"), 6)
                link(dve.tensor_copy(w_down[:, :, :].rearrange("p c d -> p (c d)"), bank[6][:, :]))
                link(dve.tensor_copy(up_bias[:, :], bank[5][:, 0:NC]))
                dve.sem_inc(S("f3_bias"), 1)
                link(dve.tensor_tensor(con_bias[:, 0, :], con_bias[:, 0, :], con_bias[:, 1, :], ALU.add))
                link(dve.tensor_scalar(con_bias[:, 0, :], con_bias[:, 0, :], tgate[:, 7:8], None, ALU.mult))

                def f3(t, p):
                    u = t + 2
                    if live(u):
                        wait(dve, "F3_xt", u - 1)
                        normed(xn[:, p, :], u, "F3_xn")
                    if live(t):
                        dve.tensor_tensor(tile_of(x, t), tile_of(x, t), con_bias[:, 0, :],
                                          ALU.add).then_inc(S("F3_b"), 1)
                        wait(dve, "F3_b", t + 1)
                        wait(dve, "F3_yp", t + 1)
                        dve.scalar_tensor_tensor(out=tile_of(x, t), in0=bank[2 + p][:, 0:P],
                                                 scalar=tgate[:, 7:8], in1=tile_of(x, t), op0=ALU.mult,
                                                 op1=ALU.add).then_inc(S("F3_res"), 1)
                each_tile(dve, f3, lead=2)


def kernel(**inputs):
    import numpy as _np
    import concourse.bacc as _bacc
    from concourse import mybir as _mybir
    from concourse.bass_utils import run_bass_kernel_spmd as _run

    nc = _bacc.Bacc("TRN2", target_bir_lowering=False, num_devices=1)
    arrays, args = {}, {}
    for name, a in inputs.items():
        a = _np.ascontiguousarray(a)
        arrays[f"in_{name}_dram"] = a
        args[name] = nc.dram_tensor(f"in_{name}_dram", a.shape, _mybir.dt.from_np(a.dtype), kind="ExternalInput").ap()
    out = nc.dram_tensor("out_0_dram", (NT, P, P), F32, kind="ExternalOutput").ap()
    slots = [nc.dram_tensor(f"slot_{n}", (NS * P, P), F32).ap() for n in ("in", "out")]
    scratch = [nc.dram_tensor(f"{n}_scratch", (NT, NH, P, DH), F32).ap() for n in "qvo"]
    gated_layers(nc, args, out, *scratch, *slots)
    r = _run(nc, [arrays], core_ids=[0])
    return r.results[0]["out_0_dram"]
```

```python
from contextlib import ExitStack

import concourse.bass as bass
from concourse import mybir

ALU = mybir.AluOpType
ACT = mybir.ActivationFunctionType
AX = mybir.AxisListType
F32 = mybir.dt.float32
BF16 = mybir.dt.bfloat16
I32 = mybir.dt.int32

P = 128
NT = 32
NH, DH = 16, 8
NG, HG = 4, 4
HR = 64
NPART = 3
HID = 512
NC = HID // P
NE = 8
NS = NT + NE
GC = 8
STAGES = 9
EPS = 1e-5
MAGIC = 1.5 * 2.0 ** 23
QMAX = 127.0
NEG = -1e9
SCORE_SCALE = DH ** -0.5
L1_SCALE = P ** -0.5
LOOP_FROM = 4

LAST_PHASE = "F3"
ORDER = ["L0", "F0", "L1", "F1", "L2", "F2", "L3", "F3"]


def gated_layers(nc, A, out, q_scratch, v_scratch, o_scratch, slot_in, slot_out):
    phases = ORDER[:ORDER.index(LAST_PHASE) + 1]
    ctx = ExitStack()
    with ctx:
        def sb(name, shape, dt=F32):
            return ctx.enter_context(nc.sbuf_tensor(name, shape, dt))

        def sem(name):
            return ctx.enter_context(nc.semaphore(name))

        bank = [ctx.enter_context(nc.psum_tensor(f"bank{i}", [P, 512], F32)) for i in range(8)]

        x = sb("x", [P, NT * P])
        context = sb("context", [P, NT * P])
        contextT = sb("contextT", [P, NT * P])
        shared = sb("shared", [P, NT * P])
        add_mask = shared
        stats = sb("stats", [P, NT, 6])
        mean = sb("mean", [P, NT])
        rstd = sb("rstd", [P, NT])
        var_a = sb("var_a", [P, NT])
        var_b = sb("var_b", [P, NT])
        mean_mat = sb("mean_mat", [P, P])
        ident = sb("ident", [P, P])
        ident_bf = sb("ident_bf", [P, P], BF16)
        ones = sb("ones", [P, P])
        gates = sb("gates", [P, 8])
        tgate = sb("tgate", [P, 8])

        probs_space = sb("probs_space", [P, NH * P])
        probs = probs_space[:, :].rearrange("k (g i q) -> k g i q", g=NG, i=HG)
        l0_nat = probs_space[:, 0:4 * P].rearrange("p (n d) -> p n d", d=P)
        con_nat = probs_space[:, 4 * P:8 * P].rearrange("p (n d) -> p n d", d=P)
        logits, route_a, route_b, route_c, route_d = (
            probs_space[:, i * NT * NE:(i + 1) * NT * NE].rearrange("p (t e) -> p t e", e=NE) for i in range(5))
        l0_T = sb("l0_T", [P, 4, P])
        bq_row = sb("bq_row", [P, P])
        bv_row = sb("bv_row", [P, P])
        bo_row = sb("bo_row", [P, P])
        bk_col = sb("bk_col", [P, 1])
        no_bias = sb("no_bias", [P, 1])
        late = sb("late", [P, 8 * HID])
        quant_src = late[:, 0:3 * HID].rearrange("p (i f) -> p i f", i=3)
        quant_tmp = late[:, 3 * HID:6 * HID].rearrange("p (i f) -> p i f", i=3)
        bf_t = late[:, 0:4 * HID].rearrange("p (i f) -> p i f", i=4)
        bf_w = late[:, 4 * HID:8 * HID].rearrange("p (i f) -> p i f", i=2)
        quant_bf = sb("quant_bf", [P, 3, HID], BF16)
        quant_sum = sb("quant_sum", [P, 3])
        quant_scale = sb("quant_scale", [P, 3])
        quant_inv = sb("quant_inv", [P, 3])
        ffn_wT = sb("ffn_wT", [P, 3, HID], BF16)
        ffn_sw = sb("ffn_sw", [P, 3])
        l2_wq = sb("l2_wq", [P, P])
        l2_wkv = sb("l2_wkv", [P, 2 * DH])
        l2_wo = sb("l2_wo", [P, P])
        l3_wq = sb("l3_wq", [P, P])
        l3_wkv = sb("l3_wkv", [P, 2, P])
        l3_wo = sb("l3_wo", [P, P])
        future_add = sb("future_add", [P, P])
        future_one = sb("future_one", [P, P])
        mask_nat = sb("mask_nat", [NT, P], I32)
        mask_f = sb("mask_f", [NT, P])
        keep = sb("keep", [P, NT])
        switch_w = sb("switch_w", [P, NE])
        switch_b = sb("switch_b", [P, NE])
        moe_w1 = context[:, :]
        open_mask = context
        moe_b2_rows = sb("moe_b2_rows", [P, NE * P])
        moe_w2 = sb("moe_w2", [P, NE, NC, P])
        moe_b1 = sb("moe_b1", [P, NE * NC])
        moe_b1n = sb("moe_b1n", [NE * NC, P])
        con_bias = sb("con_bias", [P, 2, P])
        bf_up = sb("bf_up", [P, 2, 2, HID])
        bf_dn = sb("bf_dn", [P, 2, HID])
        up_bias = sb("up_bias", [P, NC])
        up_row = sb("up_row", [1, HID])
        w_down = sb("w_down", [P, NC, P])

        stage_q = shared[:, :].rearrange("p (b d) -> p b d", d=P)
        stage_v = moe_w2[:, :, :, :].rearrange("p e c d -> p (e c) d")

        xn = sb("xn", [P, 2, P])
        xnT = sb("xnT", [P, 2, P])
        o_back = xnT
        hid_space = sb("hid_space", [P, 8 * HID // 2])
        parts = hid_space[:, :].bitcast(BF16).rearrange("p (s b h r) -> p s b h r", s=2, b=2, h=NH)
        hid = hid_space[:, 0:2 * HID].rearrange("p (b f) -> p b f", b=2)
        hid2 = hid_space[:, 2 * HID:4 * HID].rearrange("p (b f) -> p b f", b=2)
        ctx_one = sb("ctx_one", [P, 2, P])
        qT = sb("qT", [P, 2, NH // 2 * P], BF16)
        kT = sb("kT", [P, 2, NH // 2 * P], BF16)
        rest = sb("rest", [P, 2, 2, P])
        VW = P + NH
        vals = sb("vals", [P, 2, (NH + 1) * VW])
        nmax = sb("nmax", [P, 2, 2, 2, NH // 2])
        nmax_parts = sb("nmax_parts", [P, 2, 2, HR], BF16)
        nmaxT = sb("nmaxT", [P, 2, P], BF16)
        head_rows = sb("head_rows", [P, NH // 2, P], BF16)
        head_rows_f = hid_space[:, 0:NH // 2 * P].rearrange("r (h k) -> r h k", h=NH // 2)
        future_bf = sb("future_bf", [P, P], BF16)
        o_inv = sb("o_inv", [P, 2, NH])
        o_tok = sb("o_tok", [P, 2, P])
        oT = sb("oT", [P, 2, P])
        hid_bf = sb("hid_bf", [P, 2, HID], BF16)
        hidT_bf = sb("hidT_bf", [P, 2, HID], BF16)
        xq_f = sb("xq_f", [P, 2, P])
        q_rows = om_one = xq_f
        xq_bf = sb("xq_bf", [P, 2, P], BF16)
        xqT_bf = sb("xqT_bf", [P, 2, P], BF16)
        small = sb("small", [P, 2, 16])
        route_m = sb("route_m", [P, 3, NT])
        expert_no = sb("expert_no", [P, NE])
        gate = sb("gate", [P, NT])
        earlier = sb("earlier", [P, P])
        slot_x = hid_bf.ap().rearrange("p b f -> p (b f)").bitcast(F32).rearrange("p (b r d) -> p b r d", b=2, r=2)
        slot_y = hidT_bf.ap().rearrange("p b f -> p (b f)").bitcast(F32).rearrange("p (b r d) -> p b r d", b=2, r=2)
        zeros = sb("zeros", [P, P])
        expert_of = sb("expert_of", [P, NS])
        expert_int = sb("expert_int", [1, NS], I32)
        slot_no = sb("slot_no", [P, NS])
        dest_int = sb("dest_int", [P, NT], I32)
        fill = sb("fill", [P, 4, NE])

        s = {}
        A_TILE = {"st": 4, "sp": 4, "ex": 4, "mx": 4, "pv": 4, "na": 4, "qb": 3, "sk": 4, "sq": 4, "qa": 4}
        OF_L0_TOO = {"kp", "sk", "sq", "tk", "tq", "ke", "qe", "st", "ex", "mx", "na", "mt", "me", "sp", "pv",
                     "oi", "on", "ot", "oe", "yp", "res"}

        def shared_name(name):
            phase, _, signal = name.partition("_")
            a_tile = A_TILE.get(signal, 1)
            if phase in ("L0", "L2", "L3") and (phase != "L0" or signal in OF_L0_TOO):
                before = {"L0": 0, "L2": 1, "L3": 2}[phase] - (signal not in OF_L0_TOO)
                if signal == "om":
                    before = 0
                return "att_" + signal, before * a_tile * NT
            if phase in ("F0", "F1"):
                return "bit_" + signal, (phase == "F1" and signal != "hm") * a_tile * NT
            return name, 0

        def S(name):
            name = shared_name(name)[0]
            if name not in s:
                s[name] = sem(name)
            return s[name]

        def wait(eng, name, value):
            if not isinstance(value, int) or value > 0:
                eng.wait_ge(S(name), value + shared_name(name)[1])
                if not isinstance(value, int) and eng.engine in (nc.sync.engine, nc.gpsimd.engine):
                    eng.sem_inc(S("sp_passed" if eng.engine == nc.sync.engine else "pool_passed"), 1)

        def up_to(value, most):
            return min(value, most) if isinstance(value, int) else value

        def live(u, n=NT):
            return not isinstance(u, int) or 0 <= u < n

        def each_tile(eng, body, lead=1, tail=1, n=NT, loop_from=LOOP_FROM):
            for t in range(-lead, loop_from):
                body(t, t % 2)
            loop_to = n - max(2, 2 * ((lead + 1) // 2))
            with eng.Fori(loop_from, loop_to - 1, 2) as i:
                body(i, 0)
                body(i + 1, 1)
            for t in range(loop_to, n + tail):
                body(t, t % 2)

        def values_of(p, h=None):
            if h is None:
                return vals[:, p, 0:NH * (VW + DH)].rearrange("k (h c) -> k h c", h=NH)[:, :, 0:DH]
            return vals[:, p, h * VW:(h + 1) * VW]

        def tile_of(buf, t):
            return buf[:, bass.ds(t * P, P)]

        def column(buf, t):
            return buf[:, bass.ds(t, 1)]

        def over_blocks(ap, n):
            return ap.unsqueeze(1).broadcast_to([ap.shape[0], n, ap.shape[1]])

        ATT = {
            "L0": dict(gate=0, lag=3, loop_from=8), "L2": dict(gate=2, lag=1, loop_from=LOOP_FROM),
            "L3": dict(gate=3, lag=1, loop_from=LOOP_FROM),
        }

        def blocks_of(operand, first, step, n):
            v = operand.rearrange("p h (b d) -> p h b d", d=DH)
            return v[:, :, first:first + step * (n - 1) + 1:step, :]

        def head(g, i):
            return 2 * HG * (g // 2) + 2 * i + g % 2

        def place(g, i=0):
            return g % 2, HG * (g // 2) + i

        BLOCKS = {"q": dict(high=(0, 1, 3), middle=(3, 2, 2), low=(4, 1, 1)),
                  "k": dict(high=(2, 1, 3), middle=(0, 5, 2), low=(1, 1, 1))}

        SET_IDENT, SET_VALS, SET_L0 = 4, 10, 18
        block = ctx.enter_context(nc.Block())

        @block.sync
        def _(sp):
            tok = "b s d -> s b d"
            for c in range(4):
                b = slice(8 * c, 8 * c + 8)
                sp.dma_start(x[:, 1024 * c:1024 * c + 1024].rearrange("p (b d) -> p b d", d=P),
                             A["x"][b].rearrange(tok)).then_inc(S("x_in"), 16)
                if c == 0:
                    sp.dma_start(l0_nat[:, 0, :], A["L0_xattn_wq"]).then_inc(S("w_l0"), 16)
                    sp.dma_start(l0_nat[:, 1, :], A["L0_xattn_wk"]).then_inc(S("w_l0"), 16)
                    sp.dma_start(l0_nat[:, 2, :], A["L0_xattn_wv"]).then_inc(S("w_l0"), 16)
                    sp.dma_start(l0_nat[:, 3, :], A["L0_xattn_wo"]).then_inc(S("w_l0"), 16)
            for c in range(4):
                b = slice(8 * c, 8 * c + 8)
                sp.dma_start(context[:, 1024 * c:1024 * c + 1024].rearrange("p (b d) -> p b d", d=P),
                             A["ctx_1024"][b].rearrange(tok)).then_inc(S("ctx_in"), 16)

            def l0b(t, p):
                u = t - 1
                if live(u):
                    wait(sp, "L0_o_out", 16 * u)
                    wait(sp, "L0_on", u + 1)
                    sp.dma_start(o_scratch[bass.ds(u, 1)].rearrange("u h i d -> i (u h) d"),
                                 o_tok[:, 1 - p, :].rearrange("i (h d) -> i h d", d=DH)).then_inc(S("L0_o_out"), 16)
                u = t - 2
                if live(u):
                    wait(sp, "L0_o_out", 16 * (u + 1))
                    wait(sp, "L0_o_in", 16 * u)
                    sp.dma_start(tile_of(shared, u),
                                 o_scratch[bass.ds(u, 1)].rearrange("u h (r c) d -> (u h r) (c d)", r=8)
                                 ).then_inc(S("L0_o_in"), 16)
                if isinstance(t, int) and t == 0:
                    sp.wait_ge(S("l0a_stored"), 32 * 4)
                u = t + 4
                if live(u):
                    wait(sp, "L0_q_in", 16 * u)
                    wait(sp, "L0_sq", 4 * (u - 1))
                    sp.dma_start(q_rows[:, p, :].rearrange("i (h d) -> i h d", d=DH),
                                 q_scratch[bass.ds(u, 1)].rearrange("u h i d -> i (u h) d")).then_inc(S("L0_q_in"), 16)
                u = t + 2
                if live(u):
                    wait(sp, "L0_v_in", 16 * u)
                    wait(sp, "L0_pv", 4 * (u - 1))
                    sp.dma_start(values_of(p),
                                 v_scratch[bass.ds(u, 1)].rearrange("u h i d -> i (u h) d")).then_inc(S("L0_v_in"), 16)

            for c in range(4):
                sp.wait_ge(S("a_qv"), 2 * 8 * (c + 1))
                if c > 0:
                    sp.wait_ge(S("l0a_stored"), 32 * c)
                for scratch, stage in ((q_scratch, stage_q), (v_scratch, stage_v)):
                    sp.dma_start(scratch[8 * c:8 * c + 8].rearrange("u h (r c) d -> (h r) u (c d)", r=8),
                                 stage[:, 8 * c:8 * c + 8, :]).then_inc(S("l0a_stored"), 16)
            sp.wait_ge(S("pool_set"), SET_VALS)
            each_tile(sp, l0b, lead=4, tail=2)

            sp.wait_ge(S("L0_os"), NT)
            sp.dma_start(add_mask[:, :].rearrange("p (b d) -> p b d", d=P),
                         A["mask_BxSxS2_ff0"].rearrange(tok)).then_inc(S("mask_in"), 16)
            sp.wait_ge(S("zero_set"), 1)
            sp.dma_start(slot_in.rearrange("(s p) d -> p s d", p=P), over_blocks(zeros[:, :], NS)
                         ).then_inc(S("zeroed"), 16)
            sp.dma_start(moe_w2[:, :, :, :].rearrange("p e c d -> p (e c) d"),
                         A["L2_ffn_w2"].rearrange("e (c p) d -> p (e c) d", p=P)).then_inc(S("w_exp"), 16)
            if "F1" in phases:
                sp.wait_ge(S("wq_ready"), 2)
                for i, name in enumerate(("L1_ffn_w_gate", "L1_ffn_w_up")):
                    sp.dma_start(quant_src[:, i, :].rearrange("p (c d) -> p c d", d=P),
                                 A[name].rearrange("(c p) d -> p c d", p=P)).then_inc(S("w_f1"), 16)
                sp.dma_start(quant_src[:, 2, :], A["L1_ffn_w_down"]).then_inc(S("w_f1"), 16)
            if "L2" in phases:
                sp.wait_ge(S("L1_pv"), NT)
                sp.dma_start(moe_w1.rearrange("d (e f) -> d e f", e=NE), A["L2_ffn_w1"].rearrange("e d f -> d e f")
                             ).then_inc(S("w_exp"), 16)
            if "F3" in phases:
                for n in range(2 * STAGES):
                    src = A["L3_ffn_up_weights"][n] if n < STAGES else A["L3_ffn_down_weights"][2 * STAGES - 1 - n]
                    if n >= 2:
                        wait(sp, "bf_used", n - 1)
                    else:
                        sp.wait_ge(S("wq_ready"), 5)
                    wait(sp, "bf_in", 16 * n)
                    sp.dma_start(bf_w[:, n % 2, :],
                                 src.rearrange("k i j -> (k i j)").unsqueeze(0).broadcast_to([P, 1024])
                                 ).then_inc(S("bf_in"), 16)

            if "F2" in phases:
                sp.wait_ge(S("scattered"), 16 * NT)

                def slots(j, q):
                    u = j + 2
                    if live(u, NS // 2):
                        wait(sp, "G_in", 16 * u)
                        wait(sp, "G_xt", 2 * (u - 1))
                        sp.dma_start(slot_x[:, q, :, :], slot_in[bass.ds(u * 2 * P, 2 * P), :]
                                     .rearrange("(r p) d -> p r d", p=P)).then_inc(S("G_in"), 16)
                    u = j - 1
                    if live(u, NS // 2):
                        wait(sp, "G_out", 16 * u)
                        wait(sp, "G_yo", 2 * (u + 1))
                        sp.dma_start(slot_out[bass.ds(u * 2 * P, 2 * P), :].rearrange("(r p) d -> p r d", p=P),
                                     slot_y[:, 1 - q, :, :]).then_inc(S("G_out"), 16)
                each_tile(sp, slots, lead=2, n=NS // 2)
                wait(sp, "G_hp", NS)
                sp.dma_start(open_mask[:, :].bitcast(I32),
                             A["mask_BxS2_ik0"].rearrange("b s -> (b s)").unsqueeze(0).broadcast_to([P, NT * P])
                             ).then_inc(S("open_in"), 16)
            done = {"L0": "L0_res", "F0": "F0_res", "L1": "L1_res", "F1": "F1_res", "L2": "L2_res",
                    "F2": "B_res", "L3": "L3_res", "F3": "F3_res"}[LAST_PHASE]

            def store(t, p):
                u = t - 1
                if live(u):
                    wait(sp, done, u + 1)
                    sp.dma_start(out[bass.ds(u, 1)].rearrange("u s d -> (u s) d"),
                                 tile_of(x, u)).then_inc(S("stored"), 16)
            each_tile(sp, store)
            sp.wait_ge(S("stored"), 16 * NT)
            wait(sp, "L0_o_in", 16 * NT)

        @block.gpsimd
        def _(pool):
            n_set = 0

            def const(ins):
                nonlocal n_set
                n_set += 1
                ins.then_inc(S("pool_set"), 1)

            def settle():
                pool.wait_ge(S("pool_set"), n_set)

            const(pool.memset(ident[:, :], 0.0))
            const(pool.memset(ones[:, :], 1.0))
            settle()
            const(pool.affine_select(out=ident[:, :], in_=ident[:, :], compare_op=ALU.not_equal, fill=1.0,
                                     base=0, pattern=[[-1, P]], channel_multiplier=1))
            settle()
            const(pool.tensor_copy(ident_bf[:, :], ident[:, :]))
            settle()
            const(pool.memset(vals[:, :, :], 0.0))
            const(pool.memset(nmax_parts[:, :, :, :], 0.0))
            settle()
            for b in range(2):
                const(pool.memset(vals[:, b, P:P + NH * (VW + 1):VW + 1], 1.0))
                const(pool.memset(vals[:, b, NH * VW + P:(NH + 1) * VW], 1.0))
            settle()
            assert n_set == SET_VALS
            const(pool.memset(head_rows_f, 0.0))
            settle()
            for first in (HR * half + NH // 2 * n for half in range(2) for n in range(NPART)):
                const(pool.affine_select(out=head_rows_f, in_=head_rows_f, compare_op=ALU.not_equal, fill=1.0,
                                         base=-first, pattern=[[-1, NH // 2], [0, P]], channel_multiplier=1))
                settle()
            const(pool.tensor_copy(head_rows[:, :, :], head_rows_f))
            assert n_set == SET_L0
            pool.memset(future_add[:, :], 0.0).then_inc(S("fut"), 1)
            pool.memset(future_one[:, :], 0.0).then_inc(S("fut"), 1)
            pool.wait_ge(S("fut"), 2)
            pool.affine_select(out=future_add[:, :], in_=future_add[:, :], compare_op=ALU.is_ge, fill=NEG,
                               base=0, pattern=[[-1, P]], channel_multiplier=1).then_inc(S("fut"), 1)
            pool.wait_ge(S("fut"), 3)
            pool.tensor_copy(future_bf[:, :], future_add[:, :]).then_inc(S("fut"), 1)
            pool.affine_select(out=future_one[:, :], in_=future_one[:, :], compare_op=ALU.is_ge, fill=1.0,
                               base=0, pattern=[[1, P]], channel_multiplier=-1).then_inc(S("fut"), 1)
            pool.memset(zeros[:, :], 0.0).then_inc(S("zero_set"), 1)
            pool.iota(slot_no[:, :], [[1, NS]], base=0, channel_multiplier=0,
                      allow_small_or_imprecise_dtypes=True).then_inc(S("fut"), 1)
            pool.affine_select(out=earlier[:, :], in_=ones[:, :], compare_op=ALU.is_gt, fill=0.0,
                               base=0, pattern=[[1, P]], channel_multiplier=-1).then_inc(S("fut"), 1)
            pool.iota(expert_no[:, :], [[1, NE]], base=0, channel_multiplier=0,
                      allow_small_or_imprecise_dtypes=True).then_inc(S("fut"), 1)

            def tile_copies(layer):
                def body(t, p):
                    u = t + 3
                    if live(u):
                        wait(pool, layer + "_vp", u - 1)
                        pool.tensor_copy(ctx_one[:, 1 - p, :], tile_of(contextT, u)).then_inc(S(layer + "_cs"), 1)
                    u = t + 1
                    if layer == "L3" and live(u):
                        wait(pool, "L3_pv", 4 * (u - 1))
                        pool.tensor_copy(om_one[:, 1 - p, :], tile_of(open_mask, u)).then_inc(S("L3_om"), 1)
                each_tile(pool, body, lead=3)

            def keep_ctxT(t, p):
                if live(t + 2):
                    wait(pool, "a_cs", t + 3)
                    pool.tensor_copy(tile_of(contextT, t + 2), oT[:, p, :]).then_inc(S("a_ctxT"), 1)
            each_tile(pool, keep_ctxT, lead=2)
            if "L2" in phases:
                tile_copies("L2")
            if "F3" in phases:
                pool.wait_ge(S("w_f3"), 16 * 2)
                pool.wait_ge(S("con_T"), 1)
                pool.wait_ge(S("wq_ready"), 5)
                step = 0
                for n in range(2 * STAGES):
                    up = n < STAGES
                    k = n if up else 2 * STAGES - 1 - n
                    w_n = 2 ** k
                    src, dst = n % 2, (n + 1) % 2
                    pool.wait_ge(S("bf_in"), 16 * (n + 1))
                    wv = bf_w[:, n % 2, :].rearrange("p (n s c) -> p c n s", s=w_n, c=4)
                    if up:
                        m = 2

                        def half(buf, i):
                            return buf.rearrange("p m (n two s) -> p two m n s", two=2, s=w_n)[:, i]

                        def tmp(i):
                            return bf_t[:, i, :].rearrange("p (m n s) -> p m n s", m=m, s=w_n)

                        def wgt(c):
                            return wv[:, c].unsqueeze(1).broadcast_to([P, m, HID // 2 // w_n, w_n])
                        a_in, b_in = half(bf_up[:, src], 0), half(bf_up[:, src], 1)
                        a_out, b_out = half(bf_up[:, dst], 0), half(bf_up[:, dst], 1)
                        order = (0, 1, 2, 3)
                    else:
                        src, dst = (n - STAGES) % 2, (n - STAGES + 1) % 2

                        def half(buf, i):
                            return buf.rearrange("p (n two s) -> p two n s", two=2, s=w_n)[:, i]

                        def tmp(i):
                            return bf_t[:, i, 0:HID // 2].rearrange("p (n s) -> p n s", s=w_n)

                        def wgt(c):
                            return wv[:, c]
                        a_in, b_in = half(bf_dn[:, src], 0), half(bf_dn[:, src], 1)
                        a_out, b_out = half(bf_dn[:, dst], 0), half(bf_dn[:, dst], 1)
                        order = (0, 2, 1, 3)
                    for i, (c, d) in enumerate(zip(order, (a_in, b_in, a_in, b_in))):
                        last = pool.tensor_tensor(tmp(i), d, wgt(c), ALU.mult)
                        last.then_inc(S("bf_step"), 1)
                    step += 4
                    pool.wait_ge(S("bf_step"), step)
                    pool.tensor_tensor(a_out, tmp(0), tmp(1), ALU.add).then_inc(S("bf_step"), 1)
                    pool.tensor_tensor(b_out, tmp(2), tmp(3), ALU.add).then_inc(S("bf_step"), 1)
                    step += 2
                    pool.wait_ge(S("bf_step"), step)
                    pool.sem_inc(S("bf_used"), 1)
            if "F2" in phases:
                pool.wait_ge(S("zeroed"), 16)
                pool.wait_ge(S("R_dest"), 1)
                for t in range(NT):
                    pool.indirect_dma_start(
                        out=slot_in, out_offset=bass.IndirectOffsetOnAxis(ap=dest_int[:, t:t + 1], axis=0),
                        in_=shared[:, t * P:(t + 1) * P], in_offset=None).then_inc(S("scattered"), 16)
                pool.wait_ge(S("scattered"), 16 * NT)
                pool.wait_ge(S("G_out"), 16 * (NS // 2))
                for t in range(NT):
                    pool.indirect_dma_start(
                        out=shared[:, t * P:(t + 1) * P], out_offset=None, in_=slot_out,
                        in_offset=bass.IndirectOffsetOnAxis(ap=dest_int[:, t:t + 1], axis=0)
                    ).then_inc(S(f"gathered_{t // GC}"), 16)
            if "L3" in phases:
                pool.wait_ge(S("open"), 2)
                tile_copies("L3")

        @block.scalar
        def _(act):
            def row(name):
                return A[name].unsqueeze(0).broadcast_to([P, A[name].shape[0]])
            act.dma_start(gates[:, 0:4], row("g_xattn")).then_inc(S("gates_in"), 16)
            act.dma_start(gates[:, 4:8], row("g_ffn")).then_inc(S("gates_in"), 16)
            act.dma_start(bq_row[:, :], row("L0_xattn_bq")).then_inc(S("bias_in"), 16)
            act.dma_start(bv_row[:, :], row("L0_xattn_bv")).then_inc(S("bias_in"), 16)
            act.dma_start(bo_row[:, :], row("L0_xattn_bo")).then_inc(S("bias_in"), 16)
            act.dma_start(bk_col[:, :], A["L0_xattn_bk"].unsqueeze(1)).then_inc(S("bias_in"), 16)
            act.dma_start(quant_src[:, 0, :].rearrange("p (c d) -> p c d", d=P),
                          A["L0_ffn_w1"].rearrange("(c p) d -> p c d", p=P)).then_inc(S("w_f0"), 16)
            act.dma_start(quant_src[:, 2, :], A["L0_ffn_w2"]).then_inc(S("w_f0"), 16)
            act.dma_start(l2_wq[:, :], A["L2_xattn_w_q"]).then_inc(S("w_att"), 16)
            act.dma_start(l2_wkv[:, :], A["L2_xattn_w_kv"]).then_inc(S("w_att"), 16)
            act.dma_start(l2_wo[:, :], A["L2_xattn_w_concat"]).then_inc(S("w_att"), 16)
            act.dma_start(l3_wq[:, :], A["L3_xattn_WQ"]).then_inc(S("w_att"), 16)
            act.dma_start(l3_wkv[:, 0, :], A["L3_xattn_WK"]).then_inc(S("w_att"), 16)
            act.dma_start(l3_wkv[:, 1, :], A["L3_xattn_WV"]).then_inc(S("w_att"), 16)
            act.dma_start(l3_wo[:, :], A["L3_xattn_WO"]).then_inc(S("w_att"), 16)
            act.dma_start(switch_w[:, :], A["L2_ffn_switch_w"]).then_inc(S("w_moe"), 16)
            act.dma_start(switch_b[:, :], row("L2_ffn_switch_b")).then_inc(S("w_moe"), 16)
            act.dma_start(moe_b1n[:, :], A["L2_ffn_b1"].rearrange("e (c p) -> (e c) p", p=P)).then_inc(S("w_moe"), 16)
            act.dma_start(moe_b2_rows[:, :], A["L2_ffn_b2"].rearrange("e d -> (e d)").unsqueeze(0).broadcast_to([P, NE * P])
                          ).then_inc(S("w_moe"), 16)
            act.dma_start(con_nat[:, :, :], A["L3_ffn_W_con"].rearrange("(c p) d -> p c d", p=P)).then_inc(S("w_con"), 16)
            act.dma_start(con_bias[:, 0, :], row("L3_ffn_b_con")).then_inc(S("w_con"), 16)
            act.dma_start(con_bias[:, 1, :], row("L3_ffn_down_bias")).then_inc(S("w_con"), 16)
            act.dma_start(up_row[:, :], A["L3_ffn_up_bias"].unsqueeze(0)).then_inc(S("w_con"), 16)
            act.dma_start(bf_up[:, 0, 0, :], A["L3_ffn_W_exp"]).then_inc(S("w_f3"), 16)
            act.dma_start(bf_up[:, 0, 1, :], row("L3_ffn_b_exp")).then_inc(S("w_f3"), 16)
            act.dma_start(mask_nat[:, :], A["mask_BxS2_ik0"]).then_inc(S("keep_in"), 16)

            act.wait_ge(S("gates_in"), 32)
            act.activation(tgate[:, :], gates[:, :], ACT.Tanh).then_inc(S("tgate"), 1)

            def root(n):
                act.wait_ge(S("var"), n)
                act.activation(var_a[:, :], var_b[:, :], ACT.Sqrt).then_inc(S("std"), 1)

            root(1)

            def l0a(t, p):
                if live(t + 2):
                    wait(act, "a_xt", t + 3)
                    wait(act, "a_qp", t + 1)
                    act.activation(xnT[:, p, :], bank[p][:, 0:P], ACT.Copy).then_inc(S("a_xe"), 1)
            each_tile(act, l0a, lead=2)

            def attention(layer):
                wide, own = layer != "L2", layer != "L0"
                lag, loop_from = ATT[layer]["lag"], ATT[layer]["loop_from"]

                def exponentials(u, g):
                    wait(act, layer + "_st", 4 * u + g + 1)
                    wait(act, layer + "_pv", 4 * (u - 1) + g + 1)
                    act.activation(probs[:, g, :, :].rearrange("k i q -> k (i q)"), bank[2 + g % 2][:, :],
                                   ACT.Exp).then_inc(S(layer + "_ex"), 1)

                def operand(u, p, dst, src, made, out, width):
                    wait(act, layer + made, u + 1)
                    wait(act, layer + "_st", 4 * (u - 1))
                    act.activation(dst[:, p, 0:width], src[:, :].bitcast(BF16)[:, 0:width],
                                   ACT.Copy).then_inc(S(layer + out), 1)

                def body(t, p):
                    if own and live(t + 1):
                        v = bank[7][:, 3 * P:4 * P]
                        wait(act, layer + "_vp", t + 2)
                        wait(act, layer + "_kp", up_to(t + 3, NT))
                        wait(act, layer + "_pv", 4 * t)
                        if wide:
                            act.activation(values_of(1 - p, NH)[:, 0:P], v, ACT.Copy)
                            act.activation(values_of(1 - p), v.rearrange("k (h d) -> k h d", d=DH),
                                           ACT.Copy).then_inc(S(layer + "_ve"), 1)
                        else:
                            act.activation(values_of(1 - p), over_blocks(v[:, 0:DH], NH),
                                           ACT.Copy).then_inc(S(layer + "_ve"), 1)
                    if own and live(t + 2):
                        wait(act, layer + "_xt", t + 3)
                        wait(act, layer + "_kp", t + 3)
                        wait(act, layer + "_qp", t + 1)
                        act.activation(xnT[:, p, :], bank[7][:, 0:P], ACT.Copy).then_inc(S(layer + "_xe"), 1)
                    if live(t):
                        exponentials(t, 0)
                        exponentials(t, 1)
                    u = t - lag
                    if live(u):
                        wait(act, layer + "_ot", u + 1)
                        if own:
                            wait(act, layer + "_sq", up_to(4 * (t + 2) + 2, 4 * NT))
                        wait(act, layer + "_yp", u - 1)
                        act.activation(oT[:, 1 - p, :], bank[7][:, 0:P], ACT.Copy).then_inc(S(layer + "_oe"), 1)
                    if live(t):
                        exponentials(t, 2)
                    if live(t + 2):
                        operand(t + 2, p, kT, bank[6], "_tk", "_ke", NH // 2 * P if wide else P)
                    if live(t):
                        exponentials(t, 3)
                    if live(t + 1):
                        wait(act, layer + "_mt", t + 2)
                        wait(act, layer + "_st", 4 * t)
                        act.activation(nmaxT[:, 1 - p, :], bank[7][:, :].bitcast(BF16)[:, 0:P],
                                       ACT.Copy).then_inc(S(layer + "_me"), 1)
                    if live(t + 2):
                        operand(t + 2, p, qT, bank[5], "_tq", "_qe", NH // 2 * P)
                each_tile(act, body, lead=2, tail=lag, loop_from=loop_from)

            attention("L0")

            def bit_ffn(layer, gated):
                def body(t, p):
                    if live(t + 2):
                        wait(act, layer + "_xt", t + 3)
                        wait(act, layer + "_hp", t + 1)
                        act.activation(xqT_bf[:, p, :], bank[5][:, :].bitcast(BF16)[:, 0:P],
                                       ACT.Copy).then_inc(S(layer + "_xe"), 1)
                    if live(t + 2):
                        wait(act, layer + "_hp", t + 3)
                        wait(act, layer + "_hq", t + 1)
                        act.activation(hid[:, p, :], bank[2 * p][:, :], ACT.Silu if gated else ACT.Gelu,
                                       scale=small[:, p, 3:4]).then_inc(S(layer + "_ge"), 1)
                    if live(t + 1):
                        wait(act, layer + "_ht", t + 2)
                        wait(act, layer + "_yp", t)
                        act.activation(hidT_bf[:, 1 - p, :], bank[4][:, :].bitcast(BF16)[:, 0:HID],
                                       ACT.Copy).then_inc(S(layer + "_he"), 1)
                each_tile(act, body, lead=2)

            if "F0" in phases:
                root(2)
                bit_ffn("F0", False)
            if "L1" in phases:
                root(3)

                def l1(t, p):
                    if live(t + 3):
                        wait(act, "L1_xt", t + 4)
                        wait(act, "L1_sp", t + 2)
                        act.activation(xnT[:, 1 - p, :], bank[1 - p][:, 0:P], ACT.Copy).then_inc(S("L1_xe"), 1)
                    if live(t + 1):
                        wait(act, "L1_nm", t + 2)
                        wait(act, "L1_tp", t)
                        wait(act, "L1_r", 2 * t)
                        act.activation(hid2[:, 1 - p, 0:P], hid[:, 1 - p, 0:P], ACT.Exp,
                                       bias=small[:, 1 - p, 0:1],
                                       accum_out=small[:, 1 - p, 1:2]).then_inc(S("L1_ex"), 1)
                    if live(t):
                        wait(act, "L1_tp", t + 1)
                        wait(act, "L1_pv", t - 1)
                        act.activation(oT[:, p, :], bank[4 + p][:, 0:P], ACT.Copy).then_inc(S("L1_te"), 1)
                each_tile(act, l1, lead=3)
            if "F1" in phases:
                root(4)
                bit_ffn("F1", True)
            if "L2" in phases:
                root(5)
                attention("L2")
            if "F2" in phases:
                root(6)

                def route(t, p):
                    if live(t + 1):
                        wait(act, "R_xt", t + 2)
                        wait(act, "R_lp", t)
                        act.activation(xnT[:, 1 - p, :], bank[1 - p][:, 0:P], ACT.Copy).then_inc(S("R_xe"), 1)
                each_tile(act, route)
                act.wait_ge(S("R_sub"), 1)
                act.activation(route_a[:, :, :], route_b[:, :, :], ACT.Exp).then_inc(S("R_exp"), 1)

                act.wait_ge(S("R_slots"), 1)

                def slots(j, q):
                    for p in range(2):
                        t = 2 * j + p
                        if live(t + 2, NS):
                            wait(act, "G_xt", t + 3)
                            wait(act, "G_hp", t + 1)
                            act.activation(xnT[:, p, :], bank[(4, 7)[p]][:, 0:P], ACT.Copy).then_inc(S("G_xe"), 1)
                        if live(t, NS):
                            e = act.value_load(expert_int[0:1, bass.ds(t, 1)], min_val=0, max_val=NE - 1)
                            wait(act, "G_ht", t + 1)
                            wait(act, "G_yp", t - 1)
                            for c in range(NC):
                                m = act.activation(hid2[:, p, c * P:(c + 1) * P], bank[2 + p][:, c * P:(c + 1) * P],
                                                   ACT.Gelu_apprx_tanh, bias=moe_b1[:, bass.ds(e * NC + c, 1)])
                            m.then_inc(S("G_ge"), 1)
                act.wait_ge(S("R_b1"), 1)
                each_tile(act, slots, n=NS // 2)
            if "L3" in phases:
                root(7)
                attention("L3")
            if "F3" in phases:
                root(8)
                act.wait_ge(S("f3_bias"), 1)

                def f3(t, p):
                    if live(t + 2):
                        wait(act, "F3_xt", t + 3)
                        wait(act, "F3_hp", t + 1)
                        act.activation(xnT[:, p, :], bank[4 + p][:, 0:P], ACT.Copy).then_inc(S("F3_xe"), 1)
                    if live(t + 1):
                        wait(act, "F3_hp", t + 2)
                        wait(act, "F3_yp", t)
                        for c in range(NC):
                            g = act.activation(hid[:, 1 - p, c * P:(c + 1) * P], bank[1 - p][:, c * P:(c + 1) * P],
                                               ACT.Gelu, bias=up_bias[:, c:c + 1])
                        g.then_inc(S("F3_ge"), 1)
                each_tile(act, f3, lead=2)

        @block.tensor
        def _(pe):
            pe.wait_ge(S("pool_set"), SET_IDENT)
            pe.wait_ge(S("w_l0"), 64)
            for i in range(4):
                m = pe.transpose(bank[7][:, i * P:(i + 1) * P], l0_nat[:, i, :], ident[:, :])
            m.then_inc(S("wT"), 1)
            pe.wait_ge(S("w_con"), 64)
            for i in range(NC):
                m = pe.transpose(bank[6][:, i * P:(i + 1) * P], con_nat[:, i, :], ident[:, :])
            m.then_inc(S("wT"), 1)
            pe.wait_ge(S("w_moe"), 16 * 4)
            pe.transpose(bank[5][:, 0:NE * NC], moe_b1n[:, :], ident[0:NE * NC, 0:NE * NC]).then_inc(S("wT"), 1)
            pe.wait_ge(S("mask_f"), 1)
            pe.transpose(bank[5][:, P:P + NT], mask_f[:, :], ident[0:NT, 0:NT]).then_inc(S("wT"), 1)
            pe.wait_ge(S("wT_out"), 1)

            def l0a(t, p):
                if live(t + 2):
                    wait(pe, "a_xn", t + 3)
                    wait(pe, "a_xe", t + 1)
                    wait(pe, "a_cs", t + 1)
                    pe.transpose(bank[p][:, 0:P], xn[:, p, :], ident[:, :])
                    pe.transpose(bank[4 + p][:, 0:P], ctx_one[:, p, :], ident[:, :]).then_inc(S("a_xt"), 1)
                if live(t + 1):
                    o = bank[3 - p]
                    wait(pe, "a_xe", t + 2)
                    wait(pe, "a_cs", t + 2)
                    wait(pe, "a_qv", 2 * t)
                    pe.matmul(o[:, 0:P], xnT[:, 1 - p, :], l0_T[:, 0, :], start=True, stop=True)
                    pe.matmul(o[:, P:2 * P], oT[:, 1 - p, :], l0_T[:, 2, :], start=True,
                              stop=True).then_inc(S("a_qp"), 1)
            each_tile(pe, l0a, lead=2)

            def attention(layer):
                wide, own = layer != "L2", layer != "L0"
                lag, loop_from = ATT[layer]["lag"], ATT[layer]["loop_from"]
                pe.wait_ge(S("pool_set"), SET_L0)
                if own:
                    pe.wait_ge(S("w_att"), 16 * 7)
                    pe.wait_ge(S("fut"), 8)
                else:
                    pe.wait_ge(S("a_ctxT"), NT)
                wq, wo = {"L0": (None, l0_T[:, 3, :]), "L2": (l2_wq, l2_wo[:, :]), "L3": (l3_wq, l3_wo[:, :])}[layer]

                def first_projections(t, p):
                    wait(pe, layer + "_me", up_to(t + 1, NT))
                    if live(t + 1):
                        wait(pe, layer + "_sk", 4 * (t + 1) + 2)
                        wait(pe, layer + "_sq", 4 * (t + 1) + 2)
                    if own and live(t + 1):
                        wv = l3_wkv[:, 1, :] if wide else l2_wkv[:, DH:2 * DH]
                        wait(pe, layer + "_cs", t + 2)
                        pe.matmul(bank[7][:, 3 * P:3 * P + wv.shape[1]], ctx_one[:, 1 - p, :], wv, start=True,
                                  stop=True).then_inc(S(layer + "_vp"), 1)
                    if own and live(t + 2):
                        wait(pe, layer + "_xn", t + 3)
                        pe.transpose(bank[7][:, 0:P], xn[:, p, :], ident[:, :]).then_inc(S(layer + "_xt"), 1)
                        wk = l3_wkv[:, 0, :] if wide else l2_wkv[:, 0:DH]
                        wait(pe, layer + "_cs", t + 3)
                        pe.matmul(bank[7][:, 2 * P:2 * P + wk.shape[1]], ctx_one[:, p, :], wk, start=True,
                                  stop=True).then_inc(S(layer + "_kp"), 1)
                    if not own and live(t + 2):
                        pe.matmul(bank[7][:, 2 * P:3 * P], l0_T[:, 1, :], tile_of(contextT, t + 2),
                                  start=True, stop=True).then_inc(S(layer + "_kp"), 1)

                def queries_and_output(t, p):
                    if own:
                        wait(pe, layer + "_ve", up_to(t + 2, NT))
                        wait(pe, layer + "_xe", up_to(t + 3, NT))
                    wait(pe, layer + "_sk", up_to(4 * (t + 2) + 2, 4 * NT))
                    if own and live(t + 2):
                        pe.matmul(bank[7][:, P:2 * P], xnT[:, p, :], wq[:, :],
                                  start=True, stop=True).then_inc(S(layer + "_qp"), 1)
                    u = t - lag
                    if live(u):
                        wait(pe, layer + ("_on" if own else "_os"), u + 1)
                        wait(pe, layer + "_me", up_to(t + 1, NT))
                        wait(pe, layer + "_res", u)
                        pe.transpose(bank[7][:, 0:P], (o_tok if own else o_back)[:, 1 - p, :], ident[:, :]
                                     ).then_inc(S(layer + "_ot"), 1)

                def output_projected(t, p):
                    if own:
                        wait(pe, layer + "_sq", up_to(4 * (t + 2) + 2, 4 * NT))
                    wait(pe, layer + "_oe", t - lag + 1)
                    pe.matmul(bank[7][:, 3 * P:4 * P], oT[:, 1 - p, :], wo, start=True,
                              stop=True).then_inc(S(layer + "_yp"), 1)

                def maxima_transposed(t, p):
                    wait(pe, layer + "_na", 4 * (t + 2))
                    wait(pe, layer + "_sk", up_to(4 * (t + 2) + 2, 4 * NT))
                    if own:
                        wait(pe, layer + "_sq", up_to(4 * (t + 2) + 2, 4 * NT))
                    wait(pe, layer + "_res", t - lag + 1)
                    pe.transpose(bank[7][:, :].bitcast(BF16)[:, 0:P],
                                 nmax_parts[:, 1 - p, :, :].rearrange("q n r -> q (n r)"),
                                 ident_bf[:, :]).then_inc(S(layer + "_mt"), 1)

                def operand(u, p, side):
                    b, split, read, made = ((bank[5], "_sq", "_qe", "_tq"), (bank[6], "_sk", "_ke", "_tk"))[side]
                    wait(pe, layer + split, 4 * (u + 1))
                    wait(pe, layer + read, u)
                    for i in range(1 if side == 1 and not wide else NH // 2):
                        m = pe.transpose(b[:, :].bitcast(BF16)[:, i * P:(i + 1) * P],
                                         parts[:, side, p, 2 * i:2 * i + 2, :].rearrange("q h r -> q (h r)"),
                                         ident_bf[:, :])
                    m.then_inc(S(layer + made), 1)

                def rows_of(buf, p, h, shared_by_all=False):
                    first = HR * (h % 2)
                    b = 0 if shared_by_all else h // 2
                    return buf[first:first + HR, p, b * P:(b + 1) * P]

                def scores(u, p, g):
                    if g == 0:
                        wait(pe, layer + "_ke", u + 1)
                        wait(pe, layer + "_qe", u + 1)
                    wait(pe, layer + "_mx", 4 * u + g - 1)
                    if layer == "L3":
                        pe.matmul(bank[g % 2][:, :], ident_bf[:, :], over_blocks(future_bf[:, :], HG),
                                  start=True, stop=False)
                    for i in range(HG):
                        h = head(g, i)
                        m = pe.matmul(bank[g % 2][:, i * P:(i + 1) * P], rows_of(qT, p, h),
                                      rows_of(kT, p, h, not wide), start=(layer != "L3"),
                                      stop=(layer != "L3" or i == HG - 1))
                    m.then_inc(S(layer + "_sp"), 1)

                def scores_by_key(u, p, g):
                    if g == 0:
                        wait(pe, layer + "_me", u + 1)
                    wait(pe, layer + "_ex", 4 * u + g - 1)
                    if layer == "L3":
                        pe.matmul(bank[2 + g % 2][:, :], future_bf[:, :], over_blocks(ident_bf[:, :], HG),
                                  start=True, stop=False)
                    for i in range(HG):
                        h, (half, n) = head(g, i), place(g, i)
                        r = slice(HR * half, HR * (half + 1))
                        o = bank[2 + g % 2][:, i * P:(i + 1) * P]
                        pe.matmul(o, head_rows[r, n, :], nmaxT[r, p, :], start=(layer != "L3"), stop=False)
                        m = pe.matmul(o, rows_of(kT, p, h, not wide), rows_of(qT, p, h), start=False,
                                      stop=(layer != "L3" or i == HG - 1))
                    m.then_inc(S(layer + "_st"), 1)

                def weighted_values(u, p, g):
                    if g == 0:
                        wait(pe, layer + "_on", u)
                        if own:
                            wait(pe, layer + "_ve", u + 1)
                        else:
                            wait(pe, "L0_v_in", 16 * (u + 1))
                        if layer == "L3":
                            wait(pe, "L3_om", u + 1)
                            pe.matmul(bank[4][:, 0:VW], om_one[:, p, :], values_of(p, NH), start=True,
                                      stop=False)
                    wait(pe, layer + "_ex", 4 * u + g + 1)
                    for i in range(HG):
                        m = pe.matmul(bank[4][:, 0:VW], probs[:, g, i, :], values_of(p, head(g, i)),
                                      start=(layer != "L3" and g == 0 and i == 0),
                                      stop=(g == NG - 1 and i == HG - 1))
                    m.then_inc(S(layer + "_pv"), 1)

                def body(t, p):
                    first_projections(t, p)
                    if live(t):
                        scores_by_key(t, p, 0)
                        scores_by_key(t, p, 1)
                    if live(t + 1):
                        scores(t + 1, 1 - p, 0)
                        scores(t + 1, 1 - p, 1)
                    if own:
                        queries_and_output(t, p)
                    if live(t):
                        weighted_values(t, p, 0)
                    if not own:
                        queries_and_output(t, p)
                    if live(t + 1):
                        scores(t + 1, 1 - p, 2)
                    if live(t):
                        scores_by_key(t, p, 2)
                    if live(t + 1):
                        scores(t + 1, 1 - p, 3)
                    if live(t + 2):
                        operand(t + 2, p, 1)
                    if live(t):
                        weighted_values(t, p, 1)
                    if live(t - lag):
                        output_projected(t, p)
                    if live(t):
                        scores_by_key(t, p, 3)
                    if live(t + 2):
                        operand(t + 2, p, 0)
                    if live(t):
                        weighted_values(t, p, 2)
                    if live(t + 1):
                        maxima_transposed(t, p)
                    if live(t):
                        weighted_values(t, p, 3)
                each_tile(pe, body, lead=2, tail=lag, loop_from=loop_from)

            attention("L0")

            def bit_ffn(layer, gated):
                for i in (0, 1, 2):
                    if i == 1 and not gated:
                        continue
                    n = {("F0", 0): 1, ("F0", 2): 2, ("F1", 0): 3, ("F1", 1): 4, ("F1", 2): 5}[layer, i]
                    pe.wait_ge(S("wq_ready"), n)
                    for c in range(NC):
                        m = pe.transpose(bank[i][:, :].bitcast(BF16)[:, c * P:(c + 1) * P],
                                         quant_bf[:, i, c * P:(c + 1) * P], ident_bf[:, :])
                    m.then_inc(S("wqT"), 1)
                pe.wait_ge(S("wqT_out"), 2 if not gated else 5)

                def body(t, p):
                    if live(t + 2):
                        wait(pe, layer + "_xn", t + 3)
                        wait(pe, layer + "_xe", t + 2)
                        pe.transpose(bank[5][:, :].bitcast(BF16)[:, 0:P], xq_bf[:, p, :],
                                     ident_bf[:, :]).then_inc(S(layer + "_xt"), 1)
                    if live(t):
                        wait(pe, layer + "_he", t + 1)
                        wait(pe, layer + "_res", t - 1)
                        for c in range(NC):
                            m = pe.matmul(bank[6 + p][:, 0:P], hidT_bf[:, p, c * P:(c + 1) * P],
                                          ffn_wT[:, 2, c * P:(c + 1) * P], start=(c == 0), stop=(c == NC - 1))
                        m.then_inc(S(layer + "_yp"), 1)
                    if live(t + 2):
                        wait(pe, layer + "_xe", t + 3)
                        wait(pe, layer + ("_hm" if gated else "_ge"), t + 1)
                        m = pe.matmul(bank[2 * p][:, :], xqT_bf[:, p, :], ffn_wT[:, 0, :], start=True, stop=True)
                        if gated:
                            m = pe.matmul(bank[2 * p + 1][:, :], xqT_bf[:, p, :], ffn_wT[:, 1, :],
                                          start=True, stop=True)
                        m.then_inc(S(layer + "_hp"), 1)
                    if live(t + 1):
                        wait(pe, layer + "_hq", t + 2)
                        wait(pe, layer + "_he", t + 1)
                        for c in range(NC):
                            m = pe.transpose(bank[4][:, :].bitcast(BF16)[:, c * P:(c + 1) * P],
                                             hid_bf[:, 1 - p, c * P:(c + 1) * P], ident_bf[:, :])
                        m.then_inc(S(layer + "_ht"), 1)
                each_tile(pe, body, lead=2)

            if "F0" in phases:
                pe.wait_ge(S("wsum"), 1)
                pe.matmul(bank[7][:, 0:3], mean_mat[:, :], quant_sum[:, 0:3], start=True,
                          stop=True).then_inc(S("wmean"), 1)
                bit_ffn("F0", False)
            if "L1" in phases:
                def l1(t, p):
                    if live(t + 3):
                        wait(pe, "L1_xn", t + 4)
                        wait(pe, "L1_xe", t + 2)
                        pe.transpose(bank[1 - p][:, 0:P], xn[:, 1 - p, :], ident[:, :]).then_inc(S("L1_xt"), 1)
                    if live(t + 2):
                        wait(pe, "L1_xe", t + 3)
                        wait(pe, "L1_sm", t + 1)
                        pe.matmul(bank[2 + p][:, 0:P], xnT[:, p, :], tile_of(contextT, t + 2), start=True,
                                  stop=True).then_inc(S("L1_sp"), 1)
                    if live(t):
                        wait(pe, "L1_ex", t + 1)
                        wait(pe, "L1_te", t - 1)
                        pe.transpose(bank[4 + p][:, 0:P], hid2[:, p, 0:P], ident[:, :]).then_inc(S("L1_tp"), 1)
                    if live(t - 1):
                        wait(pe, "L1_te", t)
                        wait(pe, "L1_res", t - 2)
                        pe.matmul(bank[7 - p][:, 0:P], oT[:, 1 - p, :], tile_of(context, t - 1), start=True,
                                  stop=True).then_inc(S("L1_pv"), 1)
                each_tile(pe, l1, lead=3)
            if "F1" in phases:
                pe.wait_ge(S("wsum"), 2)
                pe.matmul(bank[7][:, 0:3], mean_mat[:, :], quant_sum[:, 0:3], start=True,
                          stop=True).then_inc(S("wmean"), 1)
                bit_ffn("F1", True)
            if "L2" in phases:
                attention("L2")
            if "F2" in phases:
                def route(t, p):
                    if live(t + 1):
                        wait(pe, "R_xn", t + 2)
                        wait(pe, "R_xe", t)
                        pe.transpose(bank[1 - p][:, 0:P], xn[:, 1 - p, :], ident[:, :]).then_inc(S("R_xt"), 1)
                    if live(t):
                        wait(pe, "R_xe", t + 1)
                        wait(pe, "R_lg", t - 1)
                        pe.matmul(bank[2 + p][:, 0:NE], xnT[:, p, :], switch_w[:, :], start=True,
                                  stop=True).then_inc(S("R_lp"), 1)
                each_tile(pe, route)

                pe.wait_ge(S("R_hot"), 1)
                hot = route_b[:, :, :].rearrange("p t e -> p (t e)")
                pe.matmul(bank[0][:, 0:NT * NE], earlier[:, :], hot, start=True, stop=True)
                pe.matmul(bank[1][:, 0:NT * NE], ones[:, :], hot, start=True, stop=True).then_inc(S("R_rank"), 1)

                w2 = moe_w2[:, :, :, :].rearrange("f e c d -> f (e c d)")

                def slots(j, q):
                    for p in range(2):
                        t = 2 * j + p
                        if live(t + 2, NS):
                            if p == 0:
                                wait(pe, "G_in", 16 * (j + 2))
                            wait(pe, "G_xe", t + 1)
                            pe.transpose(bank[(4, 7)[p]][:, 0:P], slot_x[:, 1 - q, p, :], ident[:, :]
                                         ).then_inc(S("G_xt"), 1)
                        if live(t + 1, NS):
                            e = pe.value_load(expert_int[0:1, bass.ds(t + 1, 1)], min_val=0, max_val=NE - 1)
                            wait(pe, "G_xe", t + 2)
                            wait(pe, "G_hs", t)
                            pe.matmul(bank[1 - p][:, :], xnT[:, 1 - p, :], moe_w1[:, bass.ds(e * HID, HID)],
                                      start=True, stop=True).then_inc(S("G_hp"), 1)
                        if live(t, NS):
                            wait(pe, "G_hs", t + 1)
                            wait(pe, "G_ge", t - 1)
                            for c in range(NC):
                                m = pe.transpose(bank[2 + p][:, c * P:(c + 1) * P], hid[:, p, c * P:(c + 1) * P],
                                                 ident[:, :])
                            m.then_inc(S("G_ht"), 1)
                        if live(t - 1, NS):
                            e = pe.value_load(expert_int[0:1, bass.ds(t - 1, 1)], min_val=0, max_val=NE - 1)
                            wait(pe, "G_ge", t)
                            wait(pe, "G_yo", t - 2)
                            for c in range(NC):
                                m = pe.matmul(bank[5 + 1 - p][:, 0:P], hid2[:, 1 - p, c * P:(c + 1) * P],
                                              w2[:, bass.ds(e * HID + c * P, P)], start=(c == 0), stop=(c == NC - 1))
                            m.then_inc(S("G_yp"), 1)
                pe.wait_ge(S("w_exp"), 32)
                pe.wait_ge(S("R_slots"), 1)
                each_tile(pe, slots, n=NS // 2)
            if "L3" in phases:
                attention("L3")
            if "F3" in phases:
                pe.wait_ge(S("bf_used"), 2 * STAGES)
                for c in range(NC):
                    m = pe.transpose(bank[6][:, c * P:(c + 1) * P], bf_dn[:, STAGES % 2, c * P:(c + 1) * P],
                                     ident[:, :])
                m.then_inc(S("wT"), 1)
                pe.wait_ge(S("up_row"), 1)
                for c in range(NC):
                    m = pe.matmul(bank[5][:, c:c + 1], up_row[0:1, c * P:(c + 1) * P], ones[0:1, 0:1],
                                  start=True, stop=True)
                m.then_inc(S("wT"), 1)
                pe.wait_ge(S("f3_bias"), 1)

                def f3(t, p):
                    if live(t + 2):
                        wait(pe, "F3_xn", t + 3)
                        wait(pe, "F3_xe", t + 1)
                        pe.transpose(bank[4 + p][:, 0:P], xn[:, p, :], ident[:, :]).then_inc(S("F3_xt"), 1)
                    if live(t + 1):
                        wait(pe, "F3_xe", t + 2)
                        wait(pe, "F3_ge", t)
                        for c in range(NC):
                            m = pe.matmul(bank[1 - p][:, c * P:(c + 1) * P],
                                          bf_up[:, STAGES % 2, 0, c * P:(c + 1) * P], xnT[:, 1 - p, :],
                                          start=True, stop=True)
                        m.then_inc(S("F3_hp"), 1)
                    if live(t):
                        wait(pe, "F3_ge", t + 1)
                        wait(pe, "F3_res", t - 1)
                        for c in range(NC):
                            m = pe.matmul(bank[2 + p][:, 0:P], hid[:, p, c * P:(c + 1) * P], w_down[:, c, :],
                                          start=(c == 0), stop=(c == NC - 1))
                        m.then_inc(S("F3_yp"), 1)
                each_tile(pe, f3, lead=2)

        @block.vector
        def _(dve):
            n_link = 0

            def link(ins):
                nonlocal n_link
                n_link += 1
                ins.then_inc(S("dve_link"), 1)
                dve.wait_ge(S("dve_link"), n_link)

            def count(ins, name, n=1):
                ins.then_inc(S(name), n)

            def tile_stats(u):
                if isinstance(u, int):
                    dve.bn_stats(stats[:, u, :], x[:, u * P:(u + 1) * P]).then_inc(S("stats"), 1)
                    return
                dve.bn_stats(stats[:, bass.ds(u, 1), :].rearrange("p u s -> p (u s)"), tile_of(x, u)
                             ).then_inc(S("stats"), 1)

            def norm_stats(n, scale_by_keep=False):
                dve.wait_ge(S("stats"), NT * n)
                link(dve.tensor_tensor(var_a[:, :], stats[:, :, 2], stats[:, :, 5], ALU.add))
                link(dve.tensor_tensor(var_b[:, :], stats[:, :, 1], stats[:, :, 4], ALU.subtract))
                link(dve.scalar_tensor_tensor(out=var_b[:, :], in0=var_b[:, :], scalar=0.25, in1=var_b[:, :],
                                              op0=ALU.mult, op1=ALU.mult))
                link(dve.scalar_tensor_tensor(out=var_b[:, :], in0=var_a[:, :], scalar=1.0 / P, in1=var_b[:, :],
                                              op0=ALU.mult, op1=ALU.add))
                link(dve.tensor_scalar(var_b[:, :], var_b[:, :], EPS, None, ALU.add))
                dve.sem_inc(S("var"), 1)
                link(dve.tensor_tensor(mean[:, :], stats[:, :, 1], stats[:, :, 4], ALU.add))
                link(dve.tensor_scalar(mean[:, :], mean[:, :], 0.5, None, ALU.mult))
                dve.wait_ge(S("std"), n)
                link(dve.reciprocal(rstd[:, :], var_a[:, :]))
                if scale_by_keep:
                    link(dve.tensor_tensor(rstd[:, :], rstd[:, :], keep[:, :], ALU.mult))

            def normed(dst, u, name):
                dve.tensor_scalar(dst, tile_of(x, u), column(mean, u), column(rstd, u), ALU.subtract,
                                  ALU.mult).then_inc(S(name), 1)

            dve.wait_ge(S("pool_set"), 2)
            dve.memset(mean_mat[:, :], 1.0 / (P * HID)).then_inc(S("mean_mat"), 1)
            link(dve.memset(no_bias[:, :], 0.0))
            dve.wait_ge(S("wT"), 1)
            link(dve.tensor_copy(l0_T[:, :, :].rearrange("i n o -> i (n o)"), bank[7][:, :]))
            dve.wait_ge(S("x_in"), 64)
            for u in range(NT):
                tile_stats(u)
            norm_stats(1)
            dve.wait_ge(S("wT"), 2)
            dve.tensor_copy(bf_dn[:, 0, :], bank[6][:, :]).then_inc(S("con_T"), 1)
            dve.wait_ge(S("keep_in"), 16)
            dve.tensor_copy(mask_f[:, :], mask_nat[:, :]).then_inc(S("mask_f"), 1)
            dve.wait_ge(S("wT"), 4)
            dve.tensor_copy(moe_b1[:, :], bank[5][:, 0:NE * NC]).then_inc(S("R_b1"), 1)
            link(dve.tensor_scalar(keep[:, :], bank[5][:, P:P + NT], 0.0, None, ALU.is_equal))
            dve.sem_inc(S("wT_out"), 1)
            dve.wait_ge(S("bias_in"), 64)
            dve.wait_ge(S("tgate"), 1)
            link(dve.tensor_scalar(bo_row[:, :], bo_row[:, :], tgate[:, 0:1], None, ALU.mult))

            dve.wait_ge(S("ctx_in"), 64)

            def l0a(t, p):
                if live(t + 3):
                    wait(dve, "a_xt", t + 2)
                    dve.tensor_copy(ctx_one[:, 1 - p, :], tile_of(context, t + 3)).then_inc(S("a_cc"), 1)
                    wait(dve, "a_cc", t + 4)
                    normed(xn[:, 1 - p, :], t + 3, "a_xn")
                if live(t):
                    wait(dve, "a_qp", t + 1)
                    for stage, half, bias in ((stage_q, 0, bq_row), (stage_v, 1, bv_row)):
                        dve.tensor_tensor(stage[:, bass.ds(t, 1), :].rearrange("p u d -> p (u d)"),
                                          bank[2 + p][:, half * P:(half + 1) * P], bias[:, :],
                                          ALU.add).then_inc(S("a_qv"), 1)
                if live(t + 2):
                    wait(dve, "a_xt", t + 3)
                    wait(dve, "a_qp", t + 1)
                    wait(dve, "a_ctxT", t + 1)
                    dve.tensor_copy(oT[:, p, :], bank[4 + p][:, 0:P]).then_inc(S("a_cs"), 1)
            each_tile(dve, l0a, lead=3)

            def attention(layer):
                wide, own = layer != "L2", layer != "L0"
                lag, loop_from = ATT[layer]["lag"], ATT[layer]["loop_from"]
                gate = ATT[layer]["gate"]

                def side_of(u, p, side):
                    if side == 0:
                        src = bank[7][:, P:2 * P] if own else q_rows[:, p, :]
                        return dict(src=src.rearrange("p (h d) -> p h d", d=DH), heads=NH, scalar=SCORE_SCALE,
                                    op=ALU.mult, **BLOCKS["q"])
                    src = bank[7][:, 2 * P:3 * P].rearrange("p (h d) -> p h d", d=DH) if wide else \
                        over_blocks(bank[7][:, 2 * P:2 * P + DH], 2)
                    return dict(src=src, heads=NH if wide else 2, scalar=(no_bias if own else bk_col)[:, 0:1],
                                op=ALU.add, **BLOCKS["k"])

                def in_parts(u, p, side, step):
                    w = side_of(u, p, side)
                    name, done = layer + ("_sq", "_sk")[side], 4 * u
                    dst = parts[:, side, p, 0:w["heads"], :]
                    r = rest[:, p, side, 0:w["heads"] * DH].rearrange("p (h d) -> p h d", d=DH)
                    high, middle, low = w["high"][0], w["middle"][0], w["low"][0]
                    if step == 0:
                        if side == 1 or own:
                            wait(dve, layer + ("_qp", "_kp")[side], u + 1)
                            if own:
                                wait(dve, layer + ("_ot", "_xe")[side], (u - 2, u + 1)[side])
                        else:
                            wait(dve, "L0_q_in", 16 * (u + 1))
                        wait(dve, layer + ("_tq", "_tk")[side], u - 1)
                        dve.tensor_scalar(blocks_of(dst, *w["high"]),
                                          w["src"].unsqueeze(2).broadcast_to([P, w["heads"], 3, DH]),
                                          w["scalar"], None, w["op"]).then_inc(S(name), 1)
                        wait(dve, name, done + 1)
                        dve.scalar_tensor_tensor(out=r, in0=w["src"], scalar=w["scalar"],
                                                 in1=dst[:, :, high * DH:(high + 1) * DH], op0=w["op"],
                                                 op1=ALU.subtract).then_inc(S(name), 1)
                    else:
                        wait(dve, name, done + 2)
                        dve.tensor_copy(blocks_of(dst, *w["middle"]),
                                        r.unsqueeze(2).broadcast_to([P, w["heads"], 2, DH])).then_inc(S(name), 1)
                        wait(dve, name, done + 3)
                        dve.tensor_tensor(dst[:, :, low * DH:(low + 1) * DH], r,
                                          dst[:, :, middle * DH:(middle + 1) * DH], ALU.subtract
                                          ).then_inc(S(name), 1)

                def maxima(t, p, g):
                    wait(dve, layer + "_sp", 4 * (t + 1) + g + 1)
                    half, n = place(g)
                    dve.tensor_reduce(nmax[:, 1 - p, 0, half, n:n + HG],
                                      bank[g % 2][:, :].rearrange("q (i k) -> q i k", i=HG), AX.X, ALU.max,
                                      negate=True).then_inc(S(layer + "_mx"), 1)

                def maxima_in_parts(t, p):
                    NA, done = layer + "_na", 4 * (t + 1)
                    whole, left = nmax[:, 1 - p, 0, :, :], nmax[:, 1 - p, 1, :, :]
                    part = [nmax_parts[:, 1 - p, :, NH // 2 * n:NH // 2 * (n + 1)] for n in range(NPART)]
                    wait(dve, layer + "_mx", 4 * (t + 2))
                    wait(dve, layer + "_mt", t)
                    dve.tensor_copy(part[0], whole).then_inc(S(NA), 1)
                    wait(dve, NA, done + 1)
                    dve.tensor_tensor(left, whole, part[0], ALU.subtract).then_inc(S(NA), 1)
                    wait(dve, NA, done + 2)
                    dve.tensor_copy(part[1], left).then_inc(S(NA), 1)
                    wait(dve, NA, done + 3)
                    dve.tensor_tensor(part[2], left, part[1],
                                      ALU.subtract).then_inc(S(NA), 1)

                def body(t, p):
                    u = t - lag
                    if not own and live(u):
                        wait(dve, "L0_o_in", 16 * (u + 1))
                        wait(dve, "L0_ot", u - 1)
                        dve.tensor_copy(o_back[:, 1 - p, :], tile_of(shared, u)).then_inc(S("L0_os"), 1)
                        dve.tensor_tensor(tile_of(x, u), tile_of(x, u), bo_row[:, :], ALU.add).then_inc(S("c_b"), 1)
                    if live(t + 2):
                        in_parts(t + 2, p, 1, 0)
                    if live(t + 1):
                        maxima(t, p, 0)
                        maxima(t, p, 1)
                    if live(t + 2):
                        in_parts(t + 2, p, 1, 1)
                        in_parts(t + 2, p, 0, 0)
                    if live(t + 1):
                        maxima(t, p, 2)
                    if live(t + 2):
                        in_parts(t + 2, p, 0, 1)
                    if live(t + 1):
                        maxima(t, p, 3)
                        maxima_in_parts(t, p)
                    if live(u):
                        if not own:
                            wait(dve, "c_b", u + 1)
                        wait(dve, layer + "_yp", u + 1)
                        dve.scalar_tensor_tensor(out=tile_of(x, u), in0=bank[7][:, 3 * P:4 * P],
                                                 scalar=tgate[:, gate:gate + 1], in1=tile_of(x, u),
                                                 op0=ALU.mult, op1=ALU.add).then_inc(S(layer + "_res"), 1)
                    if own and live(t + 3):
                        wait(dve, layer + "_xt", t + 2)
                        normed(xn[:, 1 - p, :], t + 3, layer + "_xn")
                    if live(u):
                        wait(dve, layer + "_res", u + 1)
                        tile_stats(u)
                    if live(t):
                        wait(dve, layer + "_pv", 4 * (t + 1))
                        dve.reciprocal(o_inv[:, p, :], bank[4][:, P:VW]).then_inc(S(layer + "_oi"), 1)
                        wait(dve, layer + "_oi", t + 1)
                        if own:
                            wait(dve, layer + "_ot", t - 1)
                        else:
                            wait(dve, "L0_o_out", 16 * (t - 1))
                        dve.tensor_tensor(o_tok[:, p, :].rearrange("q (h d) -> q h d", d=DH),
                                          bank[4][:, 0:P].rearrange("q (h d) -> q h d", d=DH),
                                          o_inv[:, p, :].unsqueeze(2).broadcast_to([P, NH, DH]),
                                          ALU.mult).then_inc(S(layer + "_on"), 1)
                dve.wait_ge(S("pool_set"), SET_L0)
                link(dve.memset(parts.rearrange("p s b h r -> p (s b h) r")[:, :, 6 * DH:HR], 0.0))
                each_tile(dve, body, lead=3, tail=lag, loop_from=loop_from)

            attention("L0")

            def quantised_weights(which, n_sum):
                for i in which:
                    link(dve.tensor_reduce(quant_sum[:, i:i + 1], quant_src[:, i, :], AX.X, ALU.add,
                                           apply_absolute_value=True))
                dve.sem_inc(S("wsum"), 1)
                dve.wait_ge(S("wmean"), n_sum)
                link(dve.tensor_scalar(quant_scale[:, :], bank[7][:, 0:3], EPS, None, ALU.max))
                link(dve.reciprocal(quant_inv[:, :], quant_scale[:, :]))
                for i in which:
                    link(dve.tensor_scalar(quant_tmp[:, i, :], quant_src[:, i, :], quant_inv[:, i:i + 1], MAGIC,
                                           ALU.mult, ALU.add))
                    link(dve.tensor_scalar(quant_tmp[:, i, :], quant_tmp[:, i, :], MAGIC, 1.0, ALU.subtract,
                                           ALU.min))
                    dve.tensor_scalar(quant_bf[:, i, :], quant_tmp[:, i, :], -1.0, None,
                                      ALU.max).then_inc(S("wq_ready"), 1)

            def bit_ffn(layer, gated, gate):
                base = 0 if not gated else 2
                for k, i in enumerate((0, 1, 2) if gated else (0, 2)):
                    dve.wait_ge(S("wqT"), base + k + 1)
                    dve.tensor_copy(ffn_wT[:, i, :], bank[i][:, :].bitcast(BF16)[:, 0:HID]).then_inc(S("wqT_out"), 1)
                link(dve.tensor_copy(ffn_sw[:, :], quant_scale[:, :]))
                link(dve.tensor_scalar(ffn_sw[:, 2:3], ffn_sw[:, 2:3], tgate[:, gate:gate + 1], None, ALU.mult))

                LA, LB = layer + "_qa", layer + "_qb"

                def body(t, p):
                    u, v, q = t + 3, t + 1, 1 - p
                    a, b = live(u), live(v)
                    wa, wb = 4 * u, 3 * v
                    hidden = hid2 if gated else hid
                    if a:
                        wait(dve, layer + "_qx", u - 1)
                        normed(xn[:, q, :], u, LA)
                    if b:
                        wait(dve, layer + "_ge", v + 1)
                        if gated:
                            dve.scalar_tensor_tensor(out=hid2[:, q, :], in0=bank[2 * q + 1][:, :],
                                                     scalar=small[:, q, 4:5], in1=hid[:, q, :], op0=ALU.mult,
                                                     op1=ALU.mult).then_inc(S(layer + "_hm"), 1)
                    if a:
                        wait(dve, LA, wa + 1)
                        dve.tensor_reduce(small[:, q, 0:1], xn[:, q, :], AX.X, ALU.max,
                                          apply_absolute_value=True).then_inc(S(LA), 1)
                    if b:
                        if gated:
                            wait(dve, layer + "_hm", v + 1)
                        dve.tensor_reduce(small[:, q, 6:7], hidden[:, q, :], AX.X, ALU.max,
                                          apply_absolute_value=True).then_inc(S(LB), 1)
                    if a:
                        wait(dve, layer + ("_hm" if gated else "_ge"), u - 1)
                        wait(dve, LA, wa + 2)
                        dve.tensor_scalar(small[:, q, 2:3], small[:, q, 0:1], EPS, 1.0 / QMAX, ALU.max,
                                          ALU.mult).then_inc(S(LA), 1)
                    if b:
                        wait(dve, LB, wb + 1)
                        dve.tensor_scalar(small[:, q, 7:8], small[:, q, 6:7], EPS, 1.0 / QMAX, ALU.max,
                                          ALU.mult).then_inc(S(LB), 1)
                    if a:
                        wait(dve, LA, wa + 3)
                        dve.reciprocal(small[:, q, 1:2], small[:, q, 2:3]).then_inc(S(LA), 1)
                        dve.tensor_tensor(small[:, q, 3:5], ffn_sw[:, 0:2],
                                          small[:, q, 2:3].broadcast_to([P, 2]), ALU.mult)
                    if b:
                        wait(dve, LB, wb + 2)
                        dve.reciprocal(small[:, q, 8:9], small[:, q, 7:8]).then_inc(S(LB), 1)
                        dve.tensor_tensor(small[:, q, 9:10], small[:, q, 7:8], ffn_sw[:, 2:3], ALU.mult)
                    if a:
                        wait(dve, LA, wa + 4)
                        dve.tensor_scalar(xq_f[:, q, :], xn[:, q, :], small[:, q, 1:2], MAGIC, ALU.mult,
                                          ALU.add).then_inc(S(layer + "_qx"), 1)
                    if b:
                        wait(dve, LB, wb + 3)
                        dve.tensor_scalar(hidden[:, q, :], hidden[:, q, :], small[:, q, 8:9], MAGIC, ALU.mult,
                                          ALU.add).then_inc(S(layer + "_qh"), 1)
                    if a:
                        wait(dve, layer + "_qx", u + 1)
                        wait(dve, layer + "_xt", u - 1)
                        dve.tensor_scalar(xq_bf[:, q, :], xq_f[:, q, :], MAGIC, QMAX, ALU.subtract,
                                          ALU.min).then_inc(S(layer + "_xn"), 1)
                    if b:
                        wait(dve, layer + "_qh", v + 1)
                        wait(dve, layer + "_ht", v - 1)
                        dve.tensor_scalar(hid_bf[:, q, :], hidden[:, q, :], MAGIC, QMAX, ALU.subtract,
                                          ALU.min).then_inc(S(layer + "_hq"), 1)
                    if live(t):
                        wait(dve, layer + "_yp", t + 1)
                        dve.scalar_tensor_tensor(out=tile_of(x, t), in0=bank[6 + p][:, 0:P],
                                                 scalar=small[:, p, 9:10], in1=tile_of(x, t), op0=ALU.mult,
                                                 op1=ALU.add).then_inc(S(layer + "_res"), 1)
                    if live(t - 1):
                        wait(dve, layer + "_res", t)
                        tile_stats(t - 1)
                each_tile(dve, body, lead=3)

            if "F0" in phases:
                dve.wait_ge(S("w_f0"), 32)
                link(dve.memset(quant_sum[:, :], 0.0))
                quantised_weights((0, 2), 1)
                norm_stats(2)
                bit_ffn("F0", False, 4)
            if "L1" in phases:
                norm_stats(3)

                def l1(t, p):
                    if live(t + 4):
                        wait(dve, "L1_xt", t + 3)
                        normed(xn[:, p, :], t + 4, "L1_xn")
                    if live(t + 2):
                        wait(dve, "L1_sp", t + 3)
                        wait(dve, "L1_ex", t + 1)
                        dve.scalar_tensor_tensor(out=hid[:, p, 0:P], in0=bank[2 + p][:, 0:P], scalar=L1_SCALE,
                                                 in1=tile_of(add_mask, t + 2), op0=ALU.mult,
                                                 op1=ALU.add).then_inc(S("L1_sm"), 1)
                    if live(t):
                        wait(dve, "L1_ex", t + 1)
                        dve.reciprocal(small[:, p, 2:3], small[:, p, 1:2]).then_inc(S("L1_r"), 1)
                    if live(t + 2):
                        wait(dve, "L1_sm", t + 3)
                        dve.tensor_reduce(small[:, p, 0:1], hid[:, p, 0:P], AX.X, ALU.max,
                                          negate=True).then_inc(S("L1_nm"), 1)
                    if live(t):
                        wait(dve, "L1_r", 2 * t + 1)
                        dve.tensor_scalar(small[:, p, 3:4], small[:, p, 2:3], tgate[:, 1:2], None,
                                          ALU.mult).then_inc(S("L1_r"), 1)
                    if live(t - 1):
                        wait(dve, "L1_r", 2 * t)
                        wait(dve, "L1_pv", t)
                        dve.scalar_tensor_tensor(out=tile_of(x, t - 1), in0=bank[7 - p][:, 0:P],
                                                 scalar=small[:, 1 - p, 3:4], in1=tile_of(x, t - 1), op0=ALU.mult,
                                                 op1=ALU.add).then_inc(S("L1_res"), 1)
                    if live(t - 2):
                        wait(dve, "L1_res", t - 1)
                        tile_stats(t - 2)
                dve.wait_ge(S("mask_in"), 16)
                each_tile(dve, l1, lead=4, tail=2)
            if "F1" in phases:
                dve.wait_ge(S("w_f1"), 48)
                quantised_weights((0, 1, 2), 2)
                norm_stats(4)
                bit_ffn("F1", True, 5)
            if "L2" in phases:
                norm_stats(5)
                attention("L2")
            if "F2" in phases:
                norm_stats(6)

                def route(t, p):
                    if live(t + 2):
                        wait(dve, "R_xt", t + 1)
                        wait(dve, "R_xd", t + 1)
                        normed(xn[:, p, :], t + 2, "R_xn")
                    if live(t + 1):
                        wait(dve, "R_xn", t + 2)
                        dve.tensor_copy(tile_of(shared, t + 1), xn[:, 1 - p, :]).then_inc(S("R_xd"), 1)
                    if live(t):
                        wait(dve, "R_lp", t + 1)
                        dve.tensor_tensor(logits[:, bass.ds(t, 1), :].rearrange("p u e -> p (u e)"),
                                          bank[2 + p][:, 0:NE], switch_b[:, :], ALU.add).then_inc(S("R_lg"), 1)
                each_tile(dve, route, lead=2)
                dve.wait_ge(S("R_lg"), NT)

                def by_tile(i):
                    return route_m[:, i, :].unsqueeze(2).broadcast_to([P, NT, NE])

                def by_expert(ap):
                    return over_blocks(ap, NT)
                link(dve.tensor_reduce(route_m[:, 0, :], logits[:, :, :], AX.X, ALU.max))
                link(dve.tensor_tensor(route_b[:, :, :], logits[:, :, :], by_tile(0), ALU.subtract))
                dve.sem_inc(S("R_sub"), 1)
                dve.wait_ge(S("R_exp"), 1)
                link(dve.tensor_reduce(route_m[:, 1, :], route_a[:, :, :], AX.X, ALU.add))
                link(dve.reciprocal(route_m[:, 2, :], route_m[:, 1, :]))
                link(dve.tensor_scalar(route_a[:, :, :], route_b[:, :, :], 0.0, float(NE), ALU.is_lt, ALU.mult))
                link(dve.tensor_tensor(route_a[:, :, :], route_a[:, :, :], by_expert(expert_no[:, :]), ALU.add))
                link(dve.tensor_reduce(route_m[:, 0, :], route_a[:, :, :], AX.X, ALU.min))
                link(dve.tensor_tensor(route_b[:, :, :], by_expert(expert_no[:, :]), by_tile(0), ALU.is_equal))
                dve.sem_inc(S("R_hot"), 1)
                link(dve.tensor_scalar(gate[:, :], route_m[:, 2, :], tgate[:, 6:7], None, ALU.mult))
                dve.wait_ge(S("R_rank"), 1)
                here, upto, other = (bank[1][:, 0:NT * NE].rearrange("p (t e) -> p t e", e=NE), route_c, route_d)
                link(dve.tensor_copy(upto[:, :, :], here))
                back = 1
                while back < NT:
                    dve.tensor_copy(other[:, 0:back, :], upto[:, 0:back, :])
                    link(dve.tensor_tensor(other[:, back:NT, :], upto[:, back:NT, :], upto[:, 0:NT - back, :],
                                           ALU.add))
                    upto, other = other, upto
                    back *= 2
                link(dve.tensor_scalar(fill[:, 0, :], upto[:, NT - 1, :], 1.0 / P, (P - 1) / P - 0.498,
                                       ALU.mult, ALU.add))
                link(dve.tensor_scalar(fill[:, 0, :], fill[:, 0, :], MAGIC, None, ALU.add))
                link(dve.tensor_scalar(fill[:, 0, :], fill[:, 0, :], MAGIC, None, ALU.subtract))
                link(dve.tensor_copy(fill[:, 1, :], fill[:, 0, :]))
                now, then = 1, 2
                back = 1
                while back < NE:
                    dve.tensor_copy(fill[:, then, 0:back], fill[:, now, 0:back])
                    link(dve.tensor_tensor(fill[:, then, back:NE], fill[:, now, back:NE],
                                           fill[:, now, 0:NE - back], ALU.add))
                    now, then = then, now
                    back *= 2
                link(dve.tensor_scalar(expert_of[:, :], slot_no[:, :], fill[:, now, 0:1], None, ALU.is_ge))
                for e in range(1, NE - 1):
                    link(dve.scalar_tensor_tensor(out=expert_of[:, :], in0=slot_no[:, :],
                                                  scalar=fill[:, now, e:e + 1], in1=expert_of[:, :],
                                                  op0=ALU.is_ge, op1=ALU.add))
                dve.tensor_copy(expert_int[:, :], expert_of[0:1, :]).then_inc(S("R_slots"), 1)
                link(dve.tensor_tensor(fill[:, 3, :], fill[:, now, :], fill[:, 0, :], ALU.subtract))
                link(dve.tensor_scalar(fill[:, 3, :], fill[:, 3, :], float(P), None, ALU.mult))
                link(dve.tensor_tensor(upto[:, :, :], upto[:, :, :], here, ALU.subtract))
                link(dve.tensor_tensor(upto[:, :, :], upto[:, :, :],
                                       bank[0][:, 0:NT * NE].rearrange("p (t e) -> p t e", e=NE), ALU.add))
                link(dve.tensor_tensor(upto[:, :, :], upto[:, :, :], by_expert(fill[:, 3, :]), ALU.add))
                link(dve.tensor_tensor(upto[:, :, :], upto[:, :, :], route_b[:, :, :], ALU.mult))
                link(dve.tensor_reduce(route_m[:, 0, :], upto[:, :, :], AX.X, ALU.add))
                dve.tensor_copy(dest_int[:, :], route_m[:, 0, :]).then_inc(S("R_dest"), 1)

                def slots(j, q):
                    for p in range(2):
                        t = 2 * j + p
                        if live(t + 1, NS):
                            wait(dve, "G_hp", t + 2)
                            wait(dve, "G_ht", t)
                            dve.tensor_copy(hid[:, 1 - p, :], bank[1 - p][:, :]).then_inc(S("G_hs"), 1)
                        if live(t - 1, NS):
                            e = dve.value_load(expert_int[0:1, bass.ds(t - 1, 1)], min_val=0, max_val=NE - 1)
                            wait(dve, "G_yp", t)
                            if p == 1:
                                wait(dve, "G_out", 16 * (j - 1))
                            y = slot_y[:, q, 0, :] if p == 1 else slot_y[:, 1 - q, 1, :]
                            dve.tensor_tensor(y, bank[5 + 1 - p][:, 0:P], moe_b2_rows[:, bass.ds(e * P, P)],
                                              ALU.add).then_inc(S("G_yo"), 1)
                dve.wait_ge(S("R_slots"), 1)
                each_tile(dve, slots, n=NS // 2)

                if "L3" in phases:
                    dve.wait_ge(S("open_in"), 16)
                    dve.wait_ge(S("fut"), 8)
                    dve.tensor_scalar(open_mask[:, :], open_mask[:, :].bitcast(I32), 0.0, None,
                                      ALU.not_equal).then_inc(S("open"), 1)
                    dve.wait_ge(S("open"), 1)
                    dve.tensor_tensor(open_mask[:, :].rearrange("k (t q) -> k t q", q=P),
                                      open_mask[:, :].rearrange("k (t q) -> k t q", q=P),
                                      over_blocks(future_one[:, :], NT), ALU.mult).then_inc(S("open"), 1)
                for c in range(NT // GC):
                    dve.wait_ge(S(f"gathered_{c}"), 16 * GC)
                    for t in range(c * GC, (c + 1) * GC):
                        dve.scalar_tensor_tensor(out=x[:, t * P:(t + 1) * P], in0=shared[:, t * P:(t + 1) * P],
                                                 scalar=gate[:, t:t + 1], in1=x[:, t * P:(t + 1) * P],
                                                 op0=ALU.mult, op1=ALU.add).then_inc(S("B_res"), 1)
                    dve.wait_ge(S("B_res"), (c + 1) * GC)
                    for t in range(c * GC, (c + 1) * GC):
                        tile_stats(t)
            if "L3" in phases:
                norm_stats(7, scale_by_keep=True)
                attention("L3")
            if "F3" in phases:
                norm_stats(8)
                dve.wait_ge(S("bf_used"), 2 * STAGES)
                link(dve.tensor_tensor(up_row[:, :], up_row[:, :], bf_up[0:1, STAGES % 2, 1, :], ALU.add))
                dve.sem_inc(S("up_row"), 1)
                dve.wait_ge(S("wT"), 6)
                link(dve.tensor_copy(w_down[:, :, :].rearrange("p c d -> p (c d)"), bank[6][:, :]))
                link(dve.tensor_copy(up_bias[:, :], bank[5][:, 0:NC]))
                dve.sem_inc(S("f3_bias"), 1)
                link(dve.tensor_tensor(con_bias[:, 0, :], con_bias[:, 0, :], con_bias[:, 1, :], ALU.add))
                link(dve.tensor_scalar(con_bias[:, 0, :], con_bias[:, 0, :], tgate[:, 7:8], None, ALU.mult))

                def f3(t, p):
                    if live(t + 3):
                        wait(dve, "F3_xt", t + 2)
                        normed(xn[:, 1 - p, :], t + 3, "F3_xn")
                    if live(t):
                        dve.tensor_tensor(tile_of(x, t), tile_of(x, t), con_bias[:, 0, :],
                                          ALU.add).then_inc(S("F3_b"), 1)
                        wait(dve, "F3_b", t + 1)
                        wait(dve, "F3_yp", t + 1)
                        dve.scalar_tensor_tensor(out=tile_of(x, t), in0=bank[2 + p][:, 0:P],
                                                 scalar=tgate[:, 7:8], in1=tile_of(x, t), op0=ALU.mult,
                                                 op1=ALU.add).then_inc(S("F3_res"), 1)
                each_tile(dve, f3, lead=3)


def kernel(**inputs):
    import numpy as _np
    import concourse.bacc as _bacc
    from concourse import mybir as _mybir
    from concourse.bass_utils import run_bass_kernel_spmd as _run

    nc = _bacc.Bacc("TRN2", target_bir_lowering=False, num_devices=1)
    arrays, args = {}, {}
    for name, a in inputs.items():
        a = _np.ascontiguousarray(a)
        arrays[f"in_{name}_dram"] = a
        args[name] = nc.dram_tensor(f"in_{name}_dram", a.shape, _mybir.dt.from_np(a.dtype), kind="ExternalInput").ap()
    out = nc.dram_tensor("out_0_dram", (NT, P, P), F32, kind="ExternalOutput").ap()
    slots = [nc.dram_tensor(f"slot_{n}", (NS * P, P), F32).ap() for n in ("in", "out")]
    scratch = [nc.dram_tensor(f"{n}_scratch", (NT, NH, P, DH), F32).ap() for n in "qvo"]
    gated_layers(nc, args, out, *scratch, *slots)
    r = _run(nc, [arrays], core_ids=[0])
    return r.results[0]["out_0_dram"]
```
